# Optimizing a Trainium2 kernel written in Bass

```python
import numpy as np
import jax
import jax.numpy as jnp

def _softmax(x, axis=-1):
    return jax.nn.softmax(x, axis=axis)

def _gelu(x):
    return jax.nn.gelu(x, approximate=True)

def _silu(x):
    return jax.nn.silu(x)

def _sigmoid(x):
    return jax.nn.sigmoid(x)

def _layernorm(x, axis=-1, eps=1e-05):
    m = jnp.mean(x, axis=axis, keepdims=True)
    v = jnp.var(x, axis=axis, keepdims=True)
    return (x - m) / jnp.sqrt(v + eps)

def _scatter_add(tgt, idx, src, axis=0):
    return tgt.at[idx].add(src)

def _segment_sum(src, seg, n):
    return jax.ops.segment_sum(src, seg, n)
kernel_name = 'mk_adj_ffn_d2_adj_r2_97bfe7'

def setup_inputs(seed: int=0):
    np.random.seed(seed)
    _w = jnp.asarray

    def _rec_inputs():
        import jax
        import jax.numpy as jnp
        _gk = jax.random.key(seed)
        x = -0.0003929 + 0.9999 * jax.random.normal(jax.random.fold_in(_gk, 1), (32, 256, 128), jnp.float32)
        _w = (1.0 + jnp.arange(256, dtype=jnp.float32)) ** (-0.5)
        _w = _w / _w.mean()
        _pij = jnp.clip(0.03125 * _w[:, None] * _w[None, :], 0.0, 1.0)
        _a = jax.random.uniform(jax.random.fold_in(_gk, 2), (256, 256)) < _pij
        _a = jnp.logical_or(_a, jnp.swapaxes(_a, -1, -2))
        _a = jnp.logical_or(_a, jnp.eye(256, dtype=bool))
        _af = _a.astype(jnp.float32)
        _af = _af * jax.random.uniform(jax.random.fold_in(_gk, 3), (256, 256), jnp.float32, 0.05, 1)
        adj = _af
        return (x, adj)
    x, adj = _rec_inputs()

    def _L0_gnn_setup():
        import jax, jax.numpy as jnp
        import numpy as np
        EPS = 1e-05

        def _batchnorm(x, gamma, beta):
            mu = jnp.mean(x, axis=0)
            var = jnp.var(x, axis=0)
            return (x - mu) * jax.lax.rsqrt(var + EPS) * gamma + beta
        key = jax.random.key(seed)
        ks = jax.random.split(key, 4)
        b, n, d, h, o = (32, 1024, 128, 256, 128)
        features = jax.random.normal(ks[0], (b, n, d), dtype=jnp.float32)
        A = jax.random.uniform(ks[1], (n, n), dtype=jnp.float32)
        lim1 = float(np.sqrt(6.0 / (d + h)))
        W1 = jax.random.uniform(ks[2], (h, d), minval=-lim1, maxval=lim1, dtype=jnp.float32)
        b1 = jnp.zeros((h,), jnp.float32)
        lim2 = float(np.sqrt(6.0 / (h + o)))
        W2 = jax.random.uniform(ks[3], (o, h), minval=-lim2, maxval=lim2, dtype=jnp.float32)
        b2 = jnp.zeros((o,), jnp.float32)
        g1 = jnp.ones((h,), jnp.float32)
        be1 = jnp.zeros((h,), jnp.float32)
        g2 = jnp.ones((o,), jnp.float32)
        be2 = jnp.zeros((o,), jnp.float32)
        return {'features': features, 'A': A, 'W1': W1, 'b1': b1, 'g1': g1, 'be1': be1, 'W2': W2, 'b2': b2, 'g2': g2, 'be2': be2}
    _L0_gnn_all = _L0_gnn_setup()
    _L0_gnn_in = {k: v for k, v in _L0_gnn_all.items() if k in ('W1', 'b1', 'g1', 'be1', 'W2', 'b2', 'g2', 'be2')}
    del _L0_gnn_all

    def _L0_ffn_setup():
        import jax, jax.numpy as jnp
        import numpy as np
        TOP_K = 2
        LN_EPS = 1e-05
        key = jax.random.key(seed)
        ks = jax.random.split(key, 8)
        B, S, D, E, H = (16, 512, 128, 8, 512)
        x = jax.random.normal(ks[0], (B, S, D), dtype=jnp.float32)
        Wr = jax.random.normal(ks[1], (D, E), dtype=jnp.float32) * 0.1
        br = jnp.zeros((E,), dtype=jnp.float32)
        ln_g = jnp.ones((E, D), dtype=jnp.float32)
        ln_b = jnp.zeros((E, D), dtype=jnp.float32)
        W1 = jax.random.normal(ks[2], (E, D, H), dtype=jnp.float32) * (1.0 / np.sqrt(D))
        b1 = jnp.zeros((E, H), dtype=jnp.float32)
        W2 = jax.random.normal(ks[3], (E, H, D), dtype=jnp.float32) * (1.0 / np.sqrt(H))
        b2 = jnp.zeros((E, D), dtype=jnp.float32)
        return {'x': x, 'Wr': Wr, 'br': br, 'ln_g': ln_g, 'ln_b': ln_b, 'W1': W1, 'b1': b1, 'W2': W2, 'b2': b2}
    _L0_ffn_all = _L0_ffn_setup()
    _L0_ffn_in = {k: v for k, v in _L0_ffn_all.items() if k in ('Wr', 'br', 'ln_g', 'ln_b', 'W1', 'b1', 'W2', 'b2')}
    del _L0_ffn_all

    def _L1_gnn_setup():
        import jax, jax.numpy as jnp
        import numpy as np
        B, T, D, H = (64, 1024, 128, 128)
        MAX_SKIP = 4

        def _lstm_last(Wih, Whh, bih, bhh, xs):
            N, _, Hd = xs.shape
            bias = bih + bhh

            def step(carry, x_t):
                h, c = carry
                g = x_t @ Wih.T + h @ Whh.T + bias
                i, f, gg, o = jnp.split(g, 4, axis=-1)
                c = jax.nn.sigmoid(f) * c + jax.nn.sigmoid(i) * jnp.tanh(gg)
                h = jax.nn.sigmoid(o) * jnp.tanh(c)
                return ((h, c), None)
            init = (jnp.zeros((N, Hd), xs.dtype), jnp.zeros((N, Hd), xs.dtype))
            (h_last, _), _ = jax.lax.scan(step, init, jnp.swapaxes(xs, 0, 1))
            return h_last
        key = jax.random.key(seed)
        ks = jax.random.split(key, 8)
        s = 0.05
        x = jax.random.normal(ks[0], (B, T, D), jnp.float32)
        adj = jax.random.uniform(ks[1], (T, T), jnp.float32) / T
        Wg0 = jax.random.normal(ks[2], (D, H), jnp.float32) * s
        bg0 = jnp.zeros((H,), jnp.float32)
        Wg1 = jax.random.normal(ks[3], (H, H), jnp.float32) * s
        bg1 = jnp.zeros((H,), jnp.float32)
        Wih = jax.random.normal(ks[4], (MAX_SKIP, 4 * H, H), jnp.float32) * s
        Whh = jax.random.normal(ks[5], (MAX_SKIP, 4 * H, H), jnp.float32) * s
        bih = jax.random.normal(ks[6], (MAX_SKIP, 4 * H), jnp.float32) * s
        bhh = jax.random.normal(ks[7], (MAX_SKIP, 4 * H), jnp.float32) * s
        return dict(x=x, adj=adj, Wg0=Wg0, bg0=bg0, Wg1=Wg1, bg1=bg1, Wih=Wih, Whh=Whh, bih=bih, bhh=bhh)
    _L1_gnn_all = _L1_gnn_setup()
    _L1_gnn_in = {k: v for k, v in _L1_gnn_all.items() if k in ('Wg0', 'bg0', 'Wg1', 'bg1', 'Wih', 'Whh', 'bih', 'bhh')}
    del _L1_gnn_all

    def _L1_ffn_setup():
        import jax, jax.numpy as jnp
        import numpy as np
        TOP_K = 2
        key = jax.random.key(seed)
        ks = jax.random.split(key, 4)
        B, L, D, H, E = (8, 2048, 128, 512, 8)
        s = 0.02
        return {'x': jax.random.normal(ks[0], (B, L, D), jnp.float32), 'Wg': jax.random.normal(ks[1], (D, E), jnp.float32) * s, 'bg': jnp.zeros((E,), jnp.float32), 'W1': jax.random.normal(ks[2], (E, D, H), jnp.float32) * s, 'b1': jnp.zeros((E, H), jnp.float32), 'W2': jax.random.normal(ks[3], (E, H, D), jnp.float32) * s, 'b2': jnp.zeros((E, D), jnp.float32)}
    _L1_ffn_all = _L1_ffn_setup()
    _L1_ffn_in = {k: v for k, v in _L1_ffn_all.items() if k in ('Wg', 'bg', 'W1', 'b1', 'W2', 'b2')}
    del _L1_ffn_all
    return {'x': x, 'adj': adj, 'L0_gnn_W1': _L0_gnn_in['W1'], 'L0_gnn_b1': _L0_gnn_in['b1'], 'L0_gnn_g1': _L0_gnn_in['g1'], 'L0_gnn_be1': _L0_gnn_in['be1'], 'L0_gnn_W2': _L0_gnn_in['W2'], 'L0_gnn_b2': _L0_gnn_in['b2'], 'L0_gnn_g2': _L0_gnn_in['g2'], 'L0_gnn_be2': _L0_gnn_in['be2'], 'L0_ffn_Wr': _L0_ffn_in['Wr'], 'L0_ffn_br': _L0_ffn_in['br'], 'L0_ffn_ln_g': _L0_ffn_in['ln_g'], 'L0_ffn_ln_b': _L0_ffn_in['ln_b'], 'L0_ffn_W1': _L0_ffn_in['W1'], 'L0_ffn_b1': _L0_ffn_in['b1'], 'L0_ffn_W2': _L0_ffn_in['W2'], 'L0_ffn_b2': _L0_ffn_in['b2'], 'L1_gnn_Wg0': _L1_gnn_in['Wg0'], 'L1_gnn_bg0': _L1_gnn_in['bg0'], 'L1_gnn_Wg1': _L1_gnn_in['Wg1'], 'L1_gnn_bg1': _L1_gnn_in['bg1'], 'L1_gnn_Wih': _L1_gnn_in['Wih'], 'L1_gnn_Whh': _L1_gnn_in['Whh'], 'L1_gnn_bih': _L1_gnn_in['bih'], 'L1_gnn_bhh': _L1_gnn_in['bhh'], 'L1_ffn_Wg': _L1_ffn_in['Wg'], 'L1_ffn_bg': _L1_ffn_in['bg'], 'L1_ffn_W1': _L1_ffn_in['W1'], 'L1_ffn_b1': _L1_ffn_in['b1'], 'L1_ffn_W2': _L1_ffn_in['W2'], 'L1_ffn_b2': _L1_ffn_in['b2']}

def reference(x, adj, L0_gnn_W1, L0_gnn_b1, L0_gnn_g1, L0_gnn_be1, L0_gnn_W2, L0_gnn_b2, L0_gnn_g2, L0_gnn_be2, L0_ffn_Wr, L0_ffn_br, L0_ffn_ln_g, L0_ffn_ln_b, L0_ffn_W1, L0_ffn_b1, L0_ffn_W2, L0_ffn_b2, L1_gnn_Wg0, L1_gnn_bg0, L1_gnn_Wg1, L1_gnn_bg1, L1_gnn_Wih, L1_gnn_Whh, L1_gnn_bih, L1_gnn_bhh, L1_ffn_Wg, L1_ffn_bg, L1_ffn_W1, L1_ffn_b1, L1_ffn_W2, L1_ffn_b2):
    import jax
    import jax.numpy as jnp

    def _L0_gnn_ref(features, A, W1, b1, g1, be1, W2, b2, g2, be2):
        import jax, jax.numpy as jnp
        import numpy as np
        EPS = 1e-05

        def _batchnorm(x, gamma, beta):
            mu = jnp.mean(x, axis=0)
            var = jnp.var(x, axis=0)
            return (x - mu) * jax.lax.rsqrt(var + EPS) * gamma + beta
        b, n, d = features.shape
        A_norm = A + jnp.eye(n, dtype=A.dtype)
        deg = jnp.sum(A_norm, axis=0) + jnp.sum(A_norm, axis=1) - jnp.diagonal(A_norm)
        dinv = jax.lax.rsqrt(deg)
        A_hat = A_norm * dinv[:, None] * dinv[None, :]
        agg = jnp.einsum('nm,bmd->bnd', A_hat, features)
        x = agg.reshape(-1, d)
        h = jax.nn.relu(_batchnorm(x @ W1.T + b1, g1, be1))
        out = h @ W2.T + b2
        out = _batchnorm(out, g2, be2)
        return out.reshape(b, n, -1)

    def _L0_ffn_ref(x, Wr, br, ln_g, ln_b, W1, b1, W2, b2):
        import jax, jax.numpy as jnp
        import numpy as np
        TOP_K = 2
        LN_EPS = 1e-05
        B, S, D = x.shape
        N = B * S
        xt = x.reshape(N, D)
        logits = xt @ Wr + br
        probs = jax.nn.softmax(logits, axis=-1)
        top_p, top_idx = jax.lax.top_k(probs, TOP_K)
        weights = top_p / top_p.sum(axis=-1, keepdims=True)
        mu = xt.mean(axis=-1, keepdims=True)
        var = ((xt - mu) ** 2).mean(axis=-1, keepdims=True)
        xn = (xt - mu) * jax.lax.rsqrt(var + LN_EPS)
        xe = xn[None, :, :] * ln_g[:, None, :] + ln_b[:, None, :]
        h = jax.nn.gelu(jnp.einsum('end,edh->enh', xe, W1) + b1[:, None, :], approximate=False)
        y = jnp.einsum('enh,ehd->end', h, W2) + b2[:, None, :]
        y_tok = jnp.transpose(y, (1, 0, 2))
        sel = jnp.take_along_axis(y_tok, top_idx[:, :, None], axis=1)
        out = (weights[:, :, None] * sel).sum(axis=1)
        return out.reshape(B, S, D)

    def _L1_gnn_ref(x, adj, Wg0, bg0, Wg1, bg1, Wih, Whh, bih, bhh):
        import jax, jax.numpy as jnp
        import numpy as np
        B, T, D, H = (64, 1024, 128, 128)
        MAX_SKIP = 4

        def _lstm_last(Wih, Whh, bih, bhh, xs):
            N, _, Hd = xs.shape
            bias = bih + bhh

            def step(carry, x_t):
                h, c = carry
                g = x_t @ Wih.T + h @ Whh.T + bias
                i, f, gg, o = jnp.split(g, 4, axis=-1)
                c = jax.nn.sigmoid(f) * c + jax.nn.sigmoid(i) * jnp.tanh(gg)
                h = jax.nn.sigmoid(o) * jnp.tanh(c)
                return ((h, c), None)
            init = (jnp.zeros((N, Hd), xs.dtype), jnp.zeros((N, Hd), xs.dtype))
            (h_last, _), _ = jax.lax.scan(step, init, jnp.swapaxes(xs, 0, 1))
            return h_last
        h = jax.nn.relu(jnp.einsum('ts,bsh->bth', adj, x @ Wg0 + bg0))
        h = jax.nn.relu(jnp.einsum('ts,bsh->bth', adj, h @ Wg1 + bg1))
        Bv, Tv, Hd = h.shape
        for p in range(1, MAX_SKIP + 1):
            nw = Tv // p
            wins = h[:, :nw * p, :].reshape(Bv * nw, p, Hd)
            last = _lstm_last(Wih[p - 1], Whh[p - 1], bih[p - 1], bhh[p - 1], wins)
            idx = jnp.arange(nw) * p + (p - 1)
            h = h.at[:, idx, :].set(last.reshape(Bv, nw, Hd))
        return h

    def _L1_ffn_ref(x, Wg, bg, W1, b1, W2, b2):
        import jax, jax.numpy as jnp
        import numpy as np
        TOP_K = 2
        B, L, D = x.shape
        E = W1.shape[0]
        xf = x.reshape(-1, D)
        gate_logits = xf @ Wg + bg
        top_w, top_i = jax.lax.top_k(gate_logits, TOP_K)
        top_w = jax.nn.softmax(top_w, axis=-1)
        w_dense = jnp.sum(jax.nn.one_hot(top_i, E, dtype=xf.dtype) * top_w[..., None], axis=1)
        out = jnp.zeros_like(xf)
        for e in range(E):
            h = jax.nn.gelu(xf @ W1[e] + b1[e], approximate=False)
            out = out + w_dense[:, e:e + 1] * (h @ W2[e] + b2[e])
        return out.reshape(B, L, D)
    x = x + _L0_gnn_ref(_layernorm(x, axis=-1), adj, L0_gnn_W1, L0_gnn_b1, L0_gnn_g1, L0_gnn_be1, L0_gnn_W2, L0_gnn_b2, L0_gnn_g2, L0_gnn_be2)
    x = x + _L0_ffn_ref(_layernorm(x, axis=-1), L0_ffn_Wr, L0_ffn_br, L0_ffn_ln_g, L0_ffn_ln_b, L0_ffn_W1, L0_ffn_b1, L0_ffn_W2, L0_ffn_b2)
    x = x + _L1_gnn_ref(_layernorm(x, axis=-1), adj, L1_gnn_Wg0, L1_gnn_bg0, L1_gnn_Wg1, L1_gnn_bg1, L1_gnn_Wih, L1_gnn_Whh, L1_gnn_bih, L1_gnn_bhh)
    x = x + _L1_ffn_ref(_layernorm(x, axis=-1), L1_ffn_Wg, L1_ffn_bg, L1_ffn_W1, L1_ffn_b1, L1_ffn_W2, L1_ffn_b2)
    return x

_drawn_inputs = setup_inputs


def setup_inputs(seed=0):
    import zlib

    import numpy as np

    out = dict(_drawn_inputs(seed))
    spreads = {'L0_gnn_b1': (0.0, 0.8),
     'L0_gnn_g1': (1.0, 0.2),
     'L0_gnn_be1': (0.0, 0.1),
     'L0_gnn_b2': (0.0, 0.8),
     'L0_gnn_g2': (1.0, 0.2),
     'L0_gnn_be2': (0.0, 0.1),
     'L0_ffn_br': (0.0, 0.1),
     'L0_ffn_ln_g': (1.0, 0.2),
     'L0_ffn_ln_b': (0.0, 0.1),
     'L0_ffn_b1': (0.0, 0.1),
     'L0_ffn_b2': (0.0, 0.1),
     'L1_gnn_bg0': (0.0, 0.1),
     'L1_gnn_bg1': (0.0, 0.377),
     'L1_ffn_bg': (0.0, 0.1),
     'L1_ffn_b1': (0.0, 0.714),
     'L1_ffn_b2': (0.0, 0.1)}
    factors = {'L1_gnn_Whh': 8.0, 'L1_gnn_bih': 4.275, 'L1_gnn_bhh': 4.346}
    for name, (base, spread) in spreads.items():
        noise = np.random.default_rng([zlib.crc32(name.encode()), seed]).standard_normal(out[name].shape)
        drawn = base * np.exp(spread * noise) if base else spread * noise
        out[name] = jnp.asarray(drawn.astype(out[name].dtype))
    for name, factor in factors.items():
        out[name] = (out[name] * factor).astype(out[name].dtype)
    return out
```

```python
from contextlib import ExitStack

import concourse.bass as bass
from concourse import mybir

F32 = mybir.dt.float32
F16 = mybir.dt.float16
BF16 = mybir.dt.bfloat16
I32 = mybir.dt.int32
ALU = mybir.AluOpType
ACT = mybir.ActivationFunctionType
AX = mybir.AxisListType

P = 128
B, T, D = 32, 256, 128
N = B * T
NT = N // P
E, H = 8, 512
HT = H // P
TOP_K = 2
EPS = 1e-5
OUTER_EPS = 1e-5
GH = 256
SKIP = 4

G = 4
GT = NT // G
BLK = 256
NBLK = (GT * P * TOP_K + E * (BLK - 1)) // BLK
SLOTS = NBLK * BLK
KMAX = GT * P // BLK
NCH = NT // 4
QT = 8
NQ = NT // QT
SC = 256.0
UNSC = 1.0 / (SC * SC)

R_FB1 = (0, 32)
R_LNG, R_LNB = 64, 72
R_B1, R_G1, R_BE1 = 80, 82, 84
R_B2, R_G2, R_BE2 = 86, 87, 88
R_BIH, R_BHH = 89, 105
R_ROWS = 121

GATES_PER_QUAD = 2 * 3 + (3 + 4) + (3 + 4 + 4) + (3 + 4 + 4 + 4)
LSTM_STEPS = [(1, 0, 0), (1, 0, 1)] + [(p, s, 0) for p in range(2, SKIP + 1) for s in range(p)]


NLSTM = 2 * SKIP - 1
C_LINKS = 1 + 5 + 1 + 1 + 2 * (1 + 2 + 3)


class Chain:

    def __init__(self, eng, sem):
        self.eng, self.sem, self.base, self.k, self.i, self.per = eng, sem, 0, 0, None, 0

    def now(self):
        return self.base + self.k if self.i is None else self.base + self.i * self.per + self.k

    def mark(self, ins):
        self.k += 1
        ins.then_inc(self.sem, 1)

    def wait(self):
        self.eng.wait_ge(self.sem, self.now())

    def link(self, ins):
        self.mark(ins)
        self.wait()

    def enter(self, i, per):
        self.base, self.k, self.i, self.per = self.base + self.k, 0, i, per

    def leave(self, count):
        assert self.k == self.per, (self.k, self.per)
        self.base, self.k, self.i = self.base + self.per * count, 0, None


def default_plan():
    return [("A",), ("P", 0, 0), ("P", 0, 1), ("X", 0, 0), ("P", 0, 2), ("X", 0, 1), ("P", 0, 3), ("X", 0, 2),
            ("D", 0, 0), ("C", 0), ("P", 1, 0), ("X", 0, 3), ("D", 0, 1), ("C", 1), ("P", 1, 1), ("W",),
            ("X", 1, 0), ("D", 0, 2), ("C", 2), ("P", 1, 2), ("X", 1, 1), ("D", 0, 3), ("C", 3),
            ("P", 1, 3), ("D", 1, 0), ("X", 1, 2), ("D", 1, 1), ("X", 1, 3), ("D", 1, 2), ("D", 1, 3)]


def graph_moe_kernel(nc, x, adj, L0_gnn_W1, L0_gnn_b1, L0_gnn_g1, L0_gnn_be1, L0_gnn_W2, L0_gnn_b2, L0_gnn_g2,
                     L0_gnn_be2, L0_ffn_Wr, L0_ffn_br, L0_ffn_ln_g, L0_ffn_ln_b, L0_ffn_W1, L0_ffn_b1, L0_ffn_W2,
                     L0_ffn_b2, L1_gnn_Wg0, L1_gnn_bg0, L1_gnn_Wg1, L1_gnn_bg1, L1_gnn_Wih, L1_gnn_Whh, L1_gnn_bih,
                     L1_gnn_bhh, L1_ffn_Wg, L1_ffn_bg, L1_ffn_W1, L1_ffn_b1, L1_ffn_W2, L1_ffn_b2, out, plan=None,
                     dump=False):
    plan = plan or default_plan()
    x_t = x.rearrange("b (h p) d -> p (b h) d", p=P)
    out_t = out.rearrange("b (h p) d -> p (b h) d", p=P)
    fW1 = (L0_ffn_W1, L1_ffn_W1)
    fW2 = (L0_ffn_W2, L1_ffn_W2)

    prep_order = [s[1:] for s in plan if s[0] == "P"]
    expert_order = [s[1:] for s in plan if s[0] == "X"]
    combine_order = [s[1:] for s in plan if s[0] == "D"]
    pool_order = []
    for s in plan:
        if s[0] == "P":
            pool_order.append(("scatter",) + s[1:])
        if s[0] == "X":
            pool_order.append(("gather",) + s[1:])

    with ExitStack() as ctx:
        def sb(name, shape, dt=F32):
            return ctx.enter_context(nc.sbuf_tensor(name, shape, dt))

        def sem(name):
            return ctx.enter_context(nc.semaphore(name))

        def dram(name, shape, dt=F32):
            return nc.dram_tensor(name, shape, dt, kind="Internal").ap()

        slots_in = [dram(f"slots_in{i}", (SLOTS, D)) for i in range(2)]
        slots_out = {inst: dram(f"slots_out{inst[0]}_{inst[1]}", (SLOTS, D)) for inst in expert_order}

        xt = sb("x_tok", [P, NT, D])
        hid = sb("hid", [P, 2, N])
        o2T = hid[:, 0, :]
        taken = [0, 0]

        def carve(half, n):
            a = taken[half]
            taken[half] += n
            assert taken[half] <= N, taken
            return hid[:, half, a:a + n]

        ident = sb("ident", [P, P])
        tri = sb("tri", [P, P], BF16)
        ones = sb("ones", [P, P], BF16)
        desc = sb("desc", [P, E])
        ej_mask = sb("ej_mask", [P, E * GT])
        k_blk = sb("k_blk", [P, KMAX])
        one8 = sb("one8", [P, E])
        iota_b = sb("iota_b", [1, NBLK])
        rows = sb("rows", [P, P])
        vec = sb("vec", [P, R_ROWS])
        bn1s = sb("bn1s", [P, 2])
        bn1t = sb("bn1t", [P, 2])
        bn2s = sb("bn2s", [P, 1])
        bn2t = sb("bn2t", [P, 1])
        lng_s = sb("lng_s", [P, E])
        eb1 = sb("eb1", [P, 2, E * HT])
        eb2 = [sb(f"eb2_{l}", [P, E, D]) for l in range(2)]
        Wr = sb("Wr", [P, 2, E])
        brb = sb("brb", [P, 2, E])
        Wg = sb("Wg", [P, 2, D])
        bg1b = sb("bg1b", [P, D])
        bg0b = sb("bg0b", [P, P])
        bmap = sb("bmap", [P, T])
        adjT = sb("adjT", [P, 2, T])
        bsum = sb("bsum", [P, SKIP * 4])
        wihT = sb("wihT", [P, SKIP, 4 * D])
        whhT = sb("whhT", [P, SKIP - 1, 4 * D])
        W1h = sb("W1h", [P, E, HT, P], F16)
        W1l = sb("W1l", [P, E, HT, P], F16)
        W2h = sb("W2h", [P, E, HT, D], F16)
        W2l = sb("W2l", [P, E, HT, D], F16)

        st = sb("st", [P, GT, 6])
        stat = sb("stat", [P, 8, GT])
        stat_all = sb("stat_all", [P, 2, NT])
        bnst = sb("bnst", [P, 2, NCH, 6])
        bnag = sb("bnag", [P, 2, 2])
        route = {k: sb(f"route_{k}", [P, GT, E]) for k in ("L", "a", "b", "oh1", "oh2", "sm")}
        M16 = sb("M16", [P, GT, E], BF16)
        ejt = sb("ejt", [P, E, GT])
        ejc = sb("ejc", [P, E, GT])
        r16 = sb("r16", [P, 6, GT])
        r8 = sb("r8", [P, 4, E])
        gtk = sb("gtk", [P, E, KMAX])
        geb = sb("geb", [1, NBLK, E - 1])
        ids = sb("ids", [1, 2 * G, NBLK + 1], I32)
        slot = sb("slot", [P, 2 * G, TOP_K, GT], I32)
        wts = sb("wts", [P, 2 * G, TOP_K, GT])

        ARENA = 9744
        arena = sb("arena", [P, ARENA])
        used = [0]

        def area(n):
            a = used[0]
            used[0] += n
            assert used[0] <= ARENA, used[0]
            return arena[:, a:a + n]

        adj_n = area(2 * T).rearrange("p (t m) -> p t m", t=2)
        adj_i = area(2 * T).rearrange("p (t m) -> p t m", t=2)
        adj_it = area(2 * T).rearrange("p (t m) -> p t m", t=2)
        ahatT = area(2 * T).rearrange("p (t m) -> p t m", t=2)
        deg = area(16).rearrange("p (k t) -> p k t", t=2)
        gw1 = area(2 * D).rearrange("p (t d) -> p t d", t=2)
        gw2 = area(GH)
        w1T = area(GH)
        w2T = area(2 * D).rearrange("p (t d) -> p t d", t=2)
        xn = [area(4 * D).rearrange("p (t d) -> p t d", t=4) for _ in range(2)]
        agg = [area(512) for _ in range(2)]
        hb = [area(1024).rearrange("p (t n) -> p t n", t=2) for _ in range(2)]
        lstm_raw = area(4 * D).rearrange("p (t d) -> p t d", t=4)
        wstage = [area(H) for _ in range(4)]
        used[0] = 0
        ygat = area(GT * TOP_K * D).rearrange("p (t k d) -> p t k d", k=TOP_K, t=GT)
        wstage1 = [area(H) for _ in range(4)]
        hh, hl = ([area(HT * BLK // 2).bitcast(F16).rearrange("p (t n) -> p t n", t=HT) for _ in range(2)]
                  for _ in range(2))
        ybn = [area(512) for _ in range(2)]
        lnx = [carve(1, GT * D).rearrange("p (t d) -> p t d", t=GT) for _ in range(2)]
        hf = carve(1, HT * BLK)
        xrow = [carve(1, 2 * D).rearrange("p (h d) -> p h d", h=2) for _ in range(2)]
        yb_out = [carve(1, 2 * D).rearrange("p (h d) -> p h d", h=2) for _ in range(2)]
        xh, xlo = ([carve(1, BLK // 2).bitcast(F16) for _ in range(2)] for _ in range(2))
        lxT = [carve(1, 512) for _ in range(2)]
        zero = carve(1, 512)
        zT = carve(0, QT * P)
        h1T = carve(0, QT * P)
        xl = carve(0, QT * D).rearrange("p (t d) -> p t d", t=QT)
        u2 = xl
        hT = carve(0, QT * P)
        gate = carve(0, 4 * 512).rearrange("p (k n) -> p k n", k=4)
        cell = carve(0, 512)
        tcell = carve(0, 512)
        tmp = zT[:, 0:512]
        hcur = h1T[:, 0:512]

        ps = ctx.enter_context(nc.psum_tensor("ps", [P, 8, 512], F32))

        def bank(i):
            return ps[:, i, :]

        s_cst = sem("s_cst")
        s_par = sem("s_par")
        s_adj = sem("s_adj")
        s_rows = sem("s_rows")
        s_xin = [sem(f"s_xin{i}") for i in range(2)]
        s_lraw = sem("s_lraw")
        s_wst = [sem(f"s_wst{i}") for i in range(4)]
        s_zero = sem("s_zero")
        s_zfill = sem("s_zfill")
        s_tr = sem("s_tr")
        s_ev = sem("s_ev")
        s_asq = sem("s_asq")
        s_need = sem("s_need")
        s_wT = sem("s_wT")
        s_fold = sem("s_fold")
        s_wh = sem("s_wh")
        s_wl = sem("s_wl")
        s_xn = sem("s_xn")
        s_agg = sem("s_agg")
        s_agc = sem("s_agc")
        s_h1 = sem("s_h1")
        s_h1c = sem("s_h1c")
        s_bn1 = sem("s_bn1")
        s_relu = sem("s_relu")
        s_o2 = sem("s_o2")
        s_o2c = sem("s_o2c")
        s_bn2 = sem("s_bn2")
        s_yb = sem("s_yb")
        s_yt = sem("s_yt")
        s_x2 = sem("s_x2")
        s_lx = sem("s_lx")
        s_lt = sem("s_lt")
        s_ltc = sem("s_ltc")
        s_lg = sem("s_lg")
        s_exn = sem("s_exn")
        s_exd = sem("s_exd")
        s_m = sem("s_m")
        s_cnt = sem("s_cnt")
        s_rt = sem("s_rt")
        s_sc = [sem(f"s_sc{i}") for i in range(2)]
        s_xr = [sem(f"s_xr{i}") for i in range(2)]
        s_T = sem("s_T")
        s_xs = sem("s_xs")
        s_U = sem("s_U")
        s_gl = sem("s_gl")
        s_hl = sem("s_hl")
        s_D = sem("s_D")
        s_y = sem("s_y")
        s_yo = [sem(f"s_yo{i}") for i in range(2)]
        s_ga = sem("s_ga")
        s_cb = sem("s_cb")
        s_out = sem("s_out")
        c_need = sem("c_need")
        c_rt = sem("c_rt")
        c_xl = sem("c_xl")
        c_z = sem("c_z")
        c_zt = sem("c_zt")
        c_w0 = sem("c_w0")
        c_hp = sem("c_hp")
        c_h1 = sem("c_h1")
        c_u = sem("c_u")
        c_u2 = sem("c_u2")
        c_g = sem("c_g")
        c_hT = sem("c_hT")
        c_gp = sem("c_gp")
        c_ga = sem("c_ga")
        c_c = sem("c_c")
        c_tc = sem("c_tc")
        c_h = sem("c_h")
        c_bk = sem("c_bk")
        c_x3 = sem("c_x3")
        d_ch = sem("d_ch")
        a_ch = sem("a_ch")
        step = {k: sem(f"step_{k}") for k in ("pe", "act", "dve")}

        block = ctx.enter_context(nc.Block())

        def begin_step(eng, me, k):
            if k > 0:
                for other in step:
                    if other != me:
                        eng.wait_ge(step[other], k)

        def end_step(eng, me):
            eng.drain().then_inc(step[me], 1)

        PAR_DMAS = 14

        @block.sync
        def _(sp):
            par = [0]

            def load(dst, src):
                par[0] += 1
                sp.dma_start(dst, src).then_inc(s_par, 16)

            sp.dma_start(xt[:, 0:NT // 2, :], x_t[:, 0:NT // 2, :]).then_inc(s_xin[0], 16)
            sp.dma_start(adj_n, adj.rearrange("(t p) m -> p t m", p=P)).then_inc(s_adj, 16)
            nrows = 0
            for r, src in ((R_FB1[0], L0_ffn_b1.rearrange("e (t p) -> (e t) p", p=P)),
                           (R_FB1[1], L1_ffn_b1.rearrange("e (t p) -> (e t) p", p=P)),
                           (R_LNG, L0_ffn_ln_g), (R_LNB, L0_ffn_ln_b),
                           (R_B1, L0_gnn_b1.rearrange("(t p) -> t p", p=P)),
                           (R_G1, L0_gnn_g1.rearrange("(t p) -> t p", p=P)),
                           (R_BE1, L0_gnn_be1.rearrange("(t p) -> t p", p=P)),
                           (R_B2, L0_gnn_b2.rearrange("(t p) -> t p", p=P)),
                           (R_G2, L0_gnn_g2.rearrange("(t p) -> t p", p=P)),
                           (R_BE2, L0_gnn_be2.rearrange("(t p) -> t p", p=P)),
                           (R_BIH, L1_gnn_bih.rearrange("s (t p) -> (s t) p", p=P)),
                           (R_BHH, L1_gnn_bhh.rearrange("s (t p) -> (s t) p", p=P))):
                sp.dma_start(rows[r:r + src.shape[0], :], src).then_inc(s_rows, 16)
                nrows += 1
            assert nrows == 12
            load(gw1, L0_gnn_W1.rearrange("(t p) d -> p t d", p=P))
            load(gw2, L0_gnn_W2)
            load(Wr[:, 0, :], L0_ffn_Wr)
            load(Wr[:, 1, :], L1_ffn_Wg)
            load(brb[:, 0, :], L0_ffn_br.partition_broadcast(P))
            load(brb[:, 1, :], L1_ffn_bg.partition_broadcast(P))
            load(Wg[:, 0, :], L1_gnn_Wg0)
            load(Wg[:, 1, :], L1_gnn_Wg1)
            load(bg1b[:, :], L1_gnn_bg1.partition_broadcast(P))
            load(bg0b[:, :], L1_gnn_bg0.partition_broadcast(P))
            load(eb2[0][:, :, :], L0_ffn_b2.partition_broadcast(P))
            load(eb2[1][:, :, :], L1_ffn_b2.partition_broadcast(P))
            par[0] += 2
            assert par[0] == PAR_DMAS
            sp.dma_start(xt[:, NT // 2:, :], x_t[:, NT // 2:, :]).then_inc(s_xin[1], 16)
            for k in range(2 * SKIP - 1):
                src = L1_gnn_Wih[k] if k < SKIP else L1_gnn_Whh[k - SKIP + 1]
                if k > 0:
                    sp.wait_ge(s_wT, k)
                sp.dma_start(lstm_raw, src.rearrange("(t p) d -> p t d", p=P)).then_inc(s_lraw, 16)

            def weights(l, bufs, first):
                for k in range(2 * E):
                    n = 2 * E * l + k
                    e = k // 2
                    if n - first >= 4:
                        sp.wait_ge(s_wl, n - 3)
                        if l == 0:
                            sp.wait_ge(s_fold, min(E, (n - 4) // 2 + 1))
                    src = fW1[l][e] if k % 2 == 0 else fW2[l][e].rearrange("(t p) d -> p t d", p=P)
                    dst = bufs[n % 4] if k % 2 == 0 else bufs[n % 4].rearrange("p (t d) -> p t d", d=D)
                    sp.dma_start(dst, src).then_inc(s_wst[n % 4], 16)

            weights(0, wstage, 0)
            sp.wait_ge(s_bn2, 1)
            sp.wait_ge(s_zero, 1)
            for s in slots_in:
                for r in range(0, SLOTS, 4 * P):
                    n = min(4 * P, SLOTS - r)
                    sp.dma_start(s[r:r + n, :].rearrange("(p a) d -> p (a d)", a=4), zero[0:n // 4, :])\
                      .then_inc(s_zfill, 16)

            def experts(m, inst):
                n_s = prep_order.index(inst)
                sp.wait_ge(s_sc[n_s % 2], 16 * GT * TOP_K * (n_s // 2 + 1))
                src = slots_in[n_s % 2].rearrange("(b p h) d -> b p h d", p=P, h=2)
                dst = slots_out[inst].rearrange("(b p h) d -> b p h d", p=P, h=2)

                def load_block(i, par):
                    sp.dma_start(xrow[par], src[bass.ds(i, 1)].rearrange("a p h d -> (a p) h d"))\
                      .then_inc(s_xr[par], 16)

                def store_block(i, par):
                    sp.wait_ge(s_y, m * NBLK + i + 1)
                    sp.dma_start(dst[bass.ds(i, 1)].rearrange("a p h d -> (a p) h d"), yb_out[par])\
                      .then_inc(s_yo[par], 16)

                load_block(0, 0)
                load_block(1, 1)
                for i in range(2):
                    sp.wait_ge(s_T, m * NBLK + i + 1)
                    load_block(i + 2, i)
                with sp.Fori(1, NBLK // 2 - 1) as j:
                    for q in range(2):
                        sp.wait_ge(s_T, m * NBLK + 2 * j + q + 1)
                        load_block(2 * j + 2 + q, q)
                        store_block(2 * j + q - 2, q)
                sp.wait_ge(s_T, m * NBLK + NBLK - 2)
                load_block(NBLK - 1, 0)
                for i in range(NBLK - 5, NBLK):
                    store_block(i, i % 2)

            done1 = 0
            m = 0
            for s in plan:
                if s[0] == "W":
                    sp.wait_ge(step["pe"], plan.index(s))
                    sp.wait_ge(step["act"], plan.index(s))
                    sp.wait_ge(step["dve"], plan.index(s))
                    weights(1, wstage1, 2 * E)
                if s[0] == "X":
                    experts(m, s[1:])
                    m += 1
                if s[0] == "D" and s[1] == 1:
                    sp.wait_ge(s_cb, combine_order.index(s[1:]) + 1)
                    sp.dma_start(out_t[:, s[2] * GT:(s[2] + 1) * GT, :], xt[:, s[2] * GT:(s[2] + 1) * GT, :])\
                      .then_inc(s_out, 16)
                    done1 += 1
            if dump:
                for k in step:
                    sp.wait_ge(step[k], len(plan))
                sp.dma_start(out_t, xt[:, :, :]).then_inc(s_out, 16)
                done1 += 1
            sp.wait_ge(s_out, 16 * done1)
            for par in range(2):
                sp.wait_ge(s_yo[par], 16 * m * ((NBLK + 1 - par) // 2)) if m else None

        @block.gpsimd
        def _(pool):
            pool.memset(ident[:, :], 0.0).then_inc(s_cst, 1)
            pool.memset(tri[:, :], 1.0).then_inc(s_cst, 1)
            pool.memset(ones[:, :], 1.0).then_inc(s_cst, 1)
            pool.memset(one8[:, :], 1.0).then_inc(s_cst, 1)
            pool.memset(ej_mask[:, :], 1.0).then_inc(s_cst, 1)
            pool.iota(desc[:, :], [[-1, E]], base=E, channel_multiplier=0,
                      allow_small_or_imprecise_dtypes=True).then_inc(s_cst, 1)
            pool.iota(k_blk[:, :], [[BLK, KMAX]], base=0, channel_multiplier=0,
                      allow_small_or_imprecise_dtypes=True).then_inc(s_cst, 1)
            pool.iota(iota_b[:, :], [[1, NBLK]], base=0, channel_multiplier=0,
                      allow_small_or_imprecise_dtypes=True).then_inc(s_cst, 1)
            pool.wait_ge(s_cst, 8)
            pool.affine_select(out=ident[:, :], in_=ident[:, :], compare_op=ALU.not_equal, fill=1.0, base=0,
                               pattern=[[-1, P]], channel_multiplier=1).then_inc(s_cst, 1)
            pool.affine_select(out=tri[:, :], in_=tri[:, :], compare_op=ALU.is_gt, fill=0.0, base=0,
                               pattern=[[1, P]], channel_multiplier=-1).then_inc(s_cst, 1)
            pool.affine_select(out=ej_mask[:, :].rearrange("p (e t) -> p e t", e=E),
                               in_=ej_mask[:, :].rearrange("p (e t) -> p e t", e=E),
                               compare_op=ALU.is_gt, fill=0.0, base=0,
                               pattern=[[0, E], [1, GT]], channel_multiplier=0).then_inc(s_cst, 1)
            pool.wait_ge(s_bn2, 1)
            pool.memset(zero, 0.0).then_inc(s_zero, 1)
            if len(plan) > 1:
                pool.wait_ge(s_zfill, 16 * 2 * (-(-SLOTS // (4 * P))))
            for what, l, g in pool_order:
                if what == "scatter":
                    n = prep_order.index((l, g))
                    pool.wait_ge(s_rt, n + 1)
                    if n >= 2:
                        mm = expert_order.index(prep_order[n - 2])
                        pool.wait_ge(s_T, (mm + 1) * NBLK)
                    for t in range(GT):
                        for k in range(TOP_K):
                            pool.indirect_dma_start(
                                slots_in[n % 2], bass.IndirectOffsetOnAxis(ap=slot[:, G * l + g, k, t:t + 1], axis=0),
                                lnx[n % 2][:, t, :], None).then_inc(s_sc[n % 2], 16)
                else:
                    m = expert_order.index((l, g))
                    if m > 0:
                        pool.wait_ge(s_cb, m)
                    pool.wait_ge(s_yo[0], 16 * (m + 1) * ((NBLK + 1) // 2))
                    pool.wait_ge(s_yo[1], 16 * (m + 1) * (NBLK // 2))
                    for t in range(GT):
                        for k in range(TOP_K):
                            pool.indirect_dma_start(
                                ygat[:, t, k, :], None, slots_out[(l, g)],
                                bass.IndirectOffsetOnAxis(ap=slot[:, G * l + g, k, t:t + 1], axis=0))\
                                .then_inc(s_ga, 16)
            if pool_order:
                ng = len(expert_order)
                pool.wait_ge(s_ga, 16 * GT * TOP_K * ng)

        @block.tensor
        def _(pe):
            mm = pe.matmul

            def setup():
                pe.wait_ge(s_cst, 11)
                pe.wait_ge(s_adj, 16)
                for mt in range(2):
                    for nt in range(2):
                        last = pe.transpose(ps[:, 0, mt * T + nt * P:mt * T + (nt + 1) * P],
                                            adj_n[:, nt, mt * P:(mt + 1) * P], ident[:, :])
                last.then_inc(s_tr, 1)
                pe.wait_ge(s_rows, 16 * 12)
                pe.transpose(ps[:, 1, 0:R_ROWS], rows[0:R_ROWS, :], ident[0:R_ROWS, 0:R_ROWS]).then_inc(s_tr, 1)
                pe.wait_ge(s_par, 16 * (PAR_DMAS - 2))
                for t in range(2):
                    pe.transpose(ps[:, 2, t * P:(t + 1) * P], gw1[:, t, :], ident[:, :])
                for t in range(2):
                    last = pe.transpose(ps[:, 2, GH + t * P:GH + (t + 1) * P], gw2[:, t * P:(t + 1) * P], ident[:, :])
                last.then_inc(s_tr, 1)
                pe.wait_ge(s_ev, 1)
                for k in range(2):
                    last = mm(ps[:, 3, 0:T], bg0b[:, :], adjT[:, k, :], start=(k == 0), stop=(k == 1))
                last.then_inc(s_tr, 1)
                pe.wait_ge(s_ev, 4)
                for mt in range(2):
                    for nt in range(2):
                        last = pe.transpose(ps[:, 4, mt * T + nt * P:mt * T + (nt + 1) * P],
                                            adj_i[:, nt, mt * P:(mt + 1) * P], ident[:, :])
                last.then_inc(s_tr, 1)
                pe.wait_ge(s_ev, 6)

            def graph0():
                def aggregate(c, q, first=False):
                    pe.wait_ge(s_xn, c + 1)
                    if not first:
                        pe.wait_ge(s_agc, c - 1)
                    for b in range(2):
                        for k in range(2):
                            last = mm(ps[:, q, b * T:(b + 1) * T], xn[q][:, 2 * b + k, :], ahatT[:, k, :],
                                      start=(k == 0), stop=(k == 1))
                    last.then_inc(s_agg, 1)

                def hidden(c, q, first=False):
                    pe.wait_ge(s_agc, c + 1)
                    if not first:
                        pe.wait_ge(s_h1c, 2 * c - 2)
                    for o in range(2):
                        mm(ps[:, 2 + 2 * q + o, :], w1T[:, o * P:(o + 1) * P], agg[q], start=True, stop=True)\
                            .then_inc(s_h1, 1)

                aggregate(0, 0, True)
                aggregate(1, 1, True)
                hidden(0, 0, True)
                aggregate(2, 0)
                hidden(1, 1, True)
                with pe.Fori(1, NCH // 2 - 1) as j:
                    for q in range(2):
                        c = 2 * j + q
                        aggregate(c + 1, 1 - q)
                        hidden(c, q)
                aggregate(NCH - 1, 1)
                hidden(NCH - 2, 0)
                hidden(NCH - 1, 1)

                def output(c, q, first=False):
                    pe.wait_ge(s_relu, 2 * c + 2)
                    if not first:
                        pe.wait_ge(s_o2c, c - 1)
                    for k in range(2):
                        last = mm(ps[:, 6 + q, :], w2T[:, k, :], hb[q][:, k, :], start=(k == 0), stop=(k == 1))
                    last.then_inc(s_o2, 1)

                output(0, 0, True)
                output(1, 1, True)
                with pe.Fori(1, NCH // 2) as j:
                    for q in range(2):
                        output(2 * j + q, q)

            def lstm_weights():
                for k in range(2 * SKIP - 1):
                    pe.wait_ge(s_lraw, 16 * (k + 1))
                    if k >= 2:
                        pe.wait_ge(s_wh, k - 1)
                    for t in range(4):
                        last = pe.transpose(ps[:, k % 2, t * P:(t + 1) * P], lstm_raw[:, t, :], ident[:, :])
                    last.then_inc(s_wT, 1)

            def fold_bias():
                for e in range(E):
                    n = 2 * e
                    pe.wait_ge(s_wst[n % 4], 16 * (n // 4 + 1))
                    for t in range(HT):
                        last = mm(ps[:, 2, e * HT + t:e * HT + t + 1], wstage[n % 4][:, t * P:(t + 1) * P],
                                  vec[:, R_LNB + e:R_LNB + e + 1], start=True, stop=True)
                    last.then_inc(s_fold, 1)

            def prep(n, l, g):
                if l == 0:
                    for c in range(GT // 4):
                        pe.wait_ge(s_yb, g * (GT // 4) + c + 1)
                        if c >= 2:
                            pe.wait_ge(s_x2, g * (GT // 4) + c - 1)
                        for t in range(4):
                            last = pe.transpose(ps[:, c % 2, t * P:(t + 1) * P], ybn[c % 2][:, t * P:(t + 1) * P],
                                                ident[:, :])
                        last.then_inc(s_yt, 1)
                pe.wait_ge(s_lx, n + 1)
                for c in range(GT // 4):
                    for t in range(4):
                        last = pe.transpose(ps[:, 2 + c, t * P:(t + 1) * P], lnx[n % 2][:, 4 * c + t, :], ident[:, :])
                    last.then_inc(s_lt, 1)
                for c in range(GT // 4):
                    pe.wait_ge(s_ltc, n * (GT // 4) + c + 1)
                    for t in range(4):
                        j = 4 * c + t
                        last = mm(ps[:, 6, j * E:(j + 1) * E], lxT[c % 2][:, t * P:(t + 1) * P], Wr[:, l, :],
                                  start=True, stop=True)
                    last.then_inc(s_lg, 1)
                pe.wait_ge(s_m, n + 1)
                m2 = M16[:, :, :].rearrange("p t e -> p (t e)")
                mm(ps[:, 7, 0:GT * E], tri[:, :], m2, start=True, stop=True)
                mm(ps[:, 7, 128:128 + GT * E], ones[:, :], m2, start=True, stop=True).then_inc(s_cnt, 1)

            def experts(m, l, g):
                inst = G * l + g
                lo = m * NBLK

                def transposes(i, q):
                    k = m * ((NBLK + 1 - q) // 2) + (i // 2 if isinstance(i, int) else i[0])
                    idx = i if isinstance(i, int) else i[1]
                    pe.wait_ge(s_xr[q], 16 * (k + 1))
                    if not (isinstance(idx, int) and idx < 2):
                        pe.wait_ge(s_xs, lo + idx - 1)
                    for h in range(2):
                        last = pe.transpose(ps[:, 6 + q, h * P:(h + 1) * P], xrow[q][:, h, :], ident[:, :])
                    last.then_inc(s_T, 1)

                def up(i, q):
                    e = pe.value_load(ids[0:1, inst, bass.ds(i, 1)], min_val=0, max_val=E - 1)
                    pe.wait_ge(s_xs, lo + i + 1)
                    for hp in range(2):
                        if not (isinstance(i, int) and i < 2):
                            pe.wait_ge(s_gl, 2 * (lo + i - 2) + hp + 1)
                        for ht in (2 * hp, 2 * hp + 1):
                            o = ps[:, 2 * q + hp, (ht % 2) * BLK:(ht % 2 + 1) * BLK]
                            wh = W1h[:, bass.ds(e, 1), ht, :].rearrange("p a c -> p (a c)")
                            wl = W1l[:, bass.ds(e, 1), ht, :].rearrange("p a c -> p (a c)")
                            mm(o, wh, xh[q], start=True, stop=False)
                            mm(o, wh, xlo[q], start=False, stop=False)
                            last = mm(o, wl, xh[q], start=False, stop=True)
                        last.then_inc(s_U, 1)

                def down(i, q):
                    e = pe.value_load(ids[0:1, inst, bass.ds(i, 1)], min_val=0, max_val=E - 1)
                    if not (isinstance(i, int) and i < 2):
                        pe.wait_ge(s_y, lo + i - 1)
                    pe.wait_ge(s_hl, 2 * (lo + i) + 2)
                    for h in range(2):
                        o = ps[:, 4 + q, h * P:(h + 1) * P]
                        for kt in range(HT):
                            wh = W2h[:, bass.ds(e, 1), kt, :].rearrange("p a c -> p (a c)")
                            wl = W2l[:, bass.ds(e, 1), kt, :].rearrange("p a c -> p (a c)")
                            a = hh[q][:, kt, h * P:(h + 1) * P]
                            mm(o, a, wh, start=(kt == 0), stop=False)
                            mm(o, a, wl, start=False, stop=False)
                            last = mm(o, hl[q][:, kt, h * P:(h + 1) * P], wh, start=False, stop=(kt == HT - 1))
                    last.then_inc(s_D, 1)

                transposes(0, 0)
                transposes(1, 1)
                up(0, 0)
                transposes(2, 0)
                up(1, 1)
                down(0, 0)
                with pe.Fori(1, NBLK // 2) as j:
                    for q in range(2):
                        i = 2 * j + q
                        transposes((j + q, i + 1), 1 - q)
                        up(i, q)
                        down(i - 1, 1 - q)
                up(NBLK - 1, 0)
                down(NBLK - 2, 1)
                down(NBLK - 1, 0)

            def graph1(g):
                hv = hT.rearrange("p (b t) -> p b t", b=4)
                with pe.Fori(2 * g, 2 * g + 2) as n:
                    pe.wait_ge(c_xl, n + 1)
                    pe.wait_ge(c_x3, 2 * n)
                    for b in range(4):
                        for k in range(2):
                            last = mm(ps[:, b // 2, (b % 2) * T:(b % 2 + 1) * T], xl[:, 2 * b + k, :], adjT[:, k, :],
                                      start=(k == 0), stop=(k == 1))
                        if b % 2:
                            last.then_inc(c_z, 1)
                    for h in range(2):
                        pe.wait_ge(c_zt, 2 * n + h + 1)
                        mm(ps[:, 2 + h, :], Wg[:, 0, :], zT[:, h * 512:(h + 1) * 512], start=True, stop=True)\
                            .then_inc(c_w0, 1)
                    for h in range(2):
                        pe.wait_ge(c_h1, 2 * n + h + 1)
                        for t in range(4):
                            last = mm(ps[:, 4 + h, t * P:(t + 1) * P], h1T[:, (4 * h + t) * P:(4 * h + t + 1) * P],
                                      Wg[:, 1, :], start=True, stop=True)
                        last.then_inc(c_u, 1)
                    for b in range(4):
                        if b % 2 == 0:
                            pe.wait_ge(c_u2, 2 * n + b // 2 + 1)
                        for k in range(2):
                            last = mm(ps[:, 6 + b // 2, (b % 2) * T:(b % 2 + 1) * T], u2[:, 2 * b + k, :],
                                      adjT[:, k, :], start=(k == 0), stop=(k == 1))
                        if b % 2:
                            last.then_inc(c_g, 1)
                    pe.wait_ge(c_hT, 2 * n + 2)
                    lo = n * GATES_PER_QUAD
                    seen = 0
                    bank_last = [0] * 8
                    for k, (p, s, half) in enumerate(LSTM_STEPS):
                        gates = (0, 2, 3) if s == 0 else (0, 1, 2, 3)
                        nw = T // p
                        nb = 2 if p == 1 else 4
                        xin = hv[:, nb * half:nb * half + nb, s:s + (nw - 1) * p + 1:p]
                        w = nb * nw
                        if s == 0 and not (p == 1 and half == 1) and k > 0:
                            pe.wait_ge(c_h, n * len(LSTM_STEPS) + k)
                        for gt in gates:
                            bk = 4 * (k % 2) + gt
                            if bank_last[bk]:
                                pe.wait_ge(c_ga, lo + bank_last[bk])
                            last = mm(ps[:, bk, 0:w], wihT[:, p - 1, gt * P:(gt + 1) * P], xin,
                                      start=True, stop=(s == 0))
                            if s == 0:
                                seen += 1
                                bank_last[bk] = seen
                                last.then_inc(c_gp, 1)
                        if s > 0:
                            pe.wait_ge(c_h, n * len(LSTM_STEPS) + k)
                            for gt in gates:
                                bk = 4 * (k % 2) + gt
                                seen += 1
                                bank_last[bk] = seen
                                mm(ps[:, bk, 0:w], whhT[:, p - 2, gt * P:(gt + 1) * P], hcur[:, 0:w],
                                   start=False, stop=True).then_inc(c_gp, 1)
                    assert seen == GATES_PER_QUAD
                    pe.wait_ge(c_h, (n + 1) * len(LSTM_STEPS))
                    pe.wait_ge(c_ga, lo + seen)
                    for h in range(2):
                        for t in range(4):
                            last = pe.transpose(ps[:, h, t * P:(t + 1) * P], hT[:, (4 * h + t) * P:(4 * h + t + 1) * P],
                                                ident[:, :])
                        last.then_inc(c_bk, 1)

            m = 0
            for k, s in enumerate(plan):
                begin_step(pe, "pe", k)
                if s[0] == "A":
                    setup()
                    graph0()
                    lstm_weights()
                    fold_bias()
                elif s[0] == "P":
                    prep(prep_order.index(s[1:]), *s[1:])
                elif s[0] == "X":
                    experts(m, *s[1:])
                    m += 1
                elif s[0] == "C":
                    graph1(s[1])
                end_step(pe, "pe")

        @block.scalar
        def _(act):
            ch = Chain(act, a_ch)
            roots = [0]

            def root(dst, src, scale, bias):
                roots[0] += 1
                act.wait_ge(s_need, roots[0])
                act.activation(dst, src, ACT.Sqrt, bias=bias, scale=scale).then_inc(s_asq, 1)

            def ln_root(ntiles):
                root(stat[:, 4, 0:ntiles], stat[:, 3, 0:ntiles], 1.0, 0.0)

            def setup_and_graph0():
                root(deg[:, 4, :], deg[:, 3, :], 1.0, 0.0)
                for k in range(NT // GT):
                    ln_root(GT)
                def copy_aggregate(c, q, first=False):
                    act.wait_ge(s_agg, c + 1)
                    if not first:
                        act.wait_ge(s_h1, 2 * c - 2)
                    act.activation(agg[q], bank(q), ACT.Copy).then_inc(s_agc, 1)

                def copy_hidden(c, q):
                    for o in range(2):
                        act.wait_ge(s_h1, 2 * c + o + 1)
                        act.activation(hid[:, o, bass.ds(c * 512, 512)], bank(2 + 2 * q + o), ACT.Identity,
                                       bias=vec[:, R_B1 + o:R_B1 + o + 1]).then_inc(s_h1c, 1)

                copy_aggregate(0, 0, True)
                copy_aggregate(1, 1, True)
                copy_hidden(0, 0)
                copy_aggregate(2, 0)
                copy_hidden(1, 1)
                with act.Fori(1, NCH // 2 - 1) as j:
                    for q in range(2):
                        copy_aggregate(2 * j + q + 1, 1 - q)
                        copy_hidden(2 * j + q, q)
                copy_aggregate(NCH - 1, 1)
                copy_hidden(NCH - 2, 0)
                copy_hidden(NCH - 1, 1)
                root(bnag[:, :, 1], bnag[:, :, 1], 1.0, 0.0)
                act.wait_ge(s_bn1, 1)

                def normalise_hidden(c, q, first=False):
                    if not first:
                        act.wait_ge(s_o2, c - 1)
                    for o in range(2):
                        act.activation(hb[q][:, o, :], hid[:, o, bass.ds(c * 512, 512)], ACT.Relu,
                                       bias=bn1t[:, o:o + 1], scale=bn1s[:, o:o + 1]).then_inc(s_relu, 1)

                normalise_hidden(0, 0, True)
                normalise_hidden(1, 1, True)
                with act.Fori(1, NCH // 2) as j:
                    for q in range(2):
                        normalise_hidden(2 * j + q, q)
                root(bnag[:, 0, 1:2], bnag[:, 0, 1:2], 1.0, 0.0)
                for k in range(2 * SKIP - 1):
                    act.wait_ge(s_wT, k + 1)
                    dst = wihT[:, k, :] if k < SKIP else whhT[:, k - SKIP, :]
                    act.activation(dst, bank(k % 2), ACT.Copy).then_inc(s_wh, 1)

            def weights(l, bufs):
                for k in range(2 * E):
                    n = 2 * E * l + k
                    e = k // 2
                    act.wait_ge(s_wst[n % 4], 16 * (n // 4 + 1))
                    dst = (W1h if k % 2 == 0 else W2h)[:, e, :, :].rearrange("p t c -> p (t c)")
                    scale = lng_s[:, e:e + 1] if l == 0 and k % 2 == 0 else SC
                    act.activation(dst, bufs[n % 4], ACT.Copy, scale=scale).then_inc(s_wh, 1)

            def prep(n, l, g):
                if l == 0:
                    for c in range(GT // 4):
                        if c >= 2:
                            act.wait_ge(s_yt, g * (GT // 4) + c - 1)
                        act.activation(ybn[c % 2], o2T[:, (g * (GT // 4) + c) * 512:(g * (GT // 4) + c + 1) * 512],
                                       ACT.Identity, bias=bn2t[:, 0:1], scale=bn2s[:, 0:1]).then_inc(s_yb, 1)
                ln_root(GT)
                for c in range(GT // 4):
                    act.wait_ge(s_lt, n * (GT // 4) + c + 1)
                    if c >= 2:
                        act.wait_ge(s_lg, n * (GT // 4) + c - 1)
                    act.activation(lxT[c % 2], bank(2 + c), ACT.Copy).then_inc(s_ltc, 1)
                if l == 0:
                    ln_root(GT)
                act.wait_ge(s_exn, n + 1)
                act.activation(r16[:, 2, :], r16[:, 2, :], ACT.Exp).then_inc(s_exd, 1)

            def experts(m, l, g):
                inst = G * l + g
                lo = m * NBLK

                def gelu(i, q):
                    e = act.value_load(ids[0:1, inst, bass.ds(i, 1)], min_val=0, max_val=E - 1)
                    for hp in range(2):
                        act.wait_ge(s_U, 2 * (lo + i) + hp + 1)
                        if not (isinstance(i, int) and i < 1):
                            act.wait_ge(s_hl, 2 * (lo + i - 1) + hp + 1)
                        if not (isinstance(i, int) and i < 2):
                            act.wait_ge(s_D, lo + i - 1)
                        for ht in (2 * hp, 2 * hp + 1):
                            ch.mark(act.activation(hf[:, ht * BLK:(ht + 1) * BLK],
                                                   ps[:, 2 * q + hp, (ht % 2) * BLK:(ht % 2 + 1) * BLK], ACT.Gelu,
                                                   bias=eb1[:, l, bass.ds(e * HT + ht, 1)], scale=UNSC))
                        ch.wait()
                        act.activation(hh[q][:, 2 * hp:2 * hp + 2, :].rearrange("p t n -> p (t n)"),
                                       hf[:, hp * 2 * BLK:(hp + 1) * 2 * BLK], ACT.Copy, scale=SC).then_inc(s_gl, 1)

                gelu(0, 0)
                gelu(1, 1)
                with act.Fori(1, NBLK // 2) as j:
                    ch.enter(j - 1, 8)
                    gelu(2 * j, 0)
                    gelu(2 * j + 1, 1)
                    ch.leave(NBLK // 2 - 1)
                gelu(NBLK - 1, 0)

            def graph1(g):
                with act.Fori(2 * g, 2 * g + 2) as n:
                    act.wait_ge(c_need, n + 1)
                    act.activation(stat[:, 4, 0:QT], stat[:, 3, 0:QT], ACT.Sqrt).then_inc(c_rt, 1)
                    for h in range(2):
                        act.wait_ge(c_z, 2 * n + h + 1)
                        act.activation(zT[:, h * 512:(h + 1) * 512], bank(h), ACT.Copy).then_inc(c_zt, 1)
                    for h in range(2):
                        act.wait_ge(c_hp, 2 * n + h + 1)
                        v = h1T[:, h * 512:(h + 1) * 512]
                        act.activation(v, v, ACT.Relu).then_inc(c_h1, 1)
                    for h in range(2):
                        act.wait_ge(c_g, 2 * n + h + 1)
                        act.activation(hT[:, h * 512:(h + 1) * 512], bank(6 + h), ACT.Relu).then_inc(c_hT, 1)
                    seen = 0
                    for k, (p, s, half) in enumerate(LSTM_STEPS):
                        gates = (0, 2, 3) if s == 0 else (0, 1, 2, 3)
                        w = (T // p) * (2 if p == 1 else 4)
                        if k > 0:
                            act.wait_ge(c_h, n * len(LSTM_STEPS) + k)
                        for gt in gates:
                            seen += 1
                            act.wait_ge(c_gp, n * GATES_PER_QUAD + seen)
                            act.activation(gate[:, gt, 0:w], ps[:, 4 * (k % 2) + gt, 0:w],
                                           ACT.Tanh if gt == 2 else ACT.Sigmoid,
                                           bias=bsum[:, (p - 1) * 4 + gt:(p - 1) * 4 + gt + 1]).then_inc(c_ga, 1)
                        act.wait_ge(c_c, n * len(LSTM_STEPS) + k + 1)
                        act.activation(tcell[:, 0:w], cell[:, 0:w], ACT.Tanh).then_inc(c_tc, 1)

            m = 0
            for k, s in enumerate(plan):
                begin_step(act, "act", k)
                if s[0] == "A":
                    setup_and_graph0()
                    weights(0, wstage)
                elif s[0] == "P":
                    prep(prep_order.index(s[1:]), *s[1:])
                elif s[0] == "X":
                    experts(m, *s[1:])
                    m += 1
                elif s[0] == "W":
                    weights(1, wstage1)
                elif s[0] == "C":
                    graph1(s[1])
                end_step(act, "act")

        @block.vector
        def _(dve):
            ch = Chain(dve, d_ch)
            link, mark = ch.link, ch.mark
            tt, ts, stt = dve.tensor_tensor, dve.tensor_scalar, dve.scalar_tensor_tensor
            nroot = [0]

            def root():
                nroot[0] += 1
                dve.wait_ge(s_asq, nroot[0])

            def tile_stats(t0, nt):
                for t in range(nt):
                    last = dve.bn_stats(st[:, t, :], xt[:, bass.ds(t0 + t, 1), :].rearrange("p a d -> p (a d)"))
                link(last)

            def ln_stats(nt):
                s = lambda k: stat[:, k, 0:nt]
                mark(tt(s(0), st[:, 0:nt, 1], st[:, 0:nt, 4], ALU.add))
                mark(tt(s(1), st[:, 0:nt, 1], st[:, 0:nt, 4], ALU.subtract))
                link(tt(s(2), st[:, 0:nt, 2], st[:, 0:nt, 5], ALU.add))
                mark(ts(s(0), s(0), 0.5, None, ALU.mult))
                link(tt(s(1), s(1), s(1), ALU.mult))
                link(stt(s(3), s(1), D / 4.0, s(2), ALU.mult, ALU.add))
                ts(s(3), s(3), 1.0 / D, EPS, ALU.mult, ALU.add).then_inc(s_need, 1)
                root()
                link(dve.reciprocal(s(5), s(4)))

            def setup():
                dve.wait_ge(s_tr, 1)
                dve.wait_ge(s_cst, 11)
                dve.wait_ge(s_adj, 16)
                ps0 = bank(0).rearrange("p (t m) -> p t m", t=2)
                dve.tensor_copy(adjT[:, :, :], ps0).then_inc(s_ev, 1)
                mark(dve.tensor_copy(adj_i, adj_n))
                link(dve.tensor_copy(adj_it, ps0))
                for t in range(2):
                    d = slice(t * P, (t + 1) * P)
                    mark(tt(adj_i[:, t, d], adj_i[:, t, d], ident[:, :], ALU.add))
                    mark(tt(adj_it[:, t, d], adj_it[:, t, d], ident[:, :], ALU.add))
                ch.wait()
                for t in range(2):
                    mark(tt(ahatT[:, 0, t * P:(t + 1) * P], adj_i[:, t, t * P:(t + 1) * P], ident[:, :], ALU.mult))
                mark(dve.reduce_sum(deg[:, 0, :], adj_i, axis=AX.X))
                mark(dve.reduce_sum(deg[:, 1, :], adj_it, axis=AX.X))
                ch.wait()
                link(dve.reduce_sum(deg[:, 2, :], ahatT[:, 0, :].rearrange("p (t m) -> p t m", t=2), axis=AX.X))
                link(tt(deg[:, 3, :], deg[:, 0, :], deg[:, 1, :], ALU.add))
                tt(deg[:, 3, :], deg[:, 3, :], deg[:, 2, :], ALU.subtract).then_inc(s_need, 1)
                dve.wait_ge(s_tr, 2)
                dve.tensor_copy(vec[:, :], ps[:, 1, 0:R_ROWS]).then_inc(s_ev, 1)
                dve.wait_ge(s_ev, 2)
                mark(ts(lng_s[:, :], vec[:, R_LNG:R_LNG + E], SC, None, ALU.mult))
                mark(tt(bsum[:, :], vec[:, R_BIH:R_BIH + 16], vec[:, R_BHH:R_BHH + 16], ALU.add))
                dve.wait_ge(s_tr, 3)
                mark(dve.tensor_copy(w1T, ps[:, 2, 0:GH]))
                dve.tensor_copy(w2T.rearrange("p t d -> p (t d)"), ps[:, 2, GH:2 * GH]).then_inc(s_ev, 1)
                root()
                link(dve.reciprocal(deg[:, 5, :], deg[:, 4, :]))
                mark(ts(adj_i[:, 0, :], adj_i[:, 0, :], deg[:, 5, 0:1], None, ALU.mult))
                ch.wait()
                ts(adj_i[:, 1, :], adj_i[:, 1, :], deg[:, 5, 1:2], None, ALU.mult).then_inc(s_ev, 1)
                dve.wait_ge(s_tr, 4)
                dve.tensor_copy(bmap[:, :], ps[:, 3, 0:T]).then_inc(s_ev, 1)
                dve.wait_ge(s_tr, 5)
                ch.wait()
                ts(ahatT[:, 0, :], ps[:, 4, 0:T], deg[:, 5, 0:1], None, ALU.mult)
                ts(ahatT[:, 1, :], ps[:, 4, T:2 * T], deg[:, 5, 1:2], None, ALU.mult).then_inc(s_ev, 1)

            def normalise_into(dst, j_of, nt):
                for t in range(nt):
                    last = ts(dst(t), j_of(t), stat[:, 0, t:t + 1], stat[:, 5, t:t + 1], ALU.subtract, ALU.mult)
                return last

            def graph0():
                for k in range(NT // GT):
                    if k in (0, NT // GT // 2):
                        dve.wait_ge(s_xin[k // (NT // GT // 2)], 16)
                    tile_stats(k * GT, GT)
                    ln_stats(GT)
                    mark(dve.tensor_copy(stat_all[:, 0, k * GT:(k + 1) * GT], stat[:, 0, 0:GT]))
                    link(dve.tensor_copy(stat_all[:, 1, k * GT:(k + 1) * GT], stat[:, 5, 0:GT]))

                def normalise(c, q):
                    if not (isinstance(c, int) and c < 2):
                        dve.wait_ge(s_agg, c - 1)
                    for t in range(4):
                        j = c * 4 + t
                        last = ts(xn[q][:, t, :], xt[:, bass.ds(j, 1), :].rearrange("p a d -> p (a d)"),
                                  stat_all[:, 0, bass.ds(j, 1)], stat_all[:, 1, bass.ds(j, 1)],
                                  ALU.subtract, ALU.mult)
                    last.then_inc(s_xn, 1)

                def stats1(c):
                    dve.wait_ge(s_h1c, 2 * c + 2)
                    for o in range(2):
                        last = dve.bn_stats(bnst[:, o, bass.ds(c, 1), :].rearrange("p a s -> p (a s)"),
                                            hid[:, o, bass.ds(c * 512, 512)])
                    mark(last)

                normalise(0, 0)
                normalise(1, 1)
                with dve.Fori(0, NCH // 2 - 1) as j:
                    ch.enter(j, 2)
                    for q in range(2):
                        stats1(2 * j + q)
                        normalise(2 * j + q + 2, q)
                    ch.leave(NCH // 2 - 1)
                stats1(NCH - 2)
                stats1(NCH - 1)
                ch.wait()
                for o in range(2):
                    mark(dve.bn_aggr(bnag[:, o, :], bnst[:, o, :, :].rearrange("p c s -> p (c s)")))
                ch.wait()
                ts(bnag[:, :, 1], bnag[:, :, 1], EPS, None, ALU.add).then_inc(s_need, 1)
                root()
                link(dve.reciprocal(bn1s[:, :], bnag[:, :, 1]))
                link(tt(bn1s[:, :], bn1s[:, :], vec[:, R_G1:R_G1 + 2], ALU.mult))
                link(tt(bn1t[:, :], bnag[:, :, 0], bn1s[:, :], ALU.mult))
                tt(bn1t[:, :], vec[:, R_BE1:R_BE1 + 2], bn1t[:, :], ALU.subtract).then_inc(s_bn1, 1)

                with dve.Fori(0, NCH // 2) as j:
                    ch.enter(j, 2)
                    for q in range(2):
                        c = 2 * j + q
                        dve.wait_ge(s_o2, c + 1)
                        ts(o2T[:, bass.ds(c * 512, 512)], bank(6 + q), vec[:, R_B2:R_B2 + 1], None, ALU.add)\
                            .then_inc(s_o2c, 1)
                        dve.wait_ge(s_o2c, c + 1)
                        last = dve.bn_stats(bnst[:, 0, bass.ds(c, 1), :].rearrange("p a s -> p (a s)"),
                                            o2T[:, bass.ds(c * 512, 512)])
                        mark(last)
                    ch.leave(NCH // 2)
                ch.wait()
                link(dve.bn_aggr(bnag[:, 0, :], bnst[:, 0, :, :].rearrange("p c s -> p (c s)")))
                ts(bnag[:, 0, 1:2], bnag[:, 0, 1:2], EPS, None, ALU.add).then_inc(s_need, 1)
                root()
                link(dve.reciprocal(bn2s[:, :], bnag[:, 0, 1:2]))
                link(tt(bn2s[:, :], bn2s[:, :], vec[:, R_G2:R_G2 + 1], ALU.mult))
                link(tt(bn2t[:, :], bnag[:, 0, 0:1], bn2s[:, :], ALU.mult))
                tt(bn2t[:, :], vec[:, R_BE2:R_BE2 + 1], bn2t[:, :], ALU.subtract).then_inc(s_bn2, 1)

            def weights(l, bufs):
                for k in range(2 * E):
                    n = 2 * E * l + k
                    e = k // 2
                    dve.wait_ge(s_wh, NLSTM + n + 1)
                    hi, lo = ((W1h, W1l) if k % 2 == 0 else (W2h, W2l))
                    scale = lng_s[:, e:e + 1] if l == 0 and k % 2 == 0 else SC
                    stt(lo[:, e, :, :].rearrange("p t c -> p (t c)"), bufs[n % 4], scale,
                        hi[:, e, :, :].rearrange("p t c -> p (t c)"), ALU.mult, ALU.subtract).then_inc(s_wl, 1)

            def expert_bias():
                dve.wait_ge(s_fold, E)
                mark(tt(eb1[:, 0, :], ps[:, 2, 0:E * HT], vec[:, R_FB1[0]:R_FB1[0] + E * HT], ALU.add))
                mark(dve.tensor_copy(eb1[:, 1, :], vec[:, R_FB1[1]:R_FB1[1] + E * HT]))

            def bc(ap, n):
                return ap.unsqueeze(2).to_broadcast([ap.shape[0], ap.shape[1], n])

            def mid(ap, m):
                return ap.unsqueeze(1).to_broadcast([ap.shape[0], m, ap.shape[1]])

            def prep(n, l, g):
                inst = G * l + g
                t0 = g * GT
                buf = lnx[n % 2]
                if l == 0:
                    for c in range(GT // 4):
                        dve.wait_ge(s_yt, g * (GT // 4) + c + 1)
                        v = xt[:, t0 + 4 * c:t0 + 4 * c + 4, :].rearrange("p t d -> p (t d)")
                        tt(v, v, bank(c % 2), ALU.add).then_inc(s_x2, 1)
                    dve.wait_ge(s_x2, (g + 1) * (GT // 4))
                tile_stats(t0, GT)
                ln_stats(GT)
                if n >= 2:
                    dve.wait_ge(s_sc[n % 2], 16 * GT * TOP_K * (n // 2))
                for t in range(GT):
                    last = ts(buf[:, t, :], xt[:, t0 + t, :], stat[:, 0, t:t + 1], stat[:, 5, t:t + 1],
                              ALU.subtract, ALU.mult)
                last.then_inc(s_lx, 1)
                if l == 0:
                    dve.wait_ge(s_lx, n + 1)
                    for t in range(GT):
                        last = dve.bn_stats(st[:, t, :], buf[:, t, :])
                    link(last)
                    ln_stats(GT)
                    dve.wait_ge(s_lt, (n + 1) * (GT // 4))
                    for t in range(GT):
                        last = ts(buf[:, t, :], buf[:, t, :], stat[:, 0, t:t + 1], stat[:, 5, t:t + 1],
                                  ALU.subtract, ALU.mult)
                    mark(last)
                L, a, b, oh1, oh2, sm = (route[k][:, :, :] for k in ("L", "a", "b", "oh1", "oh2", "sm"))
                r = lambda k: r16[:, k, :]
                dve.wait_ge(s_lg, (n + 1) * (GT // 4))
                link(tt(L, ps[:, 6, 0:GT * E].rearrange("p (t e) -> p t e", e=E), mid(brb[:, l, :], GT), ALU.add))
                for k, oh in ((0, oh1), (1, oh2)):
                    link(dve.reduce_max(r(k), L, axis=AX.X))
                    link(tt(a, L, bc(r(k), E), ALU.is_equal))
                    link(tt(a, a, mid(desc[:, :], GT), ALU.mult))
                    link(dve.reduce_max(r(3), a, axis=AX.X))
                    link(tt(oh, a, bc(r(3), E), ALU.is_equal))
                    if k == 0:
                        link(stt(L, oh, -3.0e38, L, ALU.mult, ALU.add))
                tt(M16[:, :, :], oh1, oh2, ALU.add).then_inc(s_m, 1)
                tt(r(2), r(1), r(0), ALU.subtract).then_inc(s_exn, 1)
                dve.wait_ge(s_exd, n + 1)
                link(ts(r(4), r(2), 1.0, None, ALU.add))
                link(dve.reciprocal(wts[:, inst, 0, :], r(4)))
                mark(tt(wts[:, inst, 1, :], r(2), wts[:, inst, 0, :], ALU.mult))
                dve.wait_ge(s_cnt, n + 1)
                within = ps[:, 7, 0:GT * E].rearrange("p (t e) -> p t e", e=E)
                total = ps[:, 7, 128:128 + GT * E].rearrange("p (t e) -> p e t", e=E)
                link(dve.tensor_copy(ejt[:, :, :], total))
                f = lambda z: z[:, :, :].rearrange("p e t -> p (e t)")
                link(dve.tensor_tensor_scan(f(ejc), ej_mask[:, :], f(ejt), 0.0, ALU.mult, ALU.add))
                mark(tt(ejt[:, :, :], ejc[:, :, :], ejt[:, :, :], ALU.subtract))
                link(tt(gtk[:, :, :], bc(ejc[:, :, GT - 1], KMAX), mid(k_blk[:, :], E), ALU.is_gt))
                link(dve.reduce_sum(r8[:, 0, :], gtk[:, :, :], axis=AX.X))
                link(dve.tensor_tensor_scan(r8[:, 1, :], one8[:, :], r8[:, 0, :], 0.0, ALU.mult, ALU.add))
                link(tt(r8[:, 2, :], r8[:, 1, :], r8[:, 0, :], ALU.subtract))
                mark(ts(r8[:, 2, :], r8[:, 2, :], float(BLK), None, ALU.mult))
                link(tt(geb[:, :, :], bc(iota_b[:, :], E - 1), mid(r8[0:1, 1, 0:E - 1], NBLK), ALU.is_ge))
                with nc.allow_low_precision(reason="counts are small integers"):
                    mark(dve.reduce_sum(ids[0:1, inst, 0:NBLK], geb[:, :, :], axis=AX.X))
                link(tt(sm, within, ejt[:, :, :].rearrange("p e t -> p t e"), ALU.add))
                link(tt(sm, sm, mid(r8[:, 2, :], GT), ALU.add))
                for k, oh in ((0, oh1), (1, oh2)):
                    link(tt(b, oh, sm, ALU.mult))
                    with nc.allow_low_precision(reason="slots are integers below 2^24"):
                        link(dve.reduce_sum(slot[:, inst, k, :], b, axis=AX.X))
                ts(r(5), r(4), 1.0, None, ALU.mult).then_inc(s_rt, 1)

            def experts(m, l, g):
                inst = G * l + g
                lo = m * NBLK

                def split(i, q):
                    dve.wait_ge(s_T, lo + i + 1)
                    if not (isinstance(i, int) and i < 2):
                        dve.wait_ge(s_U, 2 * (lo + i) - 2)
                    link(ts(xh[q], ps[:, 6 + q, 0:BLK], SC, None, ALU.mult))
                    stt(xlo[q], ps[:, 6 + q, 0:BLK], SC, xh[q], ALU.mult, ALU.subtract).then_inc(s_xs, 1)

                def hidden_low(i, q):
                    for hp in range(2):
                        dve.wait_ge(s_gl, 2 * (lo + i) + hp + 1)
                        if not (isinstance(i, int) and i < 2):
                            dve.wait_ge(s_D, lo + i - 1)
                        f = lambda z: z[q][:, 2 * hp:2 * hp + 2, :].rearrange("p t n -> p (t n)")
                        stt(f(hl), hf[:, hp * 2 * BLK:(hp + 1) * 2 * BLK], SC, f(hh), ALU.mult, ALU.subtract)\
                            .then_inc(s_hl, 1)

                def result(i, q, j=None):
                    e = dve.value_load(ids[0:1, inst, bass.ds(i, 1)], min_val=0, max_val=E - 1)
                    dve.wait_ge(s_D, lo + i + 1)
                    k = i // 2 if isinstance(i, int) else j
                    dve.wait_ge(s_yo[q], 16 * (m * ((NBLK + 1 - q) // 2) + k))
                    stt(yb_out[q], ps[:, 4 + q, 0:2 * D].rearrange("p (h d) -> p h d", h=2), UNSC,
                        eb2[l][:, bass.ds(e, 1), :].to_broadcast([P, 2, D]), ALU.mult, ALU.add).then_inc(s_y, 1)

                split(0, 0)
                split(1, 1)
                hidden_low(0, 0)
                split(2, 0)
                hidden_low(1, 1)
                result(0, 0)
                with dve.Fori(1, NBLK // 2) as j:
                    ch.enter(j - 1, 2)
                    for q in range(2):
                        i = 2 * j + q
                        split(i + 1, 1 - q)
                        hidden_low(i, q)
                        result(i - 1, 1 - q, j - 1 + q)
                    ch.leave(NBLK // 2 - 1)
                hidden_low(NBLK - 1, 0)
                result(NBLK - 2, 1)
                result(NBLK - 1, 0)

            def combine(m, l, g):
                inst = G * l + g
                dve.wait_ge(s_ga, 16 * GT * TOP_K * (m + 1))
                for k in range(TOP_K):
                    for t in range(GT):
                        v = xt[:, g * GT + t, :]
                        last = stt(v, ygat[:, t, k, :], wts[:, inst, k, t:t + 1], v, ALU.mult, ALU.add)
                    if k == 0:
                        link(last)
                last.then_inc(s_cb, 1)
                dve.wait_ge(s_cb, m + 1)

            def graph1(g):
                hv = hT.rearrange("p (b t) -> p b t", b=4)
                NS = len(LSTM_STEPS)
                with dve.Fori(2 * g, 2 * g + 2) as n:
                    ch.enter(n - 2 * g, C_LINKS)
                    tile_stats(n * QT, QT)
                    s = lambda k: stat[:, k, 0:QT]
                    mark(tt(s(0), st[:, 0:QT, 1], st[:, 0:QT, 4], ALU.add))
                    mark(tt(s(1), st[:, 0:QT, 1], st[:, 0:QT, 4], ALU.subtract))
                    link(tt(s(2), st[:, 0:QT, 2], st[:, 0:QT, 5], ALU.add))
                    mark(ts(s(0), s(0), 0.5, None, ALU.mult))
                    link(tt(s(1), s(1), s(1), ALU.mult))
                    link(stt(s(3), s(1), D / 4.0, s(2), ALU.mult, ALU.add))
                    ts(s(3), s(3), 1.0 / D, EPS, ALU.mult, ALU.add).then_inc(c_need, 1)
                    dve.wait_ge(c_rt, n + 1)
                    link(dve.reciprocal(s(5), s(4)))
                    for t in range(QT):
                        last = ts(xl[:, t, :], xt[:, bass.ds(n * QT + t, 1), :].rearrange("p a d -> p (a d)"),
                                  stat[:, 0, t:t + 1], stat[:, 5, t:t + 1], ALU.subtract, ALU.mult)
                    last.then_inc(c_xl, 1)
                    for h in range(2):
                        dve.wait_ge(c_w0, 2 * n + h + 1)
                        tt(h1T[:, h * 512:(h + 1) * 512].rearrange("p (b t) -> p b t", b=2),
                           bank(2 + h).rearrange("p (b t) -> p b t", b=2), mid(bmap[:, :], 2), ALU.add)\
                            .then_inc(c_hp, 1)
                    for h in range(2):
                        dve.wait_ge(c_u, 2 * n + h + 1)
                        tt(u2[:, 4 * h:4 * h + 4, :], bank(4 + h).rearrange("p (t d) -> p t d", t=4),
                           mid(bg1b[:, :], 4), ALU.add).then_inc(c_u2, 1)
                    seen = 0
                    for k, (p, sstep, half) in enumerate(LSTM_STEPS):
                        nw = T // p
                        nb = 2 if p == 1 else 4
                        w = nb * nw
                        last_step = sstep == p - 1
                        seen += 3 if sstep == 0 else 4
                        lo = n * GATES_PER_QUAD
                        cv = cell[:, 0:w]
                        if sstep == 0:
                            dve.wait_ge(c_ga, lo + seen - 1)
                            tt(cv, gate[:, 0, 0:w], gate[:, 2, 0:w], ALU.mult).then_inc(c_c, 1)
                        else:
                            dve.wait_ge(c_ga, lo + seen - 1)
                            mark(tt(tmp[:, 0:w], gate[:, 0, 0:w], gate[:, 2, 0:w], ALU.mult))
                            link(tt(cv, gate[:, 1, 0:w], cv, ALU.mult))
                            tt(cv, cv, tmp[:, 0:w], ALU.add).then_inc(c_c, 1)
                        dve.wait_ge(c_tc, n * NS + k + 1)
                        if last_step:
                            dst = hv[:, nb * half:nb * half + nb, sstep:sstep + (nw - 1) * p + 1:p]
                            v = lambda z: z.rearrange("p (b t) -> p b t", b=nb)
                        else:
                            dst = hcur[:, 0:w]
                            v = lambda z: z
                        tt(dst, v(gate[:, 3, 0:w]), v(tcell[:, 0:w]), ALU.mult).then_inc(c_h, 1)
                    for h in range(2):
                        dve.wait_ge(c_bk, 2 * n + h + 1)
                        v = xt[:, bass.ds(n * QT + 4 * h, 4), :].rearrange("p t d -> p (t d)")
                        tt(v, v, bank(h), ALU.add).then_inc(c_x3, 1)
                    dve.wait_ge(c_x3, 2 * n + 2)
                    ch.leave(2)

            m = 0
            for k, s in enumerate(plan):
                begin_step(dve, "dve", k)
                if s[0] == "A":
                    setup()
                    graph0()
                    weights(0, wstage)
                    expert_bias()
                elif s[0] == "P":
                    prep(prep_order.index(s[1:]), *s[1:])
                elif s[0] == "X":
                    experts(m, *s[1:])
                    m += 1
                elif s[0] == "D":
                    combine(combine_order.index(s[1:]), *s[1:])
                elif s[0] == "W":
                    weights(1, wstage1)
                elif s[0] == "C":
                    graph1(s[1])
                end_step(dve, "dve")


_INS = ["x", "adj", "L0_gnn_W1", "L0_gnn_b1", "L0_gnn_g1", "L0_gnn_be1", "L0_gnn_W2", "L0_gnn_b2", "L0_gnn_g2",
        "L0_gnn_be2", "L0_ffn_Wr", "L0_ffn_br", "L0_ffn_ln_g", "L0_ffn_ln_b", "L0_ffn_W1", "L0_ffn_b1", "L0_ffn_W2",
        "L0_ffn_b2", "L1_gnn_Wg0", "L1_gnn_bg0", "L1_gnn_Wg1", "L1_gnn_bg1", "L1_gnn_Wih", "L1_gnn_Whh",
        "L1_gnn_bih", "L1_gnn_bhh", "L1_ffn_Wg", "L1_ffn_bg", "L1_ffn_W1", "L1_ffn_b1", "L1_ffn_W2", "L1_ffn_b2"]


def kernel(**inputs):
    import numpy as _np
    import concourse.bacc as _bacc
    from concourse import mybir as _mybir
    from concourse.bass_utils import run_bass_kernel_spmd as _run

    nc = _bacc.Bacc("TRN2", target_bir_lowering=False, num_devices=1)
    arrays, args = {}, []
    for name in _INS:
        a = _np.ascontiguousarray(inputs[name])
        arrays[f"in_{name}"] = a
        args.append(nc.dram_tensor(f"in_{name}", a.shape, _mybir.dt.from_np(a.dtype), kind="ExternalInput").ap())
    args.append(nc.dram_tensor("out_0", (B, T, D), F32, kind="ExternalOutput").ap())
    graph_moe_kernel(nc, *args)
    r = _run(nc, [arrays], core_ids=[0])
    return r.results[0]["out_0"]
```

```python
from contextlib import ExitStack

import concourse.bass as bass
from concourse import mybir

F32 = mybir.dt.float32
F16 = mybir.dt.float16
BF16 = mybir.dt.bfloat16
I32 = mybir.dt.int32
ALU = mybir.AluOpType
ACT = mybir.ActivationFunctionType
AX = mybir.AxisListType

P = 128
B, T, D = 32, 256, 128
N = B * T
NT = N // P
E, H = 8, 512
HT = H // P
TOP_K = 2
EPS = 1e-5
OUTER_EPS = 1e-5
GH = 256
SKIP = 4

G = 4
GT = NT // G
BLK = 256
NBLK = (GT * P * TOP_K + E * (BLK - 1)) // BLK
SLOTS = NBLK * BLK
KMAX = GT * P // BLK
NCH = NT // 4
QT = 8
NQ = NT // QT
SC = 256.0
UNSC = 1.0 / (SC * SC)

R_FB1 = (0, 32)
R_LNG, R_LNB = 64, 72
R_B1, R_G1, R_BE1 = 80, 82, 84
R_B2, R_G2, R_BE2 = 86, 87, 88
R_BIH, R_BHH = 89, 105
R_ROWS = 121

GATES_PER_QUAD = 2 * 3 + (3 + 4) + (3 + 4 + 4) + (3 + 4 + 4 + 4)
LSTM_STEPS = [(1, 0, 0), (1, 0, 1)] + [(p, s, 0) for p in range(2, SKIP + 1) for s in range(p)]


NLSTM = 2 * SKIP - 1


class Chain:

    def __init__(self, eng, sem):
        self.eng, self.sem, self.base, self.k, self.i, self.per = eng, sem, 0, 0, None, 0

    def now(self):
        return self.base + self.k if self.i is None else self.base + self.i * self.per + self.k

    def mark(self, ins):
        self.k += 1
        ins.then_inc(self.sem, 1)

    def wait(self):
        self.eng.wait_ge(self.sem, self.now())

    def link(self, ins):
        self.mark(ins)
        self.wait()

    def enter(self, i, per):
        self.base, self.k, self.i, self.per = self.base + self.k, 0, i, per

    def leave(self, count):
        assert self.k == self.per, (self.k, self.per)
        self.base, self.k, self.i = self.base + self.per * count, 0, None


def default_plan():
    return [("A",), ("P", 0, 0), ("P", 0, 1), ("X", 0, 0), ("P", 0, 2), ("X", 0, 1), ("P", 0, 3), ("X", 0, 2),
            ("C", 0), ("P", 1, 0), ("X", 0, 3), ("C", 1), ("P", 1, 1), ("X", 1, 0), ("C", 2), ("P", 1, 2),
            ("X", 1, 1), ("C", 3), ("P", 1, 3), ("X", 1, 2), ("X", 1, 3)]


def graph_moe_kernel(nc, x, adj, L0_gnn_W1, L0_gnn_b1, L0_gnn_g1, L0_gnn_be1, L0_gnn_W2, L0_gnn_b2, L0_gnn_g2,
                     L0_gnn_be2, L0_ffn_Wr, L0_ffn_br, L0_ffn_ln_g, L0_ffn_ln_b, L0_ffn_W1, L0_ffn_b1, L0_ffn_W2,
                     L0_ffn_b2, L1_gnn_Wg0, L1_gnn_bg0, L1_gnn_Wg1, L1_gnn_bg1, L1_gnn_Wih, L1_gnn_Whh, L1_gnn_bih,
                     L1_gnn_bhh, L1_ffn_Wg, L1_ffn_bg, L1_ffn_W1, L1_ffn_b1, L1_ffn_W2, L1_ffn_b2, out, plan=None,
                     dump=False):
    plan = plan or default_plan()
    x_t = x.rearrange("b (h p) d -> p (b h) d", p=P)
    out_t = out.rearrange("b (h p) d -> p (b h) d", p=P)
    fW1 = (L0_ffn_W1, L1_ffn_W1)
    fW2 = (L0_ffn_W2, L1_ffn_W2)

    prep_order = [s[1:] for s in plan if s[0] == "P"]
    expert_order = [s[1:] for s in plan if s[0] == "X"]
    routed_with = {k + 1: s[1:] for k, s in enumerate(plan[:-1]) if s[0] == "P" and plan[k + 1][0] == "X"
                   and s[1:] != plan[k + 1][1:]}
    pool_order = []
    for s in plan:
        if s[0] == "P":
            pool_order.append(("scatter",) + s[1:])
        if s[0] == "X":
            pool_order.append(("gather",) + s[1:])

    with ExitStack() as ctx:
        def sb(name, shape, dt=F32):
            return ctx.enter_context(nc.sbuf_tensor(name, shape, dt))

        def sem(name):
            return ctx.enter_context(nc.semaphore(name))

        def dram(name, shape, dt=F32):
            return nc.dram_tensor(name, shape, dt, kind="Internal").ap()

        slots_in = [dram(f"slots_in{i}", (SLOTS, 2 * D), F16) for i in range(2)]
        slots_out = {inst: dram(f"slots_out{inst[0]}_{inst[1]}", (SLOTS, D)) for inst in expert_order}

        xt = sb("x_tok", [P, NT, D])
        hid = sb("hid", [P, 2, N])
        o2T = hid[:, 0, :]
        taken = [0, 0]

        def carve(half, n):
            a = taken[half]
            taken[half] += n
            assert taken[half] <= N, taken
            return hid[:, half, a:a + n]

        ident = sb("ident", [P, P])
        ident16 = sb("ident16", [P, P], F16)
        tri = sb("tri", [P, P], BF16)
        ones = sb("ones", [P, P], BF16)
        desc = sb("desc", [P, E])
        ej_mask = sb("ej_mask", [P, E * GT])
        k_blk = sb("k_blk", [P, KMAX])
        one8 = sb("one8", [P, E])
        iota_b = sb("iota_b", [1, NBLK])
        rows = sb("rows", [P, P])
        vec = sb("vec", [P, R_ROWS])
        zero = sb("zero", [P, 4 * D])
        bn1s = sb("bn1s", [P, 2])
        bn1t = sb("bn1t", [P, 2])
        bn2s = sb("bn2s", [P, 1])
        bn2t = sb("bn2t", [P, 1])
        lng_s = sb("lng_s", [P, E])
        eb1 = sb("eb1", [P, 2, E * HT])
        eb2 = [sb(f"eb2_{l}", [P, E, D]) for l in range(2)]
        Wr = sb("Wr", [P, 2, E])
        brb = sb("brb", [P, 2, E])
        Wg = sb("Wg", [P, 2, D])
        bg1b = sb("bg1b", [P, D])
        bg0b = sb("bg0b", [P, P])
        bmap = sb("bmap", [P, T])
        adjT = sb("adjT", [P, 2, T])
        bsum = sb("bsum", [P, SKIP * 4])
        wihT = sb("wihT", [P, SKIP, 4 * D])
        whhT = sb("whhT", [P, SKIP - 1, 4 * D])
        W1h = sb("W1h", [P, E, HT, P], F16)
        W1l = sb("W1l", [P, E, HT, P], F16)
        W2hl = sb("W2hl", [P, E, HT, 2, D], F16)

        st = sb("st", [P, GT, 6])
        stat = sb("stat", [P, 8, GT])
        stat_all = sb("stat_all", [P, 2, NT])
        bnst = sb("bnst", [P, 2, NCH, 6])
        bnag = sb("bnag", [P, 2, 2])
        route = {k: sb(f"route_{k}", [P, GT, E]) for k in ("L", "a", "b", "oh1", "oh2", "sm")}
        M16 = sb("M16", [P, GT, E], BF16)
        ejt = sb("ejt", [P, E, GT])
        ejc = sb("ejc", [P, E, GT])
        r16 = sb("r16", [P, 6, GT])
        r8 = sb("r8", [P, 4, E])
        gtk = sb("gtk", [P, E, KMAX])
        geb = sb("geb", [1, NBLK, E - 1])
        ids = sb("ids", [1, 2 * G, NBLK + 1], I32)
        slot = sb("slot", [P, 2 * G, TOP_K, GT], I32)
        wts = sb("wts", [P, 2 * G, TOP_K, GT])

        ARENA = 9216
        arena = sb("arena", [P, ARENA])
        used = [0]

        def area(n):
            a = used[0]
            used[0] += n
            assert used[0] <= ARENA, used[0]
            return arena[:, a:a + n]

        adj_n = area(2 * T).rearrange("p (t m) -> p t m", t=2)
        adj_i = area(2 * T).rearrange("p (t m) -> p t m", t=2)
        adj_it = area(2 * T).rearrange("p (t m) -> p t m", t=2)
        ahatT = area(2 * T).rearrange("p (t m) -> p t m", t=2)
        deg = area(16).rearrange("p (k t) -> p k t", t=2)
        gw1 = area(2 * D).rearrange("p (t d) -> p t d", t=2)
        gw2 = area(GH)
        w1T = area(GH)
        w2T = area(2 * D).rearrange("p (t d) -> p t d", t=2)
        xn = [area(4 * D).rearrange("p (t d) -> p t d", t=4) for _ in range(2)]
        agg = [area(512) for _ in range(2)]
        hb = [area(1024).rearrange("p (t n) -> p t n", t=2) for _ in range(2)]
        lstm_raw = area(4 * D).rearrange("p (t d) -> p t d", t=4)
        wstage = [area(H) for _ in range(2)]
        used[0] = 0
        ygat = area(GT * TOP_K * D).rearrange("p (t k d) -> p t k d", k=TOP_K, t=GT)
        wstage1 = [area(H) for _ in range(2)]
        hh, hl = ([area(HT * BLK // 2).bitcast(F16).rearrange("p (t n) -> p t n", t=HT) for _ in range(2)]
                  for _ in range(2))
        lnx = carve(1, GT * D).rearrange("p (t d) -> p t d", t=GT)
        lnh = [carve(1, GT * D).bitcast(F16).rearrange("p (t d) -> p t d", t=GT) if i else
               area(GT * D).bitcast(F16).rearrange("p (t d) -> p t d", t=GT) for i in range(2)]
        hf = carve(1, HT * BLK)
        xrow = [carve(1, 2 * D).bitcast(F16).rearrange("p (h d) -> p h d", h=2) for _ in range(2)]
        yb_out = [carve(1, 2 * D).rearrange("p (h d) -> p h d", h=2) for _ in range(2)]
        xs = [carve(1, BLK).bitcast(F16) for _ in range(2)]
        lxT = [hf[:, i * 512:(i + 1) * 512] for i in range(2)]
        ybn = [carve(1, 512) for _ in range(2)]
        hT, gate, cell, hcur, xl, zT, h1T, u2 = [], [], [], [], [], [], [], []
        for _ in range(2):
            hT.append(carve(0, QT * P))
            g4 = carve(0, 4 * 512)
            ch2 = carve(0, 2 * 512)
            gate.append(g4.rearrange("p (k n) -> p k n", k=4))
            cell.append(ch2[:, 0:512])
            hcur.append(ch2[:, 512:1024])
            xl.append(g4[:, 0:1024].rearrange("p (t d) -> p t d", t=QT))
            u2.append(xl[-1])
            zT.append(g4[:, 1024:2048])
            h1T.append(ch2)

        ps = ctx.enter_context(nc.psum_tensor("ps", [P, 8, 512], F32))
        xT = [ps[:, 6 + i, :].bitcast(F16) for i in range(2)]

        def bank(i):
            return ps[:, i, :]

        s_cst = sem("s_cst")
        s_par = sem("s_par")
        s_adj = sem("s_adj")
        s_rows = sem("s_rows")
        s_xin = [sem(f"s_xin{i}") for i in range(2)]
        s_lraw = sem("s_lraw")
        s_wst = [sem(f"s_wst{i}") for i in range(2)]
        s_zero = sem("s_zero")
        s_zfill = sem("s_zfill")
        s_tr = sem("s_tr")
        s_ev = sem("s_ev")
        s_asq = sem("s_asq")
        s_need = sem("s_need")
        s_wT = sem("s_wT")
        s_fold = sem("s_fold")
        s_wh = sem("s_wh")
        s_wl = sem("s_wl")
        s_xn = sem("s_xn")
        s_agg = sem("s_agg")
        s_agc = sem("s_agc")
        s_h1 = sem("s_h1")
        s_h1c = sem("s_h1c")
        s_bn1 = sem("s_bn1")
        s_relu = sem("s_relu")
        s_o2 = sem("s_o2")
        s_o2c = sem("s_o2c")
        s_bn2 = sem("s_bn2")
        s_yb = sem("s_yb")
        s_yt = sem("s_yt")
        s_x2 = sem("s_x2")
        s_lx = sem("s_lx")
        s_lt = sem("s_lt")
        s_ltc = sem("s_ltc")
        s_lg = sem("s_lg")
        s_xe = sem("s_xe")
        s_xhh = sem("s_xhh")
        s_exn = sem("s_exn")
        s_exd = sem("s_exd")
        s_m = sem("s_m")
        s_cnt = sem("s_cnt")
        s_w = sem("s_w")
        s_rt = sem("s_rt")
        s_sc = [sem(f"s_sc{i}") for i in range(2)]
        s_xr = [sem(f"s_xr{i}") for i in range(2)]
        s_T = sem("s_T")
        s_xs = sem("s_xs")
        s_U = sem("s_U")
        s_gl = sem("s_gl")
        s_hh = sem("s_hh")
        s_hl = sem("s_hl")
        s_D = sem("s_D")
        s_yh = sem("s_yh")
        s_y = sem("s_y")
        s_yo = [sem(f"s_yo{i}") for i in range(2)]
        s_ga = [sem(f"s_ga{c}") for c in range(GT // 4)]
        s_cw = sem("s_cw")
        s_cb1 = sem("s_cb1")
        s_cb = sem("s_cb")
        s_out = sem("s_out")
        c_need = sem("c_need")
        c_rt = sem("c_rt")
        c_xl = sem("c_xl")
        c_z = sem("c_z")
        c_zt = sem("c_zt")
        c_w0 = sem("c_w0")
        c_hp = sem("c_hp")
        c_h1 = sem("c_h1")
        c_u = sem("c_u")
        c_u2 = sem("c_u2")
        c_g = sem("c_g")
        c_hT = sem("c_hT")
        c_gp = [sem(f"c_gp{a}") for a in range(2)]
        c_ga = [sem(f"c_ga{a}") for a in range(2)]
        c_c = [sem(f"c_cell{a}") for a in range(2)]
        c_tc = [sem(f"c_tc{a}") for a in range(2)]
        c_h = [sem(f"c_hs{a}") for a in range(2)]
        c_bk = sem("c_bk")
        c_x3 = sem("c_x3")
        d_ch = sem("d_ch")
        a_ch = sem("a_ch")
        step = {k: sem(f"step_{k}") for k in ("pe", "act", "dve")}

        block = ctx.enter_context(nc.Block())

        def begin_step(eng, me, k):
            if k > 0:
                for other in step:
                    if other != me:
                        eng.wait_ge(step[other], k)

        def end_step(eng, me):
            eng.drain().then_inc(step[me], 1)

        def half_of_weights(e, k, low):
            if k == 0:
                return (W1l if low else W1h)[:, bass.ds(e, 1), :, :].rearrange("p a t c -> p (a t) c")
            return W2hl[:, bass.ds(e, 1), :, low, :].rearrange("p a t c -> p (a t) c")

        def expert_registers(eng, who):
            return [eng.alloc_register(f"{who}_expert{q}") for q in range(2)]

        def load_expert_id(eng, regs, q, inst, i):
            eng.load(regs[q], ids[0:1, inst, bass.ds(i, 1)])

        def expert_id(eng, regs, q):
            return eng.snap(regs[q], min_val=0, max_val=E - 1)

        PAR_DMAS = 14
        ZFILLS = 2 * -(-SLOTS // (4 * P))
        W_IN = ("C", 1)

        @block.sync
        def _(sp):
            par = [0]
            for q in range(2):
                sp.sem_inc(s_yo[q], 16)

            def load(dst, src):
                par[0] += 1
                sp.dma_start(dst, src).then_inc(s_par, 16)

            sp.dma_start(xt[:, 0:NT // 2, :], x_t[:, 0:NT // 2, :]).then_inc(s_xin[0], 16)
            sp.dma_start(adj_n, adj.rearrange("(t p) m -> p t m", p=P)).then_inc(s_adj, 16)
            nrows = 0
            for r, src in ((R_FB1[0], L0_ffn_b1.rearrange("e (t p) -> (e t) p", p=P)),
                           (R_FB1[1], L1_ffn_b1.rearrange("e (t p) -> (e t) p", p=P)),
                           (R_LNG, L0_ffn_ln_g), (R_LNB, L0_ffn_ln_b),
                           (R_B1, L0_gnn_b1.rearrange("(t p) -> t p", p=P)),
                           (R_G1, L0_gnn_g1.rearrange("(t p) -> t p", p=P)),
                           (R_BE1, L0_gnn_be1.rearrange("(t p) -> t p", p=P)),
                           (R_B2, L0_gnn_b2.rearrange("(t p) -> t p", p=P)),
                           (R_G2, L0_gnn_g2.rearrange("(t p) -> t p", p=P)),
                           (R_BE2, L0_gnn_be2.rearrange("(t p) -> t p", p=P)),
                           (R_BIH, L1_gnn_bih.rearrange("s (t p) -> (s t) p", p=P)),
                           (R_BHH, L1_gnn_bhh.rearrange("s (t p) -> (s t) p", p=P))):
                sp.dma_start(rows[r:r + src.shape[0], :], src).then_inc(s_rows, 16)
                nrows += 1
            assert nrows == 12
            load(gw1, L0_gnn_W1.rearrange("(t p) d -> p t d", p=P))
            load(gw2, L0_gnn_W2)
            load(Wr[:, 0, :], L0_ffn_Wr)
            load(Wr[:, 1, :], L1_ffn_Wg)
            load(brb[:, 0, :], L0_ffn_br.partition_broadcast(P))
            load(brb[:, 1, :], L1_ffn_bg.partition_broadcast(P))
            load(Wg[:, 0, :], L1_gnn_Wg0)
            load(Wg[:, 1, :], L1_gnn_Wg1)
            load(bg1b[:, :], L1_gnn_bg1.partition_broadcast(P))
            load(bg0b[:, :], L1_gnn_bg0.partition_broadcast(P))
            load(eb2[0][:, :, :], L0_ffn_b2.partition_broadcast(P))
            load(eb2[1][:, :, :], L1_ffn_b2.partition_broadcast(P))
            par[0] += 2
            assert par[0] == PAR_DMAS
            sp.dma_start(xt[:, NT // 2:, :], x_t[:, NT // 2:, :]).then_inc(s_xin[1], 16)
            for k in range(2 * SKIP - 1):
                src = L1_gnn_Wih[k] if k < SKIP else L1_gnn_Whh[k - SKIP + 1]
                if k > 0:
                    sp.wait_ge(s_wT, k)
                sp.dma_start(lstm_raw, src.rearrange("(t p) d -> p t d", p=P)).then_inc(s_lraw, 16)

            def load_expert(l, e, bufs):
                n = E * l + e
                for k in range(2):
                    if not (isinstance(e, int) and n == 0):
                        sp.wait_ge(s_wl, 2 * n - 1 + k)
                        if l == 0 and k == 0:
                            sp.wait_ge(s_fold, n)
                    src = fW1[l] if k == 0 else fW2[l].rearrange("e (t p) d -> e p t d", p=P)
                    if k == 0:
                        sp.dma_start(bufs[0], src[bass.ds(e, 1)].rearrange("a p h -> (a p) h")).then_inc(s_wst[0], 16)
                    else:
                        sp.dma_start(bufs[1].rearrange("p (t d) -> p t d", d=D),
                                     src[bass.ds(e, 1)].rearrange("a p t d -> (a p) t d")).then_inc(s_wst[1], 16)

            load_expert(0, 0, wstage)
            with sp.Fori(1, E) as e:
                load_expert(0, e, wstage)
            def experts(m, inst):
                n_s = prep_order.index(inst)
                sp.wait_ge(s_sc[n_s % 2], 16 * GT * TOP_K * (n_s // 2 + 1))
                src = slots_in[n_s % 2].rearrange("(b p h) d -> b p h d", p=P, h=2)
                dst = slots_out[inst].rearrange("(b p h) d -> b p h d", p=P, h=2)

                def load_block(i, par):
                    sp.dma_start(xrow[par], src[bass.ds(i, 1)].rearrange("a p h d -> (a p) h d"))\
                      .then_inc(s_xr[par], 16)

                def store_block(i, par):
                    sp.wait_ge(s_y, m * NBLK + i + 1)
                    sp.dma_start(dst[bass.ds(i, 1)].rearrange("a p h d -> (a p) h d"), yb_out[par])\
                      .then_inc(s_yo[par], 16)

                load_block(0, 0)
                load_block(1, 1)
                for i in range(2):
                    sp.wait_ge(s_T, m * NBLK + i + 1)
                    load_block(i + 2, i)
                with sp.Fori(1, NBLK // 2 - 1) as j:
                    for q in range(2):
                        sp.wait_ge(s_T, m * NBLK + 2 * j + q + 1)
                        load_block(2 * j + 2 + q, q)
                        store_block(2 * j + q - 2, q)
                sp.wait_ge(s_T, m * NBLK + NBLK - 2)
                load_block(NBLK - 1, 0)
                for i in range(NBLK - 5, NBLK):
                    store_block(i, i % 2)

            done1 = 0
            m = 0
            for s in plan:
                if s == W_IN:
                    with sp.Fori(0, E) as e:
                        load_expert(1, e, wstage1)
                if s[0] == "X":
                    experts(m, s[1:])
                    m += 1
            for mm, (l, g) in enumerate(expert_order):
                for c in range(GT // 4 if l == 1 else 0):
                    sp.wait_ge(s_cb, mm * (GT // 4) + c + 1)
                    t = g * GT + 4 * c
                    sp.dma_start(out_t[:, t:t + 4, :], xt[:, t:t + 4, :]).then_inc(s_out, 16)
                    done1 += 1
            if dump:
                for k in step:
                    sp.wait_ge(step[k], len(plan))
                sp.dma_start(out_t, xt[:, :, :]).then_inc(s_out, 16)
                done1 += 1
            sp.wait_ge(s_out, 16 * done1)
            for q in range(2):
                sp.wait_ge(s_yo[q], 16 * m * ((NBLK + 1 - q) // 2) + 16)

        @block.gpsimd
        def _(pool):
            pool.memset(ident[:, :], 0.0).then_inc(s_cst, 1)
            pool.memset(tri[:, :], 1.0).then_inc(s_cst, 1)
            pool.memset(ones[:, :], 1.0).then_inc(s_cst, 1)
            pool.memset(one8[:, :], 1.0).then_inc(s_cst, 1)
            pool.memset(ej_mask[:, :], 1.0).then_inc(s_cst, 1)
            pool.iota(desc[:, :], [[-1, E]], base=E, channel_multiplier=0,
                      allow_small_or_imprecise_dtypes=True).then_inc(s_cst, 1)
            pool.iota(k_blk[:, :], [[BLK, KMAX]], base=0, channel_multiplier=0,
                      allow_small_or_imprecise_dtypes=True).then_inc(s_cst, 1)
            pool.iota(iota_b[:, :], [[1, NBLK]], base=0, channel_multiplier=0,
                      allow_small_or_imprecise_dtypes=True).then_inc(s_cst, 1)
            pool.memset(ident16[:, :], 0.0).then_inc(s_cst, 1)
            pool.memset(zero[:, :], 0.0).then_inc(s_zero, 1)
            pool.wait_ge(s_cst, 9)
            pool.affine_select(out=ident16[:, :], in_=ident16[:, :], compare_op=ALU.not_equal, fill=1.0, base=0,
                               pattern=[[-1, P]], channel_multiplier=1).then_inc(s_cst, 1)
            pool.affine_select(out=ident[:, :], in_=ident[:, :], compare_op=ALU.not_equal, fill=1.0, base=0,
                               pattern=[[-1, P]], channel_multiplier=1).then_inc(s_cst, 1)
            pool.affine_select(out=tri[:, :], in_=tri[:, :], compare_op=ALU.is_gt, fill=0.0, base=0,
                               pattern=[[1, P]], channel_multiplier=-1).then_inc(s_cst, 1)
            pool.affine_select(out=ej_mask[:, :].rearrange("p (e t) -> p e t", e=E),
                               in_=ej_mask[:, :].rearrange("p (e t) -> p e t", e=E),
                               compare_op=ALU.is_gt, fill=0.0, base=0,
                               pattern=[[0, E], [1, GT]], channel_multiplier=0).then_inc(s_cst, 1)
            pool.wait_ge(s_zero, 1)
            for s in slots_in:
                for r in range(0, SLOTS, 4 * P):
                    n = min(4 * P, SLOTS - r)
                    pool.dma_start(s[r:r + n, :].rearrange("(p a) d -> p (a d)", a=4),
                                   zero[0:n // 4, :].bitcast(F16)).then_inc(s_zfill, 16)
            pool.wait_ge(s_zfill, 16 * ZFILLS)
            for what, l, g in pool_order:
                if what == "scatter":
                    n = prep_order.index((l, g))
                    pool.wait_ge(s_rt, n + 1)
                    if n >= 2:
                        mm = expert_order.index(prep_order[n - 2])
                        pool.wait_ge(s_T, (mm + 1) * NBLK)
                    for t in range(GT):
                        for k in range(TOP_K):
                            pool.indirect_dma_start(
                                slots_in[n % 2], bass.IndirectOffsetOnAxis(ap=slot[:, G * l + g, k, t:t + 1], axis=0),
                                lnh[n % 2][:, t, :], None).then_inc(s_sc[n % 2], 16)
                else:
                    m = expert_order.index((l, g))
                    pool.wait_ge(s_w, prep_order.index((l, g)) + 1)
                    if m > 0:
                        pool.wait_ge(s_cb, m * (GT // 4))
                    pool.wait_ge(s_yo[0], 16 * (m + 1) * ((NBLK + 1) // 2) + 16)
                    pool.wait_ge(s_yo[1], 16 * (m + 1) * (NBLK // 2) + 16)
                    for t in range(GT):
                        for k in range(TOP_K):
                            pool.indirect_dma_start(
                                ygat[:, t, k, :], None, slots_out[(l, g)],
                                bass.IndirectOffsetOnAxis(ap=slot[:, G * l + g, k, t:t + 1], axis=0))\
                                .then_inc(s_ga[t // 4], 16)
                    for c in range(GT // 4):
                        pool.wait_ge(s_ga[c], 16 * 4 * TOP_K * (m + 1))
                        c4 = slice(4 * c, 4 * c + 4)
                        v = xt[:, g * GT + 4 * c:g * GT + 4 * c + 4, :]
                        for k in range(TOP_K):
                            w = wts[:, G * l + g, k, c4].unsqueeze(2).to_broadcast([P, 4, D])
                            pool.tensor_tensor(ygat[:, c4, k, :], ygat[:, c4, k, :], w, ALU.mult)\
                                .then_inc(s_cw, 1)
                        for k in range(TOP_K):
                            pool.wait_ge(*((s_cb1, m * (GT // 4) + c + 1) if k else
                                           (s_cw, TOP_K * (m * (GT // 4) + c + 1))))
                            pool.tensor_tensor(v, v, ygat[:, c4, k, :], ALU.add).then_inc(s_cb if k else s_cb1, 1)

        @block.tensor
        def _(pe):
            regs = expert_registers(pe, "pe")
            mm = pe.matmul

            def setup():
                pe.wait_ge(s_cst, 13)
                pe.wait_ge(s_adj, 16)
                for mt in range(2):
                    for nt in range(2):
                        last = pe.transpose(ps[:, 0, mt * T + nt * P:mt * T + (nt + 1) * P],
                                            adj_n[:, nt, mt * P:(mt + 1) * P], ident[:, :])
                last.then_inc(s_tr, 1)
                pe.wait_ge(s_rows, 16 * 12)
                pe.transpose(ps[:, 1, 0:R_ROWS], rows[0:R_ROWS, :], ident[0:R_ROWS, 0:R_ROWS]).then_inc(s_tr, 1)
                pe.wait_ge(s_par, 16 * (PAR_DMAS - 2))
                for t in range(2):
                    pe.transpose(ps[:, 2, t * P:(t + 1) * P], gw1[:, t, :], ident[:, :])
                for t in range(2):
                    last = pe.transpose(ps[:, 2, GH + t * P:GH + (t + 1) * P], gw2[:, t * P:(t + 1) * P], ident[:, :])
                last.then_inc(s_tr, 1)
                pe.wait_ge(s_ev, 1)
                for k in range(2):
                    last = mm(ps[:, 3, 0:T], bg0b[:, :], adjT[:, k, :], start=(k == 0), stop=(k == 1))
                last.then_inc(s_tr, 1)
                pe.wait_ge(s_ev, 4)
                for mt in range(2):
                    for nt in range(2):
                        last = pe.transpose(ps[:, 4, mt * T + nt * P:mt * T + (nt + 1) * P],
                                            adj_i[:, nt, mt * P:(mt + 1) * P], ident[:, :])
                last.then_inc(s_tr, 1)
                pe.wait_ge(s_ev, 6)

            def graph0():
                def aggregate(c, q, first=False):
                    pe.wait_ge(s_xn, c + 1)
                    if not first:
                        pe.wait_ge(s_agc, c - 1)
                    for b in range(2):
                        for k in range(2):
                            last = mm(ps[:, q, b * T:(b + 1) * T], xn[q][:, 2 * b + k, :], ahatT[:, k, :],
                                      start=(k == 0), stop=(k == 1))
                    last.then_inc(s_agg, 1)

                def hidden(c, q, first=False):
                    pe.wait_ge(s_agc, c + 1)
                    if not first:
                        pe.wait_ge(s_h1c, 2 * c - 2)
                    for o in range(2):
                        mm(ps[:, 2 + 2 * q + o, :], w1T[:, o * P:(o + 1) * P], agg[q], start=True, stop=True)\
                            .then_inc(s_h1, 1)

                aggregate(0, 0, True)
                aggregate(1, 1, True)
                hidden(0, 0, True)
                aggregate(2, 0)
                hidden(1, 1, True)
                fold_bias(0)
                with pe.Fori(1, NCH // 2 - 1) as j:
                    for q in range(2):
                        c = 2 * j + q
                        aggregate(c + 1, 1 - q)
                        hidden(c, q)
                    fold_bias(j)
                aggregate(NCH - 1, 1)
                hidden(NCH - 2, 0)
                hidden(NCH - 1, 1)
                fold_bias(E - 1)

                def output(c, q, first=False):
                    pe.wait_ge(s_relu, 2 * c + 2)
                    if not first:
                        pe.wait_ge(s_o2c, c - 1)
                    for k in range(2):
                        last = mm(ps[:, 6 + q, :], w2T[:, k, :], hb[q][:, k, :], start=(k == 0), stop=(k == 1))
                    last.then_inc(s_o2, 1)

                output(0, 0, True)
                output(1, 1, True)
                with pe.Fori(1, NCH // 2) as j:
                    for q in range(2):
                        output(2 * j + q, q)

            def lstm_weights():
                for k in range(2 * SKIP - 1):
                    pe.wait_ge(s_lraw, 16 * (k + 1))
                    if k >= 2:
                        pe.wait_ge(s_wh, k - 1)
                    for t in range(4):
                        last = pe.transpose(ps[:, k % 2, t * P:(t + 1) * P], lstm_raw[:, t, :], ident[:, :])
                    last.then_inc(s_wT, 1)
                pe.wait_ge(s_wh, NLSTM)

            def fold_bias(e):
                pe.wait_ge(s_wst[0], 16 * (e + 1))
                for t in range(HT):
                    last = mm(ps[:, 6, bass.ds(e * HT + t, 1)], wstage[0][:, t * P:(t + 1) * P],
                              vec[:, bass.ds(e + R_LNB, 1)], start=True, stop=True)
                last.then_inc(s_fold, 1)

            def prep(n, l, g):
                if l == 0:
                    for c in range(GT // 4):
                        pe.wait_ge(s_yb, g * (GT // 4) + c + 1)
                        if c >= 2:
                            pe.wait_ge(s_x2, g * (GT // 4) + c - 1)
                        for t in range(4):
                            last = pe.transpose(ps[:, c % 2, t * P:(t + 1) * P], ybn[c % 2][:, t * P:(t + 1) * P],
                                                ident[:, :])
                        last.then_inc(s_yt, 1)
                for c in range(GT // 4):
                    pe.wait_ge(s_lx, n * (GT // 4) + c + 1)
                    for t in range(4):
                        last = pe.transpose(ps[:, 2 + c, t * P:(t + 1) * P], lnx[:, 4 * c + t, :], ident[:, :])
                    last.then_inc(s_lt, 1)
                for c in range(GT // 4):
                    pe.wait_ge(s_ltc, n * (GT // 4) + c + 1)
                    for t in range(4):
                        j = 4 * c + t
                        last = mm(ps[:, 6, j * E:(j + 1) * E], lxT[c % 2][:, t * P:(t + 1) * P], Wr[:, l, :],
                                  start=True, stop=True)
                    last.then_inc(s_lg, 1)

            def count_selected(n):
                pe.wait_ge(s_m, n + 1)
                m2 = M16[:, :, :].rearrange("p t e -> p (t e)")
                mm(ps[:, 5, 0:GT * E], tri[:, :], m2, start=True, stop=True)
                mm(ps[:, 5, 128:128 + GT * E], ones[:, :], m2, start=True, stop=True).then_inc(s_cnt, 1)

            def experts(m, l, g, routed):
                inst = G * l + g
                lo = m * NBLK

                def transposes(i, q):
                    k = m * ((NBLK + 1 - q) // 2) + (i // 2 if isinstance(i, int) else i[0])
                    pe.wait_ge(s_xr[q], 16 * (k + 1))
                    for half in range(2):
                        for h in range(2):
                            last = pe.transpose(xT[q][:, half * BLK + h * P:half * BLK + (h + 1) * P],
                                                xrow[q][:, h, half * D:(half + 1) * D], ident16[:, :])
                    last.then_inc(s_T, 1)

                def up(i, q):
                    load_expert_id(pe, regs, q, inst, i)
                    e = expert_id(pe, regs, q)
                    pe.wait_ge(s_xs, lo + i + 1)
                    for hp in range(2):
                        for ht in (2 * hp, 2 * hp + 1):
                            o = ps[:, 2 * q + hp, (ht % 2) * BLK:(ht % 2 + 1) * BLK]
                            wh = W1h[:, bass.ds(e, 1), ht, :].rearrange("p a c -> p (a c)")
                            wl = W1l[:, bass.ds(e, 1), ht, :].rearrange("p a c -> p (a c)")
                            mm(o, wh, xs[q][:, 0:BLK], start=True, stop=False)
                            mm(o, wh, xs[q][:, BLK:2 * BLK], start=False, stop=False)
                            last = mm(o, wl, xs[q][:, 0:BLK], start=False, stop=True)
                        last.then_inc(s_U, 1)

                def down(i, q):
                    e = expert_id(pe, regs, q)
                    pe.wait_ge(s_hl, 2 * (lo + i) + 2)
                    for h in range(2):
                        o = ps[:, 4 + q, h * 2 * D:(h + 1) * 2 * D]
                        for kt in range(HT):
                            w = W2hl[:, bass.ds(e, 1), kt, :, :].rearrange("p a s c -> p (a s c)")
                            wh = W2hl[:, bass.ds(e, 1), kt, 0, :].rearrange("p a c -> p (a c)")
                            mm(o, hh[q][:, kt, h * P:(h + 1) * P], w, start=(kt == 0), stop=False)
                            last = mm(o[:, 0:D], hl[q][:, kt, h * P:(h + 1) * P], wh, start=False,
                                      stop=(kt == HT - 1))
                    last.then_inc(s_D, 1)

                transposes(0, 0)
                transposes(1, 1)
                up(0, 0)
                transposes(2, 0)
                up(1, 1)
                if routed is not None:
                    count_selected(routed)
                down(0, 0)
                transposes(3, 1)
                for i in (2, 3):
                    up(i, i % 2)
                    transposes(i + 2, i % 2)
                    down(i - 1, 1 - i % 2)
                with pe.Fori(2, NBLK // 2 - 1) as j:
                    for q in range(2):
                        i = 2 * j + q
                        up(i, q)
                        transposes((j + 1, i + 2), q)
                        down(i - 1, 1 - q)
                up(NBLK - 3, 0)
                transposes(NBLK - 1, 0)
                down(NBLK - 4, 1)
                up(NBLK - 2, 1)
                down(NBLK - 3, 0)
                up(NBLK - 1, 0)
                down(NBLK - 2, 1)
                down(NBLK - 1, 0)

            def graph1(g):
                n = 2 * g
                for a in range(2):
                    pe.wait_ge(c_xl, n + a + 1)
                    for b in range(4):
                        for k in range(2):
                            last = mm(ps[:, 4 * a + b // 2, (b % 2) * T:(b % 2 + 1) * T], xl[a][:, 2 * b + k, :],
                                      adjT[:, k, :], start=(k == 0), stop=(k == 1))
                        if b % 2:
                            last.then_inc(c_z, 1)
                for a in range(2):
                    for h in range(2):
                        pe.wait_ge(c_zt, 2 * (n + a) + h + 1)
                        mm(ps[:, 4 * a + 2 + h, :], Wg[:, 0, :], zT[a][:, h * 512:(h + 1) * 512],
                           start=True, stop=True).then_inc(c_w0, 1)
                for a in range(2):
                    for h in range(2):
                        pe.wait_ge(c_h1, 2 * (n + a) + h + 1)
                        for t in range(4):
                            last = mm(ps[:, 4 * a + h, t * P:(t + 1) * P],
                                      h1T[a][:, (4 * h + t) * P:(4 * h + t + 1) * P], Wg[:, 1, :],
                                      start=True, stop=True)
                        last.then_inc(c_u, 1)
                for a in range(2):
                    for b in range(4):
                        if b % 2 == 0:
                            pe.wait_ge(c_u2, 2 * (n + a) + b // 2 + 1)
                        for k in range(2):
                            last = mm(ps[:, 4 * a + 2 + b // 2, (b % 2) * T:(b % 2 + 1) * T], u2[a][:, 2 * b + k, :],
                                      adjT[:, k, :], start=(k == 0), stop=(k == 1))
                        if b % 2:
                            last.then_inc(c_g, 1)
                NS = len(LSTM_STEPS)
                lo = g * GATES_PER_QUAD
                seen = [0, 0]
                for k, (p, s, half) in enumerate(LSTM_STEPS):
                    gates = (0, 2, 3) if s == 0 else (0, 2, 1, 3)
                    nw = T // p
                    nb = 2 if p == 1 else 4
                    w = nb * nw
                    for a in range(2):
                        hv = hT[a].rearrange("p (b t) -> p b t", b=4)
                        xin = hv[:, nb * half:nb * half + nb, s:s + (nw - 1) * p + 1:p]
                        if k == 0:
                            pe.wait_ge(c_hT, 2 * (n + a) + 2)
                        elif s == 0:
                            pe.wait_ge(c_h[a], g * NS + k)
                        if k > 0:
                            pe.wait_ge(c_ga[a], lo + seen[a])
                        for gt in gates:
                            mm_ = mm(ps[:, 4 * a + gt, 0:w], wihT[:, p - 1, gt * P:(gt + 1) * P], xin,
                                     start=True, stop=(s == 0))
                            if s > 0:
                                if gt == gates[0]:
                                    pe.wait_ge(c_h[a], g * NS + k)
                                mm_ = mm(ps[:, 4 * a + gt, 0:w], whhT[:, p - 2, gt * P:(gt + 1) * P],
                                         hcur[a][:, 0:w], start=False, stop=True)
                            mm_.then_inc(c_gp[a], 1)
                            seen[a] += 1
                for a in range(2):
                    pe.wait_ge(c_h[a], (g + 1) * NS)
                    pe.wait_ge(c_ga[a], lo + seen[a])
                    for h in range(2):
                        for t in range(4):
                            last = pe.transpose(ps[:, 4 * a + h, t * P:(t + 1) * P],
                                                hT[a][:, (4 * h + t) * P:(4 * h + t + 1) * P], ident[:, :])
                        last.then_inc(c_bk, 1)

            m = 0
            for k, s in enumerate(plan):
                begin_step(pe, "pe", k)
                if s[0] == "A":
                    setup()
                    lstm_weights()
                    graph0()
                elif s[0] == "P":
                    n = prep_order.index(s[1:])
                    prep(n, *s[1:])
                    if k + 1 not in routed_with:
                        count_selected(n)
                elif s[0] == "X":
                    experts(m, *s[1:], prep_order.index(routed_with[k]) if k in routed_with else None)
                    m += 1
                elif s[0] == "C":
                    graph1(s[1])
                end_step(pe, "pe")

        @block.scalar
        def _(act):
            regs = expert_registers(act, "act")
            ch = Chain(act, a_ch)
            roots = [0]

            def root(dst, src, scale, bias):
                roots[0] += 1
                act.wait_ge(s_need, roots[0])
                act.activation(dst, src, ACT.Sqrt, bias=bias, scale=scale).then_inc(s_asq, 1)

            def ln_root(ntiles):
                root(stat[:, 4, 0:ntiles], stat[:, 3, 0:ntiles], 1.0, 0.0)

            def high_half(l, e, k, bufs):
                act.wait_ge(s_wst[k], 16 * (E * l + e + 1))
                dst = half_of_weights(e, k, 0)
                scale = lng_s[:, bass.ds(e, 1)] if l == 0 and k == 0 else SC
                act.activation(dst, bufs[k].rearrange("p (t c) -> p t c", t=HT), ACT.Copy, scale=scale)\
                   .then_inc(s_wh, 1)

            def setup_and_graph0():
                root(deg[:, 4, :], deg[:, 3, :], 1.0, 0.0)
                for k in range(NT // GT):
                    ln_root(GT)
                for k in range(2 * SKIP - 1):
                    act.wait_ge(s_wT, k + 1)
                    dst = wihT[:, k, :] if k < SKIP else whhT[:, k - SKIP, :]
                    act.activation(dst, bank(k % 2), ACT.Copy).then_inc(s_wh, 1)

                def copy_aggregate(c, q, first=False):
                    act.wait_ge(s_agg, c + 1)
                    if not first:
                        act.wait_ge(s_h1, 2 * c - 2)
                    act.activation(agg[q], bank(q), ACT.Copy).then_inc(s_agc, 1)

                def copy_hidden(c, q):
                    for o in range(2):
                        act.wait_ge(s_h1, 2 * c + o + 1)
                        act.activation(hid[:, o, bass.ds(c * 512, 512)], bank(2 + 2 * q + o), ACT.Identity,
                                       bias=vec[:, R_B1 + o:R_B1 + o + 1]).then_inc(s_h1c, 1)

                copy_aggregate(0, 0, True)
                copy_aggregate(1, 1, True)
                copy_hidden(0, 0)
                copy_aggregate(2, 0)
                copy_hidden(1, 1)
                for k in range(2):
                    high_half(0, 0, k, wstage)
                with act.Fori(1, NCH // 2 - 1) as j:
                    for q in range(2):
                        copy_aggregate(2 * j + q + 1, 1 - q)
                        copy_hidden(2 * j + q, q)
                        high_half(0, j, q, wstage)
                copy_aggregate(NCH - 1, 1)
                copy_hidden(NCH - 2, 0)
                copy_hidden(NCH - 1, 1)
                for k in range(2):
                    high_half(0, E - 1, k, wstage)
                root(bnag[:, :, 1], bnag[:, :, 1], 1.0, 0.0)
                act.wait_ge(s_bn1, 1)

                def normalise_hidden(c, q, first=False):
                    if not first:
                        act.wait_ge(s_o2, c - 1)
                    for o in range(2):
                        act.activation(hb[q][:, o, :], hid[:, o, bass.ds(c * 512, 512)], ACT.Relu,
                                       bias=bn1t[:, o:o + 1], scale=bn1s[:, o:o + 1]).then_inc(s_relu, 1)

                normalise_hidden(0, 0, True)
                normalise_hidden(1, 1, True)
                with act.Fori(1, NCH // 2) as j:
                    for q in range(2):
                        normalise_hidden(2 * j + q, q)
                root(bnag[:, 0, 1:2], bnag[:, 0, 1:2], 1.0, 0.0)

            def prep(n, l, g):
                if l == 0:
                    for c in range(GT // 4):
                        if c >= 2:
                            act.wait_ge(s_yt, g * (GT // 4) + c - 1)
                        act.activation(ybn[c % 2], o2T[:, (g * (GT // 4) + c) * 512:(g * (GT // 4) + c + 1) * 512],
                                       ACT.Identity, bias=bn2t[:, 0:1], scale=bn2s[:, 0:1]).then_inc(s_yb, 1)
                root(stat[:, 4, :], stat[:, 6, :], 1.0, 0.0)
                if l == 0:
                    root(stat[:, 7, :], stat[:, 7, :], 1.0, 0.0)
                act.wait_ge(*((s_xe, g + 1) if l == 0 else (s_lx, (n + 1) * (GT // 4))))
                if n >= 2:
                    act.wait_ge(s_sc[n % 2], 16 * GT * TOP_K * (n // 2))
                for c in range(GT // 4):
                    act.wait_ge(s_lt, n * (GT // 4) + c + 1)
                    if c >= 2:
                        act.wait_ge(s_lg, n * (GT // 4) + c - 1)
                    act.activation(lxT[c % 2], bank(2 + c), ACT.Copy).then_inc(s_ltc, 1)
                    if l == 0:
                        for t in range(4 * c, 4 * c + 4):
                            last = act.activation(lnh[n % 2][:, t, 0:D], lnx[:, t, :], ACT.Copy,
                                                  scale=stat[:, 7, t:t + 1])
                    else:
                        last = act.activation(lnh[n % 2][:, 4 * c:4 * c + 4, 0:D], lnx[:, 4 * c:4 * c + 4, :],
                                              ACT.Copy, scale=SC)
                    last.then_inc(s_xhh, 1)

            def weight_exponentials(n):
                act.wait_ge(s_exn, n + 1)
                act.activation(r16[:, 2, :], r16[:, 2, :], ACT.Exp).then_inc(s_exd, 1)

            def experts(m, l, g, routed):
                inst = G * l + g
                lo = m * NBLK

                def gelu(i, q):
                    load_expert_id(act, regs, q, inst, i)
                    e = expert_id(act, regs, q)
                    for hp in range(2):
                        act.wait_ge(s_U, 2 * (lo + i) + hp + 1)
                        if not (isinstance(i, int) and i < 1):
                            act.wait_ge(s_hl, 2 * (lo + i - 1) + hp + 1)
                        for ht in (2 * hp, 2 * hp + 1):
                            last = act.activation(hf[:, ht * BLK:(ht + 1) * BLK],
                                                  ps[:, 2 * q + hp, (ht % 2) * BLK:(ht % 2 + 1) * BLK], ACT.Gelu,
                                                  bias=eb1[:, l, bass.ds(e * HT + ht, 1)], scale=UNSC)
                        if hp == 0:
                            last.then_inc(s_gl, 1)
                            continue
                        ch.link(last)
                        act.activation(hh[q][:, 2 * hp:2 * hp + 2, :].rearrange("p t n -> p (t n)"),
                                       hf[:, hp * 2 * BLK:(hp + 1) * 2 * BLK], ACT.Copy, scale=SC).then_inc(s_gl, 1)

                gelu(0, 0)
                gelu(1, 1)
                with act.Fori(1, NBLK // 2) as j:
                    ch.enter(j - 1, 2)
                    gelu(2 * j, 0)
                    gelu(2 * j + 1, 1)
                    ch.leave(NBLK // 2 - 1)
                gelu(NBLK - 1, 0)
                if routed is not None:
                    weight_exponentials(routed)

            def graph1(g):
                n = 2 * g
                for a in range(2):
                    act.wait_ge(c_need, n + a + 1)
                    act.activation(stat[:, 4, a * QT:(a + 1) * QT], stat[:, 3, a * QT:(a + 1) * QT], ACT.Sqrt)\
                        .then_inc(c_rt, 1)
                for a in range(2):
                    for h in range(2):
                        act.wait_ge(c_z, 2 * (n + a) + h + 1)
                        act.activation(zT[a][:, h * 512:(h + 1) * 512], bank(4 * a + h), ACT.Copy).then_inc(c_zt, 1)
                for a in range(2):
                    for h in range(2):
                        act.wait_ge(c_hp, 2 * (n + a) + h + 1)
                        v = h1T[a][:, h * 512:(h + 1) * 512]
                        act.activation(v, v, ACT.Relu).then_inc(c_h1, 1)
                for a in range(2):
                    for h in range(2):
                        act.wait_ge(c_g, 2 * (n + a) + h + 1)
                        act.activation(hT[a][:, h * 512:(h + 1) * 512], bank(4 * a + 2 + h), ACT.Relu)\
                            .then_inc(c_hT, 1)
                NS = len(LSTM_STEPS)
                lo = g * GATES_PER_QUAD
                seen = [0, 0]
                for k, (p, s, half) in enumerate(LSTM_STEPS):
                    gates = (0, 2, 3) if s == 0 else (0, 2, 1, 3)
                    w = (T // p) * (2 if p == 1 else 4)
                    for a in range(2):
                        if k > 0:
                            act.wait_ge(c_h[a], g * NS + k)
                        for gt in gates:
                            if gt == 3:
                                act.wait_ge(c_c[a], g * NS + k + 1)
                                act.activation(gate[a][:, 2, 0:w], cell[a][:, 0:w], ACT.Tanh).then_inc(c_tc[a], 1)
                            seen[a] += 1
                            act.wait_ge(c_gp[a], lo + seen[a])
                            act.activation(gate[a][:, gt, 0:w], ps[:, 4 * a + gt, 0:w],
                                           ACT.Tanh if gt == 2 else ACT.Sigmoid,
                                           bias=bsum[:, (p - 1) * 4 + gt:(p - 1) * 4 + gt + 1]).then_inc(c_ga[a], 1)
                        e = k - 2
                        if ("C", g) == W_IN and 0 <= e < E:
                            high_half(1, e, a, wstage1)

            m = 0
            for k, s in enumerate(plan):
                begin_step(act, "act", k)
                if s[0] == "A":
                    setup_and_graph0()
                elif s[0] == "P":
                    n = prep_order.index(s[1:])
                    prep(n, *s[1:])
                    if k + 1 not in routed_with:
                        weight_exponentials(n)
                elif s[0] == "X":
                    experts(m, *s[1:], prep_order.index(routed_with[k]) if k in routed_with else None)
                    m += 1
                elif s[0] == "C":
                    graph1(s[1])
                end_step(act, "act")

        @block.vector
        def _(dve):
            regs = expert_registers(dve, "dve")
            ch = Chain(dve, d_ch)
            link, mark = ch.link, ch.mark
            tt, ts, stt = dve.tensor_tensor, dve.tensor_scalar, dve.scalar_tensor_tensor
            nroot = [0]

            def root():
                nroot[0] += 1
                dve.wait_ge(s_asq, nroot[0])

            def tile_stats(t0, nt):
                for t in range(nt):
                    last = dve.bn_stats(st[:, t, :], xt[:, bass.ds(t0 + t, 1), :].rearrange("p a d -> p (a d)"))
                link(last)

            def ln_variance(nt):
                s = lambda k: stat[:, k, 0:nt]
                mark(tt(s(0), st[:, 0:nt, 1], st[:, 0:nt, 4], ALU.add))
                mark(tt(s(1), st[:, 0:nt, 1], st[:, 0:nt, 4], ALU.subtract))
                link(tt(s(2), st[:, 0:nt, 2], st[:, 0:nt, 5], ALU.add))
                mark(ts(s(0), s(0), 0.5, None, ALU.mult))
                link(tt(s(1), s(1), s(1), ALU.mult))
                link(stt(s(3), s(1), D / 4.0, s(2), ALU.mult, ALU.add))

            def ln_stats(nt):
                s = lambda k: stat[:, k, 0:nt]
                ln_variance(nt)
                ts(s(3), s(3), 1.0 / D, EPS, ALU.mult, ALU.add).then_inc(s_need, 1)
                root()
                link(dve.reciprocal(s(5), s(4)))

            def setup():
                dve.wait_ge(s_tr, 1)
                dve.wait_ge(s_cst, 13)
                dve.wait_ge(s_adj, 16)
                ps0 = bank(0).rearrange("p (t m) -> p t m", t=2)
                dve.tensor_copy(adjT[:, :, :], ps0).then_inc(s_ev, 1)
                mark(dve.tensor_copy(adj_i, adj_n))
                link(dve.tensor_copy(adj_it, ps0))
                for t in range(2):
                    d = slice(t * P, (t + 1) * P)
                    mark(tt(adj_i[:, t, d], adj_i[:, t, d], ident[:, :], ALU.add))
                    mark(tt(adj_it[:, t, d], adj_it[:, t, d], ident[:, :], ALU.add))
                ch.wait()
                for t in range(2):
                    mark(tt(ahatT[:, 0, t * P:(t + 1) * P], adj_i[:, t, t * P:(t + 1) * P], ident[:, :], ALU.mult))
                mark(dve.reduce_sum(deg[:, 0, :], adj_i, axis=AX.X))
                mark(dve.reduce_sum(deg[:, 1, :], adj_it, axis=AX.X))
                ch.wait()
                link(dve.reduce_sum(deg[:, 2, :], ahatT[:, 0, :].rearrange("p (t m) -> p t m", t=2), axis=AX.X))
                link(tt(deg[:, 3, :], deg[:, 0, :], deg[:, 1, :], ALU.add))
                tt(deg[:, 3, :], deg[:, 3, :], deg[:, 2, :], ALU.subtract).then_inc(s_need, 1)
                dve.wait_ge(s_tr, 2)
                dve.tensor_copy(vec[:, :], ps[:, 1, 0:R_ROWS]).then_inc(s_ev, 1)
                dve.wait_ge(s_ev, 2)
                mark(ts(lng_s[:, :], vec[:, R_LNG:R_LNG + E], SC, None, ALU.mult))
                mark(tt(bsum[:, :], vec[:, R_BIH:R_BIH + 16], vec[:, R_BHH:R_BHH + 16], ALU.add))
                dve.wait_ge(s_tr, 3)
                mark(dve.tensor_copy(w1T, ps[:, 2, 0:GH]))
                dve.tensor_copy(w2T.rearrange("p t d -> p (t d)"), ps[:, 2, GH:2 * GH]).then_inc(s_ev, 1)
                root()
                link(dve.reciprocal(deg[:, 5, :], deg[:, 4, :]))
                mark(ts(adj_i[:, 0, :], adj_i[:, 0, :], deg[:, 5, 0:1], None, ALU.mult))
                ch.wait()
                ts(adj_i[:, 1, :], adj_i[:, 1, :], deg[:, 5, 1:2], None, ALU.mult).then_inc(s_ev, 1)
                dve.wait_ge(s_tr, 4)
                dve.tensor_copy(bmap[:, :], ps[:, 3, 0:T]).then_inc(s_ev, 1)
                dve.wait_ge(s_tr, 5)
                ch.wait()
                ts(ahatT[:, 0, :], ps[:, 4, 0:T], deg[:, 5, 0:1], None, ALU.mult)
                ts(ahatT[:, 1, :], ps[:, 4, T:2 * T], deg[:, 5, 1:2], None, ALU.mult).then_inc(s_ev, 1)

            def normalise_into(dst, j_of, nt):
                for t in range(nt):
                    last = ts(dst(t), j_of(t), stat[:, 0, t:t + 1], stat[:, 5, t:t + 1], ALU.subtract, ALU.mult)
                return last

            def graph0():
                for k in range(NT // GT):
                    if k in (0, NT // GT // 2):
                        dve.wait_ge(s_xin[k // (NT // GT // 2)], 16)
                    tile_stats(k * GT, GT)
                    ln_stats(GT)
                    mark(dve.tensor_copy(stat_all[:, 0, k * GT:(k + 1) * GT], stat[:, 0, 0:GT]))
                    link(dve.tensor_copy(stat_all[:, 1, k * GT:(k + 1) * GT], stat[:, 5, 0:GT]))

                def normalise(c, q):
                    if not (isinstance(c, int) and c < 2):
                        dve.wait_ge(s_agg, c - 1)
                    for t in range(4):
                        j = c * 4 + t
                        last = ts(xn[q][:, t, :], xt[:, bass.ds(j, 1), :].rearrange("p a d -> p (a d)"),
                                  stat_all[:, 0, bass.ds(j, 1)], stat_all[:, 1, bass.ds(j, 1)],
                                  ALU.subtract, ALU.mult)
                    last.then_inc(s_xn, 1)

                def stats1(c):
                    dve.wait_ge(s_h1c, 2 * c + 2)
                    for o in range(2):
                        last = dve.bn_stats(bnst[:, o, bass.ds(c, 1), :].rearrange("p a s -> p (a s)"),
                                            hid[:, o, bass.ds(c * 512, 512)])
                    mark(last)

                normalise(0, 0)
                normalise(1, 1)
                with dve.Fori(0, NCH // 2 - 1) as j:
                    ch.enter(j, 2)
                    for q in range(2):
                        normalise(2 * j + q + 2, q)
                        stats1(2 * j + q)
                        low_half(0, j, q, wstage)
                    ch.leave(NCH // 2 - 1)
                stats1(NCH - 2)
                stats1(NCH - 1)
                for k in range(2):
                    low_half(0, E - 1, k, wstage)
                expert_bias()
                ch.wait()
                for o in range(2):
                    mark(dve.bn_aggr(bnag[:, o, :], bnst[:, o, :, :].rearrange("p c s -> p (c s)")))
                ch.wait()
                ts(bnag[:, :, 1], bnag[:, :, 1], EPS, None, ALU.add).then_inc(s_need, 1)
                root()
                link(dve.reciprocal(bn1s[:, :], bnag[:, :, 1]))
                link(tt(bn1s[:, :], bn1s[:, :], vec[:, R_G1:R_G1 + 2], ALU.mult))
                link(tt(bn1t[:, :], bnag[:, :, 0], bn1s[:, :], ALU.mult))
                tt(bn1t[:, :], vec[:, R_BE1:R_BE1 + 2], bn1t[:, :], ALU.subtract).then_inc(s_bn1, 1)

                with dve.Fori(0, NCH // 2) as j:
                    ch.enter(j, 2)
                    for q in range(2):
                        c = 2 * j + q
                        dve.wait_ge(s_o2, c + 1)
                        ts(o2T[:, bass.ds(c * 512, 512)], bank(6 + q), vec[:, R_B2:R_B2 + 1], None, ALU.add)\
                            .then_inc(s_o2c, 1)
                        dve.wait_ge(s_o2c, c + 1)
                        last = dve.bn_stats(bnst[:, 0, bass.ds(c, 1), :].rearrange("p a s -> p (a s)"),
                                            o2T[:, bass.ds(c * 512, 512)])
                        mark(last)
                    ch.leave(NCH // 2)
                ch.wait()
                link(dve.bn_aggr(bnag[:, 0, :], bnst[:, 0, :, :].rearrange("p c s -> p (c s)")))
                ts(bnag[:, 0, 1:2], bnag[:, 0, 1:2], EPS, None, ALU.add).then_inc(s_need, 1)
                root()
                link(dve.reciprocal(bn2s[:, :], bnag[:, 0, 1:2]))
                link(tt(bn2s[:, :], bn2s[:, :], vec[:, R_G2:R_G2 + 1], ALU.mult))
                link(tt(bn2t[:, :], bnag[:, 0, 0:1], bn2s[:, :], ALU.mult))
                tt(bn2t[:, :], vec[:, R_BE2:R_BE2 + 1], bn2t[:, :], ALU.subtract).then_inc(s_bn2, 1)

            def low_half(l, e, k, bufs):
                dve.wait_ge(s_wh, NLSTM + 2 * (E * l + e) + k + 1)
                scale = lng_s[:, bass.ds(e, 1)] if l == 0 and k == 0 else SC
                stt(half_of_weights(e, k, 1), bufs[k].rearrange("p (t c) -> p t c", t=HT), scale,
                    half_of_weights(e, k, 0), ALU.mult, ALU.subtract).then_inc(s_wl, 1)

            def expert_bias():
                dve.wait_ge(s_fold, E)
                mark(tt(eb1[:, 0, :], ps[:, 6, 0:E * HT], vec[:, R_FB1[0]:R_FB1[0] + E * HT], ALU.add))
                mark(dve.tensor_copy(eb1[:, 1, :], vec[:, R_FB1[1]:R_FB1[1] + E * HT]))

            def bc(ap, n):
                return ap.unsqueeze(2).to_broadcast([ap.shape[0], ap.shape[1], n])

            def mid(ap, m):
                return ap.unsqueeze(1).to_broadcast([ap.shape[0], m, ap.shape[1]])

            def prep(n, l, g):
                t0 = g * GT
                if l == 0:
                    for c in range(GT // 4):
                        dve.wait_ge(s_yt, g * (GT // 4) + c + 1)
                        v = xt[:, t0 + 4 * c:t0 + 4 * c + 4, :].rearrange("p t d -> p (t d)")
                        tt(v, v, bank(c % 2), ALU.add).then_inc(s_x2, 1)
                    dve.wait_ge(s_x2, (g + 1) * (GT // 4))
                tile_stats(t0, GT)
                z = lambda k: stat[:, k, :]
                ln_variance(GT)
                ts(z(6), z(3), 1.0 / D, EPS, ALU.mult, ALU.add).then_inc(s_need, 1)
                root()
                link(dve.reciprocal(z(5), z(4)))
                if l == 0:
                    link(tt(z(7), z(5), z(5), ALU.mult))
                    link(tt(z(7), z(7), z(3), ALU.mult))
                    ts(z(7), z(7), 1.0 / D, EPS, ALU.mult, ALU.add).then_inc(s_need, 1)
                for t in range(GT):
                    last = ts(lnx[:, t, :], xt[:, t0 + t, :], z(0)[:, t:t + 1], z(5)[:, t:t + 1],
                              ALU.subtract, ALU.mult)
                    if t % 4 == 3:
                        last.then_inc(s_lx, 1)
                if l == 0:
                    root()
                    link(dve.reciprocal(z(7), z(7)))
                    ts(z(7), z(7), SC, None, ALU.mult).then_inc(s_xe, 1)
                    dve.wait_ge(s_xe, g + 1)
                for c in range(GT // 4):
                    dve.wait_ge(s_xhh, n * (GT // 4) + c + 1)
                    v = lnh[n % 2]
                    if l == 0:
                        for t in range(4 * c, 4 * c + 4):
                            mark(stt(v[:, t, D:2 * D], lnx[:, t, :], z(7)[:, t:t + 1], v[:, t, 0:D],
                                     ALU.mult, ALU.subtract))
                    else:
                        c4 = slice(4 * c, 4 * c + 4)
                        mark(stt(v[:, c4, D:2 * D], lnx[:, c4, :], SC, v[:, c4, 0:D], ALU.mult, ALU.subtract))
                dve.wait_ge(s_lg, (n + 1) * (GT // 4))
                link(tt(route["L"][:, :, :], ps[:, 6, 0:GT * E].rearrange("p (t e) -> p t e", e=E),
                        mid(brb[:, l, :], GT), ALU.add))

            L, ra, rb, oh1, oh2, sm = (route[k][:, :, :] for k in ("L", "a", "b", "oh1", "oh2", "sm"))
            r = lambda k: r16[:, k, :]

            def select():
                for k, oh in ((0, oh1), (1, oh2)):
                    link(dve.reduce_max(r(k), L, axis=AX.X))
                    link(tt(ra, L, bc(r(k), E), ALU.is_equal))
                    link(tt(ra, ra, mid(desc[:, :], GT), ALU.mult))
                    link(dve.reduce_max(r(3), ra, axis=AX.X))
                    link(tt(oh, ra, bc(r(3), E), ALU.is_equal))
                    if k == 0:
                        link(stt(L, oh, -3.0e38, L, ALU.mult, ALU.add))
                tt(M16[:, :, :], oh1, oh2, ALU.add).then_inc(s_m, 1)
                tt(r(2), r(1), r(0), ALU.subtract).then_inc(s_exn, 1)

            def take_counts(n):
                dve.wait_ge(s_cnt, n + 1)
                mark(dve.tensor_copy(sm, ps[:, 5, 0:GT * E].rearrange("p (t e) -> p t e", e=E)))
                mark(dve.tensor_copy(ejt[:, :, :], ps[:, 5, 128:128 + GT * E].rearrange("p (t e) -> p e t", e=E)))

            def place_experts(inst):
                ch.wait()
                f = lambda z: z[:, :, :].rearrange("p e t -> p (e t)")
                link(dve.tensor_tensor_scan(f(ejc), ej_mask[:, :], f(ejt), 0.0, ALU.mult, ALU.add))
                mark(tt(ejt[:, :, :], ejc[:, :, :], ejt[:, :, :], ALU.subtract))
                link(tt(gtk[:, :, :], bc(ejc[:, :, GT - 1], KMAX), mid(k_blk[:, :], E), ALU.is_gt))
                link(dve.reduce_sum(r8[:, 0, :], gtk[:, :, :], axis=AX.X))
                link(dve.tensor_tensor_scan(r8[:, 1, :], one8[:, :], r8[:, 0, :], 0.0, ALU.mult, ALU.add))
                link(tt(r8[:, 2, :], r8[:, 1, :], r8[:, 0, :], ALU.subtract))
                mark(ts(r8[:, 2, :], r8[:, 2, :], float(BLK), None, ALU.mult))
                link(tt(geb[:, :, :], bc(iota_b[:, :], E - 1), mid(r8[0:1, 1, 0:E - 1], NBLK), ALU.is_ge))
                with nc.allow_low_precision(reason="counts are small integers"):
                    mark(dve.reduce_sum(ids[0:1, inst, 0:NBLK], geb[:, :, :], axis=AX.X))

            def place_tokens(inst):
                link(tt(sm, sm, ejt[:, :, :].rearrange("p e t -> p t e"), ALU.add))
                link(tt(sm, sm, mid(r8[:, 2, :], GT), ALU.add))
                for k, (oh, b) in enumerate(((oh1, ra), (oh2, rb))):
                    mark(tt(b, oh, sm, ALU.mult))
                ch.wait()
                with nc.allow_low_precision(reason="slots are integers below 2^24"):
                    for k, b in enumerate((ra, rb)):
                        last = dve.reduce_sum(slot[:, inst, k, :], b, axis=AX.X)
                last.then_inc(s_rt, 1)

            def weights(n, inst):
                dve.wait_ge(s_exd, n + 1)
                link(ts(r(4), r(2), 1.0, None, ALU.add))
                link(dve.reciprocal(wts[:, inst, 0, :], r(4)))
                tt(wts[:, inst, 1, :], r(2), wts[:, inst, 0, :], ALU.mult).then_inc(s_w, 1)

            def route_group(n, l, g):
                select()
                take_counts(n)
                place_experts(G * l + g)
                place_tokens(G * l + g)
                weights(n, G * l + g)

            def experts(m, l, g, routed):
                inst = G * l + g
                lo = m * NBLK
                if routed is not None:
                    n_r, inst_r = prep_order.index(routed), G * routed[0] + routed[1]

                def take(i, q):
                    dve.wait_ge(s_T, lo + i + 1)
                    dve.tensor_copy(xs[q], xT[q][:, 0:2 * BLK]).then_inc(s_xs, 1)

                def hidden_high(i, q):
                    dve.wait_ge(s_gl, 2 * (lo + i) + 1)
                    ts(hh[q][:, 0:2, :].rearrange("p t n -> p (t n)"), hf[:, 0:2 * BLK], SC, None, ALU.mult)\
                        .then_inc(s_hh, 1)

                def hidden_low(i, q, hp):
                    if hp == 0:
                        dve.wait_ge(s_hh, lo + i + 1)
                    else:
                        dve.wait_ge(s_gl, 2 * (lo + i) + 2)
                    f = lambda z: z[q][:, 2 * hp:2 * hp + 2, :].rearrange("p t n -> p (t n)")
                    stt(f(hl), hf[:, hp * 2 * BLK:(hp + 1) * 2 * BLK], SC, f(hh), ALU.mult, ALU.subtract)\
                        .then_inc(s_hl, 1)

                def result(i, q, j=None):
                    load_expert_id(dve, regs, q, inst, i)
                    e = expert_id(dve, regs, q)
                    dve.wait_ge(s_D, lo + i + 1)
                    k = i // 2 if isinstance(i, int) else j
                    dve.wait_ge(s_yo[q], 16 * (m * ((NBLK + 1 - q) // 2) + k + 1))
                    sums = ps[:, 4 + q, :].rearrange("p (h s d) -> p h s d", h=2, s=2)
                    stt(yb_out[q], sums[:, :, 0, :], UNSC, eb2[l][:, bass.ds(e, 1), :].to_broadcast([P, 2, D]),
                        ALU.mult, ALU.add).then_inc(s_yh, 1)
                    dve.wait_ge(s_yh, lo + i + 1)
                    stt(yb_out[q], sums[:, :, 1, :], UNSC, yb_out[q], ALU.mult, ALU.add).then_inc(s_y, 1)

                take(0, 0)
                take(1, 1)
                if routed is not None:
                    select()
                hidden_high(0, 0)
                hidden_low(0, 0, 0)
                hidden_low(0, 0, 1)
                take(2, 0)
                hidden_high(1, 1)
                hidden_low(1, 1, 0)
                if routed is not None:
                    take_counts(n_r)
                result(0, 0)
                hidden_low(1, 1, 1)
                take(3, 1)
                for i in (2, 3):
                    hidden_high(i, i % 2)
                    take(i + 2, i % 2)
                    hidden_low(i, i % 2, 0)
                    result(i - 1, 1 - i % 2)
                    hidden_low(i, i % 2, 1)
                    if routed is not None:
                        place_experts(inst_r) if i == 2 else place_tokens(inst_r)
                with dve.Fori(2, NBLK // 2 - 1) as j:
                    for q in range(2):
                        i = 2 * j + q
                        hidden_high(i, q)
                        take(i + 2, q)
                        hidden_low(i, q, 0)
                        result(i - 1, 1 - q, j - 1 + q)
                        hidden_low(i, q, 1)
                for i in range(NBLK - 3, NBLK):
                    hidden_high(i, i % 2)
                    if i + 2 < NBLK:
                        take(i + 2, i % 2)
                    hidden_low(i, i % 2, 0)
                    result(i - 1, 1 - i % 2)
                    hidden_low(i, i % 2, 1)
                if routed is not None:
                    weights(n_r, inst_r)
                result(NBLK - 1, 0)

            def graph1(g):
                n = 2 * g
                NS = len(LSTM_STEPS)
                dve.wait_ge(s_cb, (GT // 4) * (expert_order.index((0, g)) + 1))
                tile_stats(n * QT, 2 * QT)
                ln_variance(2 * QT)
                for a in range(2):
                    r = slice(a * QT, (a + 1) * QT)
                    ts(stat[:, 3, r], stat[:, 3, r], 1.0 / D, EPS, ALU.mult, ALU.add).then_inc(c_need, 1)
                for a in range(2):
                    r = slice(a * QT, (a + 1) * QT)
                    dve.wait_ge(c_rt, n + a + 1)
                    link(dve.reciprocal(stat[:, 5, r], stat[:, 4, r]))
                    for t in range(QT):
                        j = a * QT + t
                        last = ts(xl[a][:, t, :], xt[:, n * QT + j, :], stat[:, 0, j:j + 1], stat[:, 5, j:j + 1],
                                  ALU.subtract, ALU.mult)
                    last.then_inc(c_xl, 1)
                for a in range(2):
                    for h in range(2):
                        dve.wait_ge(c_w0, 2 * (n + a) + h + 1)
                        tt(h1T[a][:, h * 512:(h + 1) * 512].rearrange("p (b t) -> p b t", b=2),
                           bank(4 * a + 2 + h).rearrange("p (b t) -> p b t", b=2), mid(bmap[:, :], 2), ALU.add)\
                            .then_inc(c_hp, 1)
                for a in range(2):
                    for h in range(2):
                        dve.wait_ge(c_u, 2 * (n + a) + h + 1)
                        tt(u2[a][:, 4 * h:4 * h + 4, :], bank(4 * a + h).rearrange("p (t d) -> p t d", t=4),
                           mid(bg1b[:, :], 4), ALU.add).then_inc(c_u2, 1)
                lo = g * GATES_PER_QUAD
                seen = [0, 0]
                for k, (p, sstep, half) in enumerate(LSTM_STEPS):
                    nw = T // p
                    nb = 2 if p == 1 else 4
                    w = nb * nw

                    def new_cell(a):
                        cv = cell[a][:, 0:w]
                        i, f, c = (gate[a][:, z, 0:w] for z in range(3))
                        dve.wait_ge(c_ga[a], lo + seen[a] + 2)
                        if sstep == 0:
                            tt(cv, i, c, ALU.mult).then_inc(c_c[a], 1)
                        else:
                            mark(tt(i, i, c, ALU.mult))
                            dve.wait_ge(c_ga[a], lo + seen[a] + 3)
                            link(tt(cv, f, cv, ALU.mult))
                            tt(cv, cv, i, ALU.add).then_inc(c_c[a], 1)
                        seen[a] += 3 if sstep == 0 else 4

                    def new_hidden(a):
                        hv = hT[a].rearrange("p (b t) -> p b t", b=4)
                        dve.wait_ge(c_tc[a], g * NS + k + 1)
                        dve.wait_ge(c_ga[a], lo + seen[a])
                        if sstep == p - 1:
                            dst = hv[:, nb * half:nb * half + nb, sstep:sstep + (nw - 1) * p + 1:p]
                            v = lambda z: z.rearrange("p (b t) -> p b t", b=nb)
                        else:
                            dst = hcur[a][:, 0:w]
                            v = lambda z: z
                        tt(dst, v(gate[a][:, 3, 0:w]), v(gate[a][:, 2, 0:w]), ALU.mult).then_inc(c_h[a], 1)

                    for a in range(2):
                        new_cell(a)
                        new_hidden(a)
                        if ("C", g) == W_IN and 0 <= k - 2 < E:
                            low_half(1, k - 2, a, wstage1)
                for a in range(2):
                    for h in range(2):
                        dve.wait_ge(c_bk, 2 * (n + a) + h + 1)
                        j = n * QT + a * QT + 4 * h
                        v = xt[:, j:j + 4, :].rearrange("p t d -> p (t d)")
                        tt(v, v, bank(4 * a + h), ALU.add).then_inc(c_x3, 1)
                dve.wait_ge(c_x3, 2 * n + 4)

            m = 0
            for k, s in enumerate(plan):
                begin_step(dve, "dve", k)
                if s[0] == "A":
                    setup()
                    graph0()
                elif s[0] == "P":
                    n = prep_order.index(s[1:])
                    prep(n, *s[1:])
                    if k + 1 not in routed_with:
                        route_group(n, *s[1:])
                elif s[0] == "X":
                    experts(m, *s[1:], routed_with.get(k))
                    m += 1
                elif s[0] == "C":
                    graph1(s[1])
                end_step(dve, "dve")


_INS = ["x", "adj", "L0_gnn_W1", "L0_gnn_b1", "L0_gnn_g1", "L0_gnn_be1", "L0_gnn_W2", "L0_gnn_b2", "L0_gnn_g2",
        "L0_gnn_be2", "L0_ffn_Wr", "L0_ffn_br", "L0_ffn_ln_g", "L0_ffn_ln_b", "L0_ffn_W1", "L0_ffn_b1", "L0_ffn_W2",
        "L0_ffn_b2", "L1_gnn_Wg0", "L1_gnn_bg0", "L1_gnn_Wg1", "L1_gnn_bg1", "L1_gnn_Wih", "L1_gnn_Whh",
        "L1_gnn_bih", "L1_gnn_bhh", "L1_ffn_Wg", "L1_ffn_bg", "L1_ffn_W1", "L1_ffn_b1", "L1_ffn_W2", "L1_ffn_b2"]


def kernel(**inputs):
    import numpy as _np
    import concourse.bacc as _bacc
    from concourse import mybir as _mybir
    from concourse.bass_utils import run_bass_kernel_spmd as _run

    nc = _bacc.Bacc("TRN2", target_bir_lowering=False, num_devices=1)
    arrays, args = {}, []
    for name in _INS:
        a = _np.ascontiguousarray(inputs[name])
        arrays[f"in_{name}"] = a
        args.append(nc.dram_tensor(f"in_{name}", a.shape, _mybir.dt.from_np(a.dtype), kind="ExternalInput").ap())
    args.append(nc.dram_tensor("out_0", (B, T, D), F32, kind="ExternalOutput").ap())
    graph_moe_kernel(nc, *args)
    r = _run(nc, [arrays], core_ids=[0])
    return r.results[0]["out_0"]
```

```python
from contextlib import ExitStack

import concourse.bass as bass
from concourse import mybir

F32 = mybir.dt.float32
F16 = mybir.dt.float16
BF16 = mybir.dt.bfloat16
I32 = mybir.dt.int32
ALU = mybir.AluOpType
ACT = mybir.ActivationFunctionType
AX = mybir.AxisListType

P = 128
B, T, D = 32, 256, 128
N = B * T
NT = N // P
E, H = 8, 512
HT = H // P
TOP_K = 2
EPS = 1e-5
OUTER_EPS = 1e-5
GH = 256
SKIP = 4

G = 4
GT = NT // G
BLK = 256
NBLK = (GT * P * TOP_K + E * (BLK - 1)) // BLK
SLOTS = NBLK * BLK
KMAX = GT * P // BLK
NCH = NT // 4
QT = 8
NQ = NT // QT
SC = 256.0
UNSC = 1.0 / (SC * SC)
HSC = 16.0

R_FB1 = (0, 32)
R_LNG, R_LNB = 64, 72
R_B1, R_G1, R_BE1 = 80, 82, 84
R_B2, R_G2, R_BE2 = 86, 87, 88
R_BIH, R_BHH = 89, 105
R_ROWS = 121

GATES_PER_QUAD = 2 * 3 + (3 + 4) + (3 + 4 + 4) + (3 + 4 + 4 + 4)
LSTM_STEPS = [(1, 0, 0), (1, 0, 1)] + [(p, s, 0) for p in range(2, SKIP + 1) for s in range(p)]


NLSTM = 2 * SKIP - 1


class Chain:

    def __init__(self, eng, sem):
        self.eng, self.sem, self.base, self.k, self.i, self.per, self.each = eng, sem, 0, 0, None, 0, 0

    def now(self):
        return self.base + self.k if self.i is None else self.base + self.i * self.each + self.k

    def mark(self, ins):
        self.k += 1
        ins.then_inc(self.sem, 1)

    def wait(self):
        self.eng.wait_ge(self.sem, self.now())

    def link(self, ins):
        self.mark(ins)
        self.wait()

    def enter(self, i, per, step=1):
        assert per % step == 0
        self.base, self.k, self.i, self.per, self.each = self.base + self.k, 0, i, per, per // step

    def leave(self, count):
        assert self.k == self.per, (self.k, self.per)
        self.base, self.k, self.i = self.base + self.per * count, 0, None


def step_order():
    return [("A",), ("P", 0, 0), ("W",), ("P", 0, 1), ("X", 0, 0), ("P", 0, 2), ("X", 0, 1), ("P", 0, 3), ("X", 0, 2),
            ("C", 0), ("P", 1, 0), ("X", 0, 3), ("C", 1), ("P", 1, 1), ("X", 1, 0), ("C", 2), ("P", 1, 2),
            ("X", 1, 1), ("C", 3), ("P", 1, 3), ("X", 1, 2), ("X", 1, 3)]


def graph_moe_kernel(nc, x, adj, L0_gnn_W1, L0_gnn_b1, L0_gnn_g1, L0_gnn_be1, L0_gnn_W2, L0_gnn_b2, L0_gnn_g2,
                     L0_gnn_be2, L0_ffn_Wr, L0_ffn_br, L0_ffn_ln_g, L0_ffn_ln_b, L0_ffn_W1, L0_ffn_b1, L0_ffn_W2,
                     L0_ffn_b2, L1_gnn_Wg0, L1_gnn_bg0, L1_gnn_Wg1, L1_gnn_bg1, L1_gnn_Wih, L1_gnn_Whh, L1_gnn_bih,
                     L1_gnn_bhh, L1_ffn_Wg, L1_ffn_bg, L1_ffn_W1, L1_ffn_b1, L1_ffn_W2, L1_ffn_b2, out):
    plan = step_order()
    x_t = x.rearrange("b (h p) d -> p (b h) d", p=P)
    out_t = out.rearrange("b (h p) d -> p (b h) d", p=P)
    fW1 = (L0_ffn_W1, L1_ffn_W1)
    fW2 = (L0_ffn_W2, L1_ffn_W2)

    prep_order = [s[1:] for s in plan if s[0] == "P"]
    expert_order = [s[1:] for s in plan if s[0] == "X"]
    routed_with = {k + 1: s[1:] for k, s in enumerate(plan[:-1]) if s[0] == "P" and plan[k + 1][0] == "X"
                   and s[1:] != plan[k + 1][1:]}
    pool_order = []
    for s in plan:
        if s[0] == "P":
            pool_order.append(("scatter",) + s[1:])
        if s[0] == "X":
            pool_order.append(("gather",) + s[1:])

    with ExitStack() as ctx:
        def sb(name, shape, dt=F32):
            return ctx.enter_context(nc.sbuf_tensor(name, shape, dt))

        def sem(name):
            return ctx.enter_context(nc.semaphore(name))

        def dram(name, shape, dt=F32):
            return nc.dram_tensor(name, shape, dt, kind="Internal").ap()

        slots_in = [dram(f"slots_in{i}", (SLOTS, 2 * D), F16) for i in range(2)]
        slots_out = {inst: dram(f"slots_out{inst[0]}_{inst[1]}", (SLOTS, D)) for inst in expert_order}

        xt = sb("x_tok", [P, NT, D])
        hid = sb("hid", [P, 2, N])
        o2T = hid[:, 0, :]
        taken = [0, 0]

        def carve(half, n):
            a = taken[half]
            taken[half] += n
            assert taken[half] <= N, taken
            return hid[:, half, a:a + n]

        ident = sb("ident", [P, P])
        ident16 = sb("ident16", [P, P], F16)
        tri = sb("tri", [P, P], BF16)
        ones = sb("ones", [P, P], BF16)
        desc = sb("desc", [P, E])
        ej_mask = sb("ej_mask", [P, E * GT])
        k_blk = sb("k_blk", [P, KMAX])
        one8 = sb("one8", [P, E])
        iota_b = sb("iota_b", [1, NBLK])
        rows = sb("rows", [P, P])
        vec = sb("vec", [P, R_ROWS])
        zero = sb("zero", [P, 4 * D])
        act_scratch = sb("act_scratch", [1, 2])
        bn1s = sb("bn1s", [P, 2])
        bn1t = sb("bn1t", [P, 2])
        bn2s = sb("bn2s", [P, 1])
        bn2t = sb("bn2t", [P, 1])
        lng_s = sb("lng_s", [P, E])
        eb1 = sb("eb1", [P, 2, E * HT])
        eb2 = [sb(f"eb2_{l}", [P, E, D]) for l in range(2)]
        Wr = sb("Wr", [P, 2, E])
        Wrhl = sb("Wrhl", [P, 2, 2, E], F16)
        brb = sb("brb", [P, 2, E])
        Wg = sb("Wg", [P, 2, D])
        bg1b = sb("bg1b", [P, D])
        bg0b = sb("bg0b", [P, P])
        bmap = sb("bmap", [P, T])
        adjT = sb("adjT", [P, 2, T])
        bsum = sb("bsum", [P, SKIP * 4])
        wihT = sb("wihT", [P, SKIP, 2, 4 * D], F16)
        whhT = sb("whhT", [P, SKIP - 1, 2, 4 * D], F16)
        W1h = sb("W1h", [P, E, HT, P], F16)
        W1l = sb("W1l", [P, E, HT, P], F16)
        W2hl = sb("W2hl", [P, E, HT, 2, D], F16)

        st = sb("st", [P, GT, 6])
        stat = sb("stat", [P, 8, GT])
        stat_all = sb("stat_all", [P, 2, NT])
        bnst = sb("bnst", [P, 2, NCH, 6])
        bnag = sb("bnag", [P, 2, 2])
        route = {k: sb(f"route_{k}", [P, GT, E]) for k in ("L", "a", "b", "oh1", "oh2", "sm")}
        M16 = sb("M16", [P, GT, E], BF16)
        ejt = sb("ejt", [P, E, GT])
        ejc = sb("ejc", [P, E, GT])
        r16 = sb("r16", [P, 6, GT])
        r8 = sb("r8", [P, 4, E])
        gtk = sb("gtk", [P, E, KMAX])
        geb = sb("geb", [1, NBLK, E - 1])
        ids = sb("ids", [1, 2 * G, NBLK + 1], I32)
        slot = sb("slot", [P, 2 * G, TOP_K, GT], I32)
        wts = sb("wts", [P, 2 * G, TOP_K, GT])

        ARENA = 9216
        arena = sb("arena", [P, ARENA])
        used = [0]

        def area(n):
            a = used[0]
            used[0] += n
            assert used[0] <= ARENA, used[0]
            return arena[:, a:a + n]

        adj_n = area(2 * T).rearrange("p (t m) -> p t m", t=2)
        adj_i = area(2 * T).rearrange("p (t m) -> p t m", t=2)
        adj_it = area(2 * T).rearrange("p (t m) -> p t m", t=2)
        ahatT = area(2 * T).rearrange("p (t m) -> p t m", t=2)
        deg = area(16).rearrange("p (k t) -> p k t", t=2)
        gw1 = area(2 * D).rearrange("p (t d) -> p t d", t=2)
        gw2 = area(GH)
        w1T = area(GH)
        w2T = area(2 * D).rearrange("p (t d) -> p t d", t=2)
        xn = [area(4 * D).rearrange("p (t d) -> p t d", t=4) for _ in range(2)]
        agg = [area(512) for _ in range(2)]
        hb = [area(1024).rearrange("p (t n) -> p t n", t=2) for _ in range(2)]
        wstage = [area(H) for _ in range(2)]
        used[0] = 0
        ygat = area(GT * TOP_K * D).rearrange("p (t k d) -> p t k d", k=TOP_K, t=GT)
        lstm_raw = [arena[:, k * 4 * D:(k + 1) * 4 * D].rearrange("p (t d) -> p t d", t=4) for k in range(NLSTM)]
        assert NLSTM * 4 * D <= used[0]
        wstage1 = [area(H) for _ in range(2)]
        hh, hl = ([area(HT * BLK // 2).bitcast(F16).rearrange("p (t n) -> p t n", t=HT) for _ in range(2)]
                  for _ in range(2))
        lnx = carve(1, GT * D).rearrange("p (t d) -> p t d", t=GT)
        lnh = [carve(1, GT * D).bitcast(F16).rearrange("p (t d) -> p t d", t=GT) if i else
               area(GT * D).bitcast(F16).rearrange("p (t d) -> p t d", t=GT) for i in range(2)]
        hf = carve(1, HT * BLK)
        xrow = [carve(1, 2 * D).bitcast(F16).rearrange("p (h d) -> p h d", h=2) for _ in range(2)]
        yb_out = [carve(1, 2 * D).rearrange("p (h d) -> p h d", h=2) for _ in range(2)]
        xs = [carve(1, BLK).bitcast(F16) for _ in range(2)]
        lxT = [hf[:, i * 512:(i + 1) * 512].bitcast(F16) for i in range(2)]
        ybn = [carve(1, 512) for _ in range(2)]
        hT, gate, cell, hcur, xl, zT, h1T, u2 = [], [], [], [], [], [], [], []
        for _ in range(2):
            hT.append(carve(0, QT * P).bitcast(F16).rearrange("p (s n) -> p s n", s=2))
            g4 = carve(0, 4 * 512)
            ch2 = carve(0, 2 * 512)
            gate.append(g4.rearrange("p (k n) -> p k n", k=4))
            cell.append(ch2[:, 0:512])
            hcur.append(ch2[:, 512:1024].bitcast(F16).rearrange("p (s n) -> p s n", s=2))
            xl.append(g4[:, 0:1024].rearrange("p (t d) -> p t d", t=QT))
            u2.append(xl[-1])
            zT.append(g4[:, 1024:2048])
            h1T.append(ch2)

        ps = ctx.enter_context(nc.psum_tensor("ps", [P, 8, 512], F32))
        xT = [ps[:, 6 + i, :].bitcast(F16) for i in range(2)]

        def bank(i):
            return ps[:, i, :]

        constants_made = sem("constants_made")
        params_loaded = sem("params_loaded")
        adj_loaded = sem("adj_loaded")
        rows_loaded = sem("rows_loaded")
        gnn_weights_loaded = sem("gnn_weights_loaded")
        x_loaded = [sem(f"x_loaded{i}") for i in range(G)]
        lstm_loaded = [sem(f"lstm_loaded{k}") for k in range(NLSTM)]
        expert_loaded = [sem(f"expert_loaded{i}") for i in range(2)]
        zero_made = sem("zero_made")
        slots_filled = sem("slots_filled")
        setup_turned = sem("setup_turned")
        setup_copied = sem("setup_copied")
        root_done = sem("root_done")
        root_wanted = sem("root_wanted")
        lstm_turned = sem("lstm_turned")
        lstm_high = sem("lstm_high")
        lstm_low = sem("lstm_low")
        bias_folded = sem("bias_folded")
        weights_high = sem("weights_high")
        weights_low = sem("weights_low")
        chunk_normalised = sem("chunk_normalised")
        chunk_aggregated = sem("chunk_aggregated")
        aggregate_copied = sem("aggregate_copied")
        hidden_sums = sem("hidden_sums")
        hidden_copied = sem("hidden_copied")
        norm1_ready = sem("norm1_ready")
        relu_done = sem("relu_done")
        output_sums = sem("output_sums")
        output_copied = sem("output_copied")
        norm2_ready = sem("norm2_ready")
        graph_normalised = sem("graph_normalised")
        graph_turned = sem("graph_turned")
        graph_added = sem("graph_added")
        tokens_normed_dve = sem("tokens_normed_dve")
        tokens_turned = sem("tokens_turned")
        router_high = sem("router_high")
        router_low = sem("router_low")
        logits_ready = sem("logits_ready")
        tokens_normed_act = sem("tokens_normed_act")
        deviations_ready = sem("deviations_ready")
        second_norm_ready = sem("second_norm_ready")
        tokens_high = sem("tokens_high")
        differences_ready = sem("differences_ready")
        exponentials_done = sem("exponentials_done")
        mask_ready = sem("mask_ready")
        counts_ready = sem("counts_ready")
        weights_ready = sem("weights_ready")
        slots_ready = sem("slots_ready")
        scattered = [sem(f"scattered{i}") for i in range(2)]
        block_loaded = [sem(f"block_loaded{i}") for i in range(2)]
        block_turned = sem("block_turned")
        block_in_sbuf = sem("block_in_sbuf")
        up_done = sem("up_done")
        gelu_done = sem("gelu_done")
        hidden_high_done = sem("hidden_high_done")
        hidden_low_done = sem("hidden_low_done")
        down_done = sem("down_done")
        result_begun = sem("result_begun")
        result_ready = sem("result_ready")
        result_stored = [sem(f"result_stored{i}") for i in range(2)]
        gathered = [sem(f"gathered{c}") for c in range(GT // 4)]
        gathered_weighted = sem("gathered_weighted")
        first_combined = sem("first_combined")
        combined = sem("combined")
        out_stored = sem("out_stored")
        c_root_wanted = sem("c_root_wanted")
        c_root_done = sem("c_root_done")
        c_normed_dve = sem("c_normed_dve")
        c_normed_act = sem("c_normed_act")
        c_deviations = sem("c_deviations")
        c_agg1 = sem("c_agg1")
        c_agg1_copied = sem("c_agg1_copied")
        c_prod1 = sem("c_prod1")
        c_prod1_bias = sem("c_prod1_bias")
        c_relu1 = sem("c_relu1")
        c_prod2 = sem("c_prod2")
        c_prod2_bias = sem("c_prod2_bias")
        c_agg2 = sem("c_agg2")
        c_relu2 = sem("c_relu2")
        c_input_high = sem("c_input_high")
        c_input_low = sem("c_input_low")
        gate_sums = [sem(f"gate_sums{a}") for a in range(2)]
        gate_done = [sem(f"gate_done{a}") for a in range(2)]
        cell_done = [sem(f"cell_done{a}") for a in range(2)]
        cell_tanh = [sem(f"cell_tanh{a}") for a in range(2)]
        state_split = [sem(f"state_split{a}") for a in range(2)]
        c_turned_back = sem("c_turned_back")
        c_added = sem("c_added")
        dve_chain = sem("dve_chain")
        act_chain = sem("act_chain")

        block = ctx.enter_context(nc.Block())

        def lstm_half(k, low):
            return wihT[:, k, low, :] if k < SKIP else whhT[:, k - SKIP, low, :]

        def lstm_bank(k):
            return (6, 7, 0, 1, 2, 3)[k % 6]

        def by_parity(m, i, q):
            return 8 * i + (16 * (m * ((NBLK + 1 - q) // 2) + 1) - 8 * q)

        def half_of_weights(e, k, low):
            if k == 0:
                return (W1l if low else W1h)[:, bass.ds(e, 1), :, :].rearrange("p a t c -> p (a t) c")
            return W2hl[:, bass.ds(e, 1), :, low, :].rearrange("p a t c -> p (a t) c")

        def expert_registers(eng, who):
            return [eng.alloc_register(f"{who}_expert{q}") for q in range(2)]

        def load_expert_id(eng, regs, q, inst, i):
            eng.load(regs[q], ids[0:1, inst, bass.ds(i, 1)])

        def expert_id(eng, regs, q):
            return eng.snap(regs[q], min_val=0, max_val=E - 1)

        PAR_DMAS = 9
        ZFILLS = 2 * -(-SLOTS // (4 * P))
        W_IN = ("C", 1)

        @block.sync
        def _(sp):
            par = [0]
            for q in range(2):
                sp.sem_inc(result_stored[q], 16)

            def load(dst, src):
                par[0] += 1
                sp.dma_start(dst, src).then_inc(params_loaded, 16)

            sp.dma_start(adj_n, adj.rearrange("(t p) m -> p t m", p=P)).then_inc(adj_loaded, 16)
            sp.dma_start(xt[:, 0:GT, :], x_t[:, 0:GT, :]).then_inc(x_loaded[0], 16)
            sp.dma_start(gw1, L0_gnn_W1.rearrange("(t p) d -> p t d", p=P)).then_inc(gnn_weights_loaded, 16)
            sp.dma_start(gw2, L0_gnn_W2).then_inc(gnn_weights_loaded, 16)
            sp.dma_start(bg0b[:, :], L1_gnn_bg0.partition_broadcast(P)).then_inc(gnn_weights_loaded, 16)
            nrows = 0
            for r, src in ((R_FB1[0], L0_ffn_b1.rearrange("e (t p) -> (e t) p", p=P)),
                           (R_FB1[1], L1_ffn_b1.rearrange("e (t p) -> (e t) p", p=P)),
                           (R_LNG, L0_ffn_ln_g), (R_LNB, L0_ffn_ln_b),
                           (R_B1, L0_gnn_b1.rearrange("(t p) -> t p", p=P)),
                           (R_G1, L0_gnn_g1.rearrange("(t p) -> t p", p=P)),
                           (R_BE1, L0_gnn_be1.rearrange("(t p) -> t p", p=P)),
                           (R_B2, L0_gnn_b2.rearrange("(t p) -> t p", p=P)),
                           (R_G2, L0_gnn_g2.rearrange("(t p) -> t p", p=P)),
                           (R_BE2, L0_gnn_be2.rearrange("(t p) -> t p", p=P)),
                           (R_BIH, L1_gnn_bih.rearrange("s (t p) -> (s t) p", p=P)),
                           (R_BHH, L1_gnn_bhh.rearrange("s (t p) -> (s t) p", p=P))):
                sp.dma_start(rows[r:r + src.shape[0], :], src).then_inc(rows_loaded, 16)
                nrows += 1
            assert nrows == 12
            for k in range(1, G):
                sp.dma_start(xt[:, k * GT:(k + 1) * GT, :], x_t[:, k * GT:(k + 1) * GT, :]).then_inc(x_loaded[k], 16)
            load(Wr[:, 0, :], L0_ffn_Wr)
            load(Wr[:, 1, :], L1_ffn_Wg)
            load(brb[:, 0, :], L0_ffn_br.partition_broadcast(P))
            load(brb[:, 1, :], L1_ffn_bg.partition_broadcast(P))
            load(Wg[:, 0, :], L1_gnn_Wg0)
            load(Wg[:, 1, :], L1_gnn_Wg1)
            load(bg1b[:, :], L1_gnn_bg1.partition_broadcast(P))
            load(eb2[0][:, :, :], L0_ffn_b2.partition_broadcast(P))
            load(eb2[1][:, :, :], L1_ffn_b2.partition_broadcast(P))
            assert par[0] == PAR_DMAS
            def load_lstm(k):
                src = L1_gnn_Wih[k] if k < SKIP else L1_gnn_Whh[k - SKIP + 1]
                sp.dma_start(lstm_raw[k], src.rearrange("(t p) d -> p t d", p=P)).then_inc(lstm_loaded[k], 16)

            def load_expert(l, e, bufs):
                n = E * l + e
                for k in range(2):
                    if not (isinstance(e, int) and n == 0):
                        sp.wait_ge(weights_low, 2 * n - 1 + k)
                        if l == 0 and k == 0:
                            sp.wait_ge(bias_folded, n)
                    src = fW1[l] if k == 0 else fW2[l].rearrange("e (t p) d -> e p t d", p=P)
                    if k == 0:
                        sp.dma_start(bufs[0], src[bass.ds(e, 1)].rearrange("a p h -> (a p) h")).then_inc(expert_loaded[0], 16)
                    else:
                        sp.dma_start(bufs[1].rearrange("p (t d) -> p t d", d=D),
                                     src[bass.ds(e, 1)].rearrange("a p t d -> (a p) t d")).then_inc(expert_loaded[1], 16)

            load_expert(0, 0, wstage)
            with sp.Fori(1, E) as e:
                load_expert(0, e, wstage)
            sp.wait_ge(norm2_ready, 1)
            for k in range(NLSTM):
                load_lstm(k)
            def experts(m, inst):
                n_s = prep_order.index(inst)
                sp.wait_ge(scattered[n_s % 2], 16 * GT * TOP_K * (n_s // 2 + 1))
                src = slots_in[n_s % 2].rearrange("(b p h) d -> b p h d", p=P, h=2)
                dst = slots_out[inst].rearrange("(b p h) d -> b p h d", p=P, h=2)

                def load_block(i, par):
                    sp.dma_start(xrow[par], src[bass.ds(i, 1)].rearrange("a p h d -> (a p) h d"))\
                      .then_inc(block_loaded[par], 16)

                def store_block(i, par):
                    sp.wait_ge(result_ready, i + (m * NBLK + 1))
                    sp.dma_start(dst[bass.ds(i, 1)].rearrange("a p h d -> (a p) h d"), yb_out[par])\
                      .then_inc(result_stored[par], 16)

                load_block(0, 0)
                load_block(1, 1)
                for i in range(4):
                    sp.wait_ge(block_turned, m * NBLK + i + 1)
                    load_block(i + 2, i % 2)
                    if i == 3:
                        store_block(0, 0)
                with sp.Fori(4, NBLK - 3, 2) as i:
                    for q in range(2):
                        sp.wait_ge(block_turned, i + (m * NBLK + q + 1))
                        load_block(i + (q + 2), q)
                        store_block(i + (q - 3), 1 - q)
                sp.wait_ge(block_turned, m * NBLK + NBLK - 2)
                load_block(NBLK - 1, 0)
                for i in range(NBLK - 6, NBLK):
                    store_block(i, i % 2)

            stores = 0
            m = 0
            for s in plan:
                if s == W_IN:
                    with sp.Fori(0, E) as e:
                        load_expert(1, e, wstage1)
                if s[0] == "X":
                    experts(m, s[1:])
                    m += 1
            for mm, (l, g) in enumerate(expert_order):
                for c in range(GT // 4 if l == 1 else 0):
                    sp.wait_ge(combined, mm * (GT // 4) + c + 1)
                    t = g * GT + 4 * c
                    sp.dma_start(out_t[:, t:t + 4, :], xt[:, t:t + 4, :]).then_inc(out_stored, 16)
                    stores += 1
            sp.wait_ge(out_stored, 16 * stores)
            for q in range(2):
                sp.wait_ge(result_stored[q], 16 * m * ((NBLK + 1 - q) // 2) + 16)

        @block.gpsimd
        def _(pool):
            pool.memset(ident[:, :], 0.0).then_inc(constants_made, 1)
            pool.memset(tri[:, :], 1.0).then_inc(constants_made, 1)
            pool.memset(ones[:, :], 1.0).then_inc(constants_made, 1)
            pool.memset(one8[:, :], 1.0).then_inc(constants_made, 1)
            pool.memset(ej_mask[:, :], 1.0).then_inc(constants_made, 1)
            pool.iota(desc[:, :], [[-1, E]], base=E, channel_multiplier=0,
                      allow_small_or_imprecise_dtypes=True).then_inc(constants_made, 1)
            pool.iota(k_blk[:, :], [[BLK, KMAX]], base=0, channel_multiplier=0,
                      allow_small_or_imprecise_dtypes=True).then_inc(constants_made, 1)
            pool.iota(iota_b[:, :], [[1, NBLK]], base=0, channel_multiplier=0,
                      allow_small_or_imprecise_dtypes=True).then_inc(constants_made, 1)
            pool.memset(ident16[:, :], 0.0).then_inc(constants_made, 1)
            pool.memset(zero[:, :], 0.0).then_inc(zero_made, 1)
            pool.memset(act_scratch[:, :], 0.0).then_inc(zero_made, 1)
            pool.wait_ge(constants_made, 9)
            pool.affine_select(out=ident16[:, :], in_=ident16[:, :], compare_op=ALU.not_equal, fill=1.0, base=0,
                               pattern=[[-1, P]], channel_multiplier=1).then_inc(constants_made, 1)
            pool.affine_select(out=ident[:, :], in_=ident[:, :], compare_op=ALU.not_equal, fill=1.0, base=0,
                               pattern=[[-1, P]], channel_multiplier=1).then_inc(constants_made, 1)
            pool.affine_select(out=tri[:, :], in_=tri[:, :], compare_op=ALU.is_gt, fill=0.0, base=0,
                               pattern=[[1, P]], channel_multiplier=-1).then_inc(constants_made, 1)
            pool.affine_select(out=ej_mask[:, :].rearrange("p (e t) -> p e t", e=E),
                               in_=ej_mask[:, :].rearrange("p (e t) -> p e t", e=E),
                               compare_op=ALU.is_gt, fill=0.0, base=0,
                               pattern=[[0, E], [1, GT]], channel_multiplier=0).then_inc(constants_made, 1)
            pool.wait_ge(zero_made, 2)
            for s in slots_in:
                for r in range(0, SLOTS, 4 * P):
                    n = min(4 * P, SLOTS - r)
                    pool.dma_start(s[r:r + n, :].rearrange("(p a) d -> p (a d)", a=4),
                                   zero[0:n // 4, :].bitcast(F16)).then_inc(slots_filled, 16)
            pool.wait_ge(slots_filled, 16 * ZFILLS)
            for what, l, g in pool_order:
                if what == "scatter":
                    n = prep_order.index((l, g))
                    pool.wait_ge(slots_ready, n + 1)
                    if n >= 2:
                        mm = expert_order.index(prep_order[n - 2])
                        pool.wait_ge(block_turned, (mm + 1) * NBLK)
                    for t in range(GT):
                        for k in range(TOP_K):
                            pool.indirect_dma_start(
                                slots_in[n % 2], bass.IndirectOffsetOnAxis(ap=slot[:, G * l + g, k, t:t + 1], axis=0),
                                lnh[n % 2][:, t, :], None).then_inc(scattered[n % 2], 16)
                else:
                    m = expert_order.index((l, g))
                    pool.wait_ge(weights_ready, prep_order.index((l, g)) + 1)
                    if m > 0:
                        pool.wait_ge(combined, m * (GT // 4))
                    pool.wait_ge(result_stored[0], 16 * (m + 1) * ((NBLK + 1) // 2) + 16)
                    pool.wait_ge(result_stored[1], 16 * (m + 1) * (NBLK // 2) + 16)
                    for t in range(GT):
                        for k in range(TOP_K):
                            pool.indirect_dma_start(
                                ygat[:, t, k, :], None, slots_out[(l, g)],
                                bass.IndirectOffsetOnAxis(ap=slot[:, G * l + g, k, t:t + 1], axis=0))\
                                .then_inc(gathered[t // 4], 16)
                    for c in range(GT // 4 if m < len(expert_order) - 1 else 0):
                        pool.wait_ge(gathered[c], 16 * 4 * TOP_K * (m + 1))
                        c4 = slice(4 * c, 4 * c + 4)
                        v = xt[:, g * GT + 4 * c:g * GT + 4 * c + 4, :]
                        for k in range(TOP_K):
                            w = wts[:, G * l + g, k, c4].unsqueeze(2).to_broadcast([P, 4, D])
                            pool.tensor_tensor(ygat[:, c4, k, :], ygat[:, c4, k, :], w, ALU.mult)\
                                .then_inc(gathered_weighted, 1)
                        for k in range(TOP_K):
                            if k:
                                pool.wait_ge(first_combined, m * (GT // 4) + c + 1)
                            else:
                                pool.wait_ge(gathered_weighted, TOP_K * (m * (GT // 4) + c + 1))
                            pool.tensor_tensor(v, v, ygat[:, c4, k, :], ALU.add).then_inc(combined if k else first_combined, 1)

        @block.tensor
        def _(pe):
            regs = expert_registers(pe, "pe")
            mm = pe.matmul

            def setup():
                pe.wait_ge(constants_made, 13)
                pe.wait_ge(adj_loaded, 16)
                for mt in range(2):
                    for nt in range(2):
                        last = pe.transpose(ps[:, 0, mt * T + nt * P:mt * T + (nt + 1) * P],
                                            adj_n[:, nt, mt * P:(mt + 1) * P], ident[:, :])
                last.then_inc(setup_turned, 1)
                pe.wait_ge(rows_loaded, 16 * 12)
                pe.transpose(ps[:, 1, 0:R_ROWS], rows[0:R_ROWS, :], ident[0:R_ROWS, 0:R_ROWS]).then_inc(setup_turned, 1)
                pe.wait_ge(gnn_weights_loaded, 16 * 3)
                for t in range(2):
                    pe.transpose(ps[:, 2, t * P:(t + 1) * P], gw1[:, t, :], ident[:, :])
                for t in range(2):
                    last = pe.transpose(ps[:, 2, GH + t * P:GH + (t + 1) * P], gw2[:, t * P:(t + 1) * P], ident[:, :])
                last.then_inc(setup_turned, 1)
                pe.wait_ge(setup_copied, 1)
                for k in range(2):
                    last = mm(ps[:, 3, 0:T], bg0b[:, :], adjT[:, k, :], start=(k == 0), stop=(k == 1))
                last.then_inc(setup_turned, 1)
                pe.wait_ge(setup_copied, 4)
                for mt in range(2):
                    for nt in range(2):
                        last = pe.transpose(ps[:, 4, mt * T + nt * P:mt * T + (nt + 1) * P],
                                            adj_i[:, nt, mt * P:(mt + 1) * P], ident[:, :])
                last.then_inc(setup_turned, 1)
                pe.wait_ge(setup_copied, 6)

            def graph0():
                def aggregate(c, q, first=False):
                    pe.wait_ge(chunk_normalised, c + 1)
                    if not first:
                        pe.wait_ge(aggregate_copied, c - 1)
                    for b in range(2):
                        for k in range(2):
                            last = mm(ps[:, q, b * T:(b + 1) * T], xn[q][:, 2 * b + k, :], ahatT[:, k, :],
                                      start=(k == 0), stop=(k == 1))
                    last.then_inc(chunk_aggregated, 1)

                def hidden(c, q, first=False):
                    pe.wait_ge(aggregate_copied, c + 1)
                    if not first:
                        pe.wait_ge(hidden_copied, 2 * c - 2)
                    for o in range(2):
                        mm(ps[:, 2 + 2 * q + o, :], w1T[:, o * P:(o + 1) * P], agg[q], start=True, stop=True)\
                            .then_inc(hidden_sums, 1)

                aggregate(0, 0, True)
                aggregate(1, 1, True)
                hidden(0, 0, True)
                aggregate(2, 0)
                hidden(1, 1, True)
                fold_bias(0)
                with pe.Fori(1, NCH // 2 - 1) as j:
                    for q in range(2):
                        c = 2 * j + q
                        aggregate(c + 1, 1 - q)
                        hidden(c, q)
                    fold_bias(j)
                aggregate(NCH - 1, 1)
                hidden(NCH - 2, 0)
                hidden(NCH - 1, 1)
                fold_bias(E - 1)

                def output(c, q, first=False):
                    pe.wait_ge(relu_done, 2 * c + 2)
                    if not first:
                        pe.wait_ge(output_copied, c - 1)
                    for k in range(2):
                        last = mm(ps[:, 6 + q, :], w2T[:, k, :], hb[q][:, k, :], start=(k == 0), stop=(k == 1))
                    last.then_inc(output_sums, 1)

                output(0, 0, True)
                output(1, 1, True)
                with pe.Fori(1, NCH // 2) as j:
                    for q in range(2):
                        output(2 * j + q, q)

            def lstm_weights():
                for k in range(NLSTM):
                    pe.wait_ge(lstm_loaded[k], 16)
                    if k >= 6:
                        pe.wait_ge(lstm_low, k - 5)
                    for t in range(4):
                        last = pe.transpose(ps[:, lstm_bank(k), t * P:(t + 1) * P], lstm_raw[k][:, t, :], ident[:, :])
                    last.then_inc(lstm_turned, 1)
                pe.wait_ge(lstm_low, NLSTM)

            def fold_bias(e):
                pe.wait_ge(expert_loaded[0], 16 * (e + 1))
                for t in range(HT):
                    last = mm(ps[:, 6, bass.ds(e * HT + t, 1)], wstage[0][:, t * P:(t + 1) * P],
                              vec[:, bass.ds(e + R_LNB, 1)], start=True, stop=True)
                last.then_inc(bias_folded, 1)

            def prep(n, l, g):
                if l == 0:
                    for c in range(GT // 4):
                        pe.wait_ge(graph_normalised, g * (GT // 4) + c + 1)
                        if c >= 2:
                            pe.wait_ge(graph_added, g * (GT // 4) + c - 1)
                        for t in range(4):
                            last = pe.transpose(ps[:, c % 2, t * P:(t + 1) * P], ybn[c % 2][:, t * P:(t + 1) * P],
                                                ident[:, :])
                        last.then_inc(graph_turned, 1)
                for c in range(GT // 4):
                    pe.wait_ge(tokens_normed_dve, n * (GT // 4) + c + 1)
                    pe.wait_ge(tokens_normed_act, n * (GT // 4) + c + 1)
                    for t in range(4):
                        last = pe.transpose(ps[:, c, t * P:(t + 1) * P], lnx[:, 4 * c + t, :], ident[:, :])
                    last.then_inc(tokens_turned, 1)
                for c in range(GT // 4):
                    pe.wait_ge(router_low, n * (GT // 4) + c + 1)
                    for t in range(4):
                        o = ps[:, 4, (4 * c + t) * 2 * E:(4 * c + t + 1) * 2 * E]
                        mm(o, lxT[c % 2][:, t * P:(t + 1) * P], Wrhl[:, l, :, :].rearrange("p k e -> p (k e)"),
                           start=True, stop=False)
                        last = mm(o[:, 0:E], lxT[c % 2][:, (4 + t) * P:(5 + t) * P], Wrhl[:, l, 0, :],
                                  start=False, stop=True)
                    last.then_inc(logits_ready, 1)

            def count_selected(n):
                pe.wait_ge(mask_ready, n + 1)
                m2 = M16[:, :, :].rearrange("p t e -> p (t e)")
                mm(ps[:, 5, 0:GT * E], tri[:, :], m2, start=True, stop=True)
                mm(ps[:, 5, 128:128 + GT * E], ones[:, :], m2, start=True, stop=True).then_inc(counts_ready, 1)

            def experts(m, l, g, routed):
                inst = G * l + g
                lo = m * NBLK

                def transposes(i, q):
                    pe.wait_ge(block_loaded[q], by_parity(m, i, q))
                    for half in range(2):
                        for h in range(2):
                            last = pe.transpose(xT[q][:, half * BLK + h * P:half * BLK + (h + 1) * P],
                                                xrow[q][:, h, half * D:(half + 1) * D], ident16[:, :])
                    last.then_inc(block_turned, 1)

                def up(i, q):
                    load_expert_id(pe, regs, q, inst, i)
                    e = expert_id(pe, regs, q)
                    pe.wait_ge(block_in_sbuf, i + (lo + 1))
                    for hp in range(2):
                        for ht in (2 * hp, 2 * hp + 1):
                            o = ps[:, 2 * q + hp, (ht % 2) * BLK:(ht % 2 + 1) * BLK]
                            wh = W1h[:, bass.ds(e, 1), ht, :].rearrange("p a c -> p (a c)")
                            wl = W1l[:, bass.ds(e, 1), ht, :].rearrange("p a c -> p (a c)")
                            mm(o, wh, xs[q][:, 0:BLK], start=True, stop=False)
                            mm(o, wh, xs[q][:, BLK:2 * BLK], start=False, stop=False)
                            last = mm(o, wl, xs[q][:, 0:BLK], start=False, stop=True)
                        last.then_inc(up_done, 1)

                def down(i, q):
                    e = expert_id(pe, regs, q)
                    pe.wait_ge(hidden_low_done, 2 * i + (2 * lo + 2))
                    for h in range(2):
                        o = ps[:, 4 + q, h * 2 * D:(h + 1) * 2 * D]
                        for kt in range(HT):
                            w = W2hl[:, bass.ds(e, 1), kt, :, :].rearrange("p a s c -> p (a s c)")
                            wh = W2hl[:, bass.ds(e, 1), kt, 0, :].rearrange("p a c -> p (a c)")
                            mm(o, hh[q][:, kt, h * P:(h + 1) * P], w, start=(kt == 0), stop=False)
                            last = mm(o[:, 0:D], hl[q][:, kt, h * P:(h + 1) * P], wh, start=False,
                                      stop=(kt == HT - 1))
                    last.then_inc(down_done, 1)

                transposes(0, 0)
                transposes(1, 1)
                up(0, 0)
                transposes(2, 0)
                up(1, 1)
                if routed is not None:
                    count_selected(routed)
                down(0, 0)
                transposes(3, 1)
                for i in (2, 3):
                    up(i, i % 2)
                    transposes(i + 2, i % 2)
                    down(i - 1, 1 - i % 2)
                with pe.Fori(4, NBLK - 3, 2) as i:
                    for q in range(2):
                        up(i + q, q)
                        transposes(i + q + 2, q)
                        down(i + q - 1, 1 - q)
                up(NBLK - 3, 0)
                transposes(NBLK - 1, 0)
                down(NBLK - 4, 1)
                up(NBLK - 2, 1)
                down(NBLK - 3, 0)
                up(NBLK - 1, 0)
                down(NBLK - 2, 1)
                down(NBLK - 1, 0)

            def graph1(g):
                n = 2 * g
                for a in range(2):
                    pe.wait_ge(c_normed_dve, n + a + 1)
                    pe.wait_ge(c_normed_act, n + a + 1)
                    for b in range(4):
                        for k in range(2):
                            last = mm(ps[:, 4 * a + b // 2, (b % 2) * T:(b % 2 + 1) * T], xl[a][:, 2 * b + k, :],
                                      adjT[:, k, :], start=(k == 0), stop=(k == 1))
                        if b % 2:
                            last.then_inc(c_agg1, 1)
                for a in range(2):
                    for h in range(2):
                        pe.wait_ge(c_agg1_copied, 2 * (n + a) + h + 1)
                        mm(ps[:, 4 * a + 2 + h, :], Wg[:, 0, :], zT[a][:, h * 512:(h + 1) * 512],
                           start=True, stop=True).then_inc(c_prod1, 1)
                for a in range(2):
                    for h in range(2):
                        pe.wait_ge(c_relu1, 2 * (n + a) + h + 1)
                        for t in range(4):
                            last = mm(ps[:, 4 * a + h, t * P:(t + 1) * P],
                                      h1T[a][:, (4 * h + t) * P:(4 * h + t + 1) * P], Wg[:, 1, :],
                                      start=True, stop=True)
                        last.then_inc(c_prod2, 1)
                for a in range(2):
                    for b in range(4):
                        if b % 2 == 0:
                            pe.wait_ge(c_prod2_bias, 2 * (n + a) + b // 2 + 1)
                        for k in range(2):
                            last = mm(ps[:, 4 * a + 2 + b // 2, (b % 2) * T:(b % 2 + 1) * T], u2[a][:, 2 * b + k, :],
                                      adjT[:, k, :], start=(k == 0), stop=(k == 1))
                        if b % 2:
                            last.then_inc(c_agg2, 1)
                NS = len(LSTM_STEPS)
                lo = g * GATES_PER_QUAD
                seen = [0, 0]
                for k, (p, s, half) in enumerate(LSTM_STEPS):
                    gates = (0, 2, 3) if s == 0 else (0, 2, 1, 3)
                    nw = T // p
                    nb = 2 if p == 1 else 4
                    w = nb * nw
                    for a in range(2):
                        hv = hT[a].rearrange("p s (b t) -> p s b t", b=4)
                        xin = hv[:, :, nb * half:nb * half + nb, s:s + (nw - 1) * p + 1:p]
                        if k == 0:
                            pe.wait_ge(c_input_low, 2 * (n + a) + 2)
                        elif s == 0:
                            pe.wait_ge(state_split[a], g * NS + k)
                        if k > 0:
                            pe.wait_ge(gate_done[a], lo + seen[a])
                        for gt in gates:
                            o = ps[:, 4 * a + gt, 0:w]
                            wi = wihT[:, p - 1, :, gt * P:(gt + 1) * P]
                            mm(o, wi[:, 0, :], xin[:, 0], start=True, stop=False)
                            mm(o, wi[:, 0, :], xin[:, 1], start=False, stop=False)
                            mm_ = mm(o, wi[:, 1, :], xin[:, 0], start=False, stop=(s == 0))
                            if s > 0:
                                if gt == gates[0]:
                                    pe.wait_ge(state_split[a], g * NS + k)
                                wh = whhT[:, p - 2, :, gt * P:(gt + 1) * P]
                                mm(o, wh[:, 0, :], hcur[a][:, 0, 0:w], start=False, stop=False)
                                mm(o, wh[:, 0, :], hcur[a][:, 1, 0:w], start=False, stop=False)
                                mm_ = mm(o, wh[:, 1, :], hcur[a][:, 0, 0:w], start=False, stop=True)
                            mm_.then_inc(gate_sums[a], 1)
                            seen[a] += 1
                for a in range(2):
                    pe.wait_ge(state_split[a], (g + 1) * NS)
                    pe.wait_ge(gate_done[a], lo + seen[a])
                    for h in range(2):
                        for t in range(4):
                            for k in range(2):
                                last = mm(ps[:, 4 * a + h, t * P:(t + 1) * P],
                                          hT[a][:, k, (4 * h + t) * P:(4 * h + t + 1) * P], ident16[:, :],
                                          start=(k == 0), stop=(k == 1))
                        last.then_inc(c_turned_back, 1)

            m = 0
            for k, s in enumerate(plan):
                if s[0] == "A":
                    setup()
                    graph0()
                elif s[0] == "W":
                    lstm_weights()
                elif s[0] == "P":
                    n = prep_order.index(s[1:])
                    prep(n, *s[1:])
                    if k + 1 not in routed_with:
                        count_selected(n)
                elif s[0] == "X":
                    experts(m, *s[1:], prep_order.index(routed_with[k]) if k in routed_with else None)
                    m += 1
                elif s[0] == "C":
                    graph1(s[1])

        @block.scalar
        def _(act):
            regs = expert_registers(act, "act")
            ch = Chain(act, act_chain)
            roots = [0]

            def warm(func):
                act.activation(act_scratch[:, 1:2], act_scratch[:, 0:1], func)

            def root(dst, src, scale, bias):
                roots[0] += 1
                act.wait_ge(root_wanted, roots[0])
                act.activation(dst, src, ACT.Sqrt, bias=bias, scale=scale).then_inc(root_done, 1)

            def ln_root(ntiles):
                root(stat[:, 4, 0:ntiles], stat[:, 3, 0:ntiles], 1.0, 0.0)

            def high_half(l, e, k, bufs):
                act.wait_ge(expert_loaded[k], 16 * (E * l + e + 1))
                dst = half_of_weights(e, k, 0)
                scale = lng_s[:, bass.ds(e, 1)] if l == 0 and k == 0 else SC
                act.activation(dst, bufs[k].rearrange("p (t c) -> p t c", t=HT), ACT.Copy, scale=scale)\
                   .then_inc(weights_high, 1)

            def setup_and_graph0():
                act.wait_ge(zero_made, 2)
                root(deg[:, 4, :], deg[:, 3, :], 1.0, 0.0)
                ln_root(GT)

                def copy_aggregate(c, q, first=False):
                    act.wait_ge(chunk_aggregated, c + 1)
                    if not first:
                        act.wait_ge(hidden_sums, 2 * c - 2)
                    act.activation(agg[q], bank(q), ACT.Copy).then_inc(aggregate_copied, 1)

                def copy_hidden(c, q):
                    for o in range(2):
                        act.wait_ge(hidden_sums, 2 * c + o + 1)
                        act.activation(hid[:, o, bass.ds(c * 512, 512)], bank(2 + 2 * q + o), ACT.Identity,
                                       bias=vec[:, R_B1 + o:R_B1 + o + 1]).then_inc(hidden_copied, 1)

                copy_aggregate(0, 0, True)
                copy_aggregate(1, 1, True)
                copy_hidden(0, 0)
                ln_root(GT)
                copy_aggregate(2, 0)
                copy_hidden(1, 1)
                for k in range(2):
                    high_half(0, 0, k, wstage)
                for q in range(2):
                    copy_aggregate(3 + q, 1 - q)
                    copy_hidden(2 + q, q)
                    if q == 0:
                        ln_root(GT)
                    high_half(0, 1, q, wstage)
                ln_root(GT)
                with act.Fori(2, NCH // 2 - 1) as j:
                    for q in range(2):
                        copy_aggregate(2 * j + q + 1, 1 - q)
                        copy_hidden(2 * j + q, q)
                        high_half(0, j, q, wstage)
                copy_aggregate(NCH - 1, 1)
                copy_hidden(NCH - 2, 0)
                copy_hidden(NCH - 1, 1)
                for k in range(2):
                    high_half(0, E - 1, k, wstage)
                root(bnag[:, :, 1], bnag[:, :, 1], 1.0, 0.0)
                act.wait_ge(norm1_ready, 1)

                def normalise_hidden(c, q, first=False):
                    if not first:
                        act.wait_ge(output_sums, c - 1)
                    for o in range(2):
                        act.activation(hb[q][:, o, :], hid[:, o, bass.ds(c * 512, 512)], ACT.Relu,
                                       bias=bn1t[:, o:o + 1], scale=bn1s[:, o:o + 1]).then_inc(relu_done, 1)

                normalise_hidden(0, 0, True)
                normalise_hidden(1, 1, True)
                with act.Fori(1, NCH // 2) as j:
                    for q in range(2):
                        normalise_hidden(2 * j + q, q)
                root(bnag[:, 0, 1:2], bnag[:, 0, 1:2], 1.0, 0.0)

            def lstm_weights():
                for k in range(NLSTM):
                    act.wait_ge(lstm_turned, k + 1)
                    act.activation(lstm_half(k, 0), bank(lstm_bank(k)), ACT.Copy, scale=SC).then_inc(lstm_high, 1)

            def prep(n, l, g):
                if l == 0:
                    act.wait_ge(norm2_ready, 1)
                    for c in range(GT // 4):
                        if c >= 2:
                            act.wait_ge(graph_turned, g * (GT // 4) + c - 1)
                        act.activation(ybn[c % 2], o2T[:, (g * (GT // 4) + c) * 512:(g * (GT // 4) + c + 1) * 512],
                                       ACT.Identity, bias=bn2t[:, 0:1], scale=bn2s[:, 0:1]).then_inc(graph_normalised, 1)
                warm(ACT.Sqrt)
                root(stat[:, 4, :], stat[:, 6, :], 1.0, 0.0)
                if l == 0:
                    root(stat[:, 7, :], stat[:, 7, :], 1.0, 0.0)
                act.wait_ge(deviations_ready, n + 1)
                for t in range(GT):
                    if t % 4 >= 2:
                        last = act.activation(lnx[:, t, :], xt[:, g * GT + t, :], ACT.Identity,
                                              bias=stat[:, 1, t:t + 1], scale=stat[:, 5, t:t + 1])
                    if t % 4 == 3:
                        last.then_inc(tokens_normed_act, 1)
                if l == 0:
                    act.wait_ge(second_norm_ready, g + 1)
                else:
                    act.wait_ge(tokens_normed_dve, (n + 1) * (GT // 4))
                act.wait_ge(tokens_normed_act, (n + 1) * (GT // 4))
                if n >= 2:
                    act.wait_ge(scattered[n % 2], 16 * GT * TOP_K * (n // 2))
                for c in range(GT // 4):
                    act.wait_ge(tokens_turned, n * (GT // 4) + c + 1)
                    if c >= 2:
                        act.wait_ge(logits_ready, n * (GT // 4) + c - 1)
                    act.activation(lxT[c % 2][:, 0:4 * P], bank(c), ACT.Copy, scale=SC).then_inc(router_high, 1)
                    if l == 0:
                        for t in range(4 * c, 4 * c + 4):
                            last = act.activation(lnh[n % 2][:, t, 0:D], lnx[:, t, :], ACT.Copy,
                                                  scale=stat[:, 7, t:t + 1])
                    else:
                        last = act.activation(lnh[n % 2][:, 4 * c:4 * c + 4, 0:D], lnx[:, 4 * c:4 * c + 4, :],
                                              ACT.Copy, scale=SC)
                    last.then_inc(tokens_high, 1)

            def weight_exponentials(n):
                act.wait_ge(differences_ready, n + 1)
                act.activation(r16[:, 2, :], r16[:, 2, :], ACT.Exp).then_inc(exponentials_done, 1)

            def experts(m, l, g, routed):
                inst = G * l + g
                lo = m * NBLK

                def gelu(i, q):
                    load_expert_id(act, regs, q, inst, i)
                    e = expert_id(act, regs, q)
                    for hp in range(2):
                        act.wait_ge(up_done, 2 * i + (2 * lo + hp + 1))
                        if not (isinstance(i, int) and i < 1):
                            act.wait_ge(hidden_low_done, 2 * i + (2 * lo + hp - 1))
                        for ht in (2 * hp, 2 * hp + 1):
                            last = act.activation(hf[:, ht * BLK:(ht + 1) * BLK],
                                                  ps[:, 2 * q + hp, (ht % 2) * BLK:(ht % 2 + 1) * BLK], ACT.Gelu,
                                                  bias=eb1[:, l, bass.ds(e * HT + ht, 1)], scale=UNSC)
                        if hp == 0:
                            last.then_inc(gelu_done, 1)
                            continue
                        ch.link(last)
                        act.activation(hh[q][:, 2 * hp:2 * hp + 2, :].rearrange("p t n -> p (t n)"),
                                       hf[:, hp * 2 * BLK:(hp + 1) * 2 * BLK], ACT.Copy, scale=SC).then_inc(gelu_done, 1)

                def take(i, q):
                    act.wait_ge(block_turned, i + (lo + 1))
                    act.activation(xs[q], xT[q][:, 0:2 * BLK], ACT.Copy).then_inc(block_in_sbuf, 1)

                warm(ACT.Gelu)
                take(0, 0)
                take(1, 1)
                gelu(0, 0)
                take(2, 0)
                gelu(1, 1)
                take(3, 1)
                with act.Fori(2, NBLK - 3, 2) as i:
                    ch.enter(i - 2, 2, 2)
                    for q in range(2):
                        gelu(i + q, q)
                        take(i + q + 2, q)
                    ch.leave(NBLK // 2 - 2)
                gelu(NBLK - 3, 0)
                take(NBLK - 1, 0)
                gelu(NBLK - 2, 1)
                gelu(NBLK - 1, 0)
                if routed is not None:
                    weight_exponentials(routed)

            def graph1(g):
                n = 2 * g
                warm(ACT.Sqrt)
                for a in range(2):
                    act.wait_ge(c_root_wanted, n + a + 1)
                    act.activation(stat[:, 4, a * QT:(a + 1) * QT], stat[:, 3, a * QT:(a + 1) * QT], ACT.Sqrt)\
                        .then_inc(c_root_done, 1)
                for a in range(2):
                    act.wait_ge(c_deviations, n + a + 1)
                    for t in range(1, QT, 2):
                        j = a * QT + t
                        last = act.activation(xl[a][:, t, :], xt[:, n * QT + j, :], ACT.Identity,
                                              bias=stat[:, 1, j:j + 1], scale=stat[:, 5, j:j + 1])
                    last.then_inc(c_normed_act, 1)
                for a in range(2):
                    for h in range(2):
                        act.wait_ge(c_agg1, 2 * (n + a) + h + 1)
                        act.activation(zT[a][:, h * 512:(h + 1) * 512], bank(4 * a + h), ACT.Copy).then_inc(c_agg1_copied, 1)
                for a in range(2):
                    for h in range(2):
                        act.wait_ge(c_prod1_bias, 2 * (n + a) + h + 1)
                        v = h1T[a][:, h * 512:(h + 1) * 512]
                        act.activation(v, v, ACT.Relu).then_inc(c_relu1, 1)
                warm(ACT.Sigmoid)
                for a in range(2):
                    for h in range(2):
                        act.wait_ge(c_agg2, 2 * (n + a) + h + 1)
                        v = h1T[a][:, h * 512:(h + 1) * 512]
                        act.activation(v, bank(4 * a + 2 + h), ACT.Relu, scale=HSC).then_inc(c_relu2, 1)
                        act.wait_ge(c_relu2, 2 * (n + a) + h + 1)
                        act.activation(hT[a][:, 0, h * 512:(h + 1) * 512], v, ACT.Copy).then_inc(c_input_high, 1)
                NS = len(LSTM_STEPS)
                lo = g * GATES_PER_QUAD
                seen = [0, 0]
                for k, (p, s, half) in enumerate(LSTM_STEPS):
                    gates = (0, 2, 3) if s == 0 else (0, 2, 1, 3)
                    w = (T // p) * (2 if p == 1 else 4)
                    for a in range(2):
                        if k > 0:
                            act.wait_ge(state_split[a], g * NS + k)
                        for gt in gates:
                            seen[a] += 1
                            act.wait_ge(gate_sums[a], lo + seen[a])
                            act.activation(gate[a][:, gt, 0:w], ps[:, 4 * a + gt, 0:w],
                                           ACT.Tanh if gt == 2 else ACT.Sigmoid, scale=1.0 / (SC * HSC),
                                           bias=bsum[:, (p - 1) * 4 + gt:(p - 1) * 4 + gt + 1]).then_inc(gate_done[a], 1)
                        act.wait_ge(cell_done[a], g * NS + k + 1)
                        act.activation(gate[a][:, 2, 0:w], cell[a][:, 0:w], ACT.Tanh).then_inc(cell_tanh[a], 1)
                        e = k - 2
                        if ("C", g) == W_IN and 0 <= e < E:
                            high_half(1, e, a, wstage1)

            m = 0
            for k, s in enumerate(plan):
                if s[0] == "A":
                    setup_and_graph0()
                elif s[0] == "W":
                    lstm_weights()
                elif s[0] == "P":
                    n = prep_order.index(s[1:])
                    prep(n, *s[1:])
                    if k + 1 not in routed_with:
                        weight_exponentials(n)
                elif s[0] == "X":
                    experts(m, *s[1:], prep_order.index(routed_with[k]) if k in routed_with else None)
                    m += 1
                elif s[0] == "C":
                    graph1(s[1])

        @block.vector
        def _(dve):
            regs = expert_registers(dve, "dve")
            ch = Chain(dve, dve_chain)
            link, mark = ch.link, ch.mark
            tt, ts, stt = dve.tensor_tensor, dve.tensor_scalar, dve.scalar_tensor_tensor
            nroot = [0]

            def root():
                nroot[0] += 1
                dve.wait_ge(root_done, nroot[0])

            def tile_stats(t0, nt):
                for t in range(nt):
                    last = dve.bn_stats(st[:, t, :], xt[:, bass.ds(t0 + t, 1), :].rearrange("p a d -> p (a d)"))
                link(last)

            def ln_variance(nt):
                s = lambda k: stat[:, k, 0:nt]
                mark(tt(s(0), st[:, 0:nt, 1], st[:, 0:nt, 4], ALU.add))
                mark(tt(s(1), st[:, 0:nt, 1], st[:, 0:nt, 4], ALU.subtract))
                link(tt(s(2), st[:, 0:nt, 2], st[:, 0:nt, 5], ALU.add))
                mark(ts(s(0), s(0), 0.5, None, ALU.mult))
                link(tt(s(1), s(1), s(1), ALU.mult))
                link(stt(s(3), s(1), D / 4.0, s(2), ALU.mult, ALU.add))

            def ln_stats(nt):
                s = lambda k: stat[:, k, 0:nt]
                ln_variance(nt)
                ts(s(3), s(3), 1.0 / D, EPS, ALU.mult, ALU.add).then_inc(root_wanted, 1)
                root()
                link(dve.reciprocal(s(5), s(4)))

            def layer_stats(k):
                dve.wait_ge(x_loaded[k], 16)
                tile_stats(k * GT, GT)
                ln_stats(GT)
                mark(dve.tensor_copy(stat_all[:, 0, k * GT:(k + 1) * GT], stat[:, 0, 0:GT]))
                link(dve.tensor_copy(stat_all[:, 1, k * GT:(k + 1) * GT], stat[:, 5, 0:GT]))

            def setup():
                dve.wait_ge(setup_turned, 1)
                dve.wait_ge(constants_made, 13)
                dve.wait_ge(adj_loaded, 16)
                ps0 = bank(0).rearrange("p (t m) -> p t m", t=2)
                dve.tensor_copy(adjT[:, :, :], ps0).then_inc(setup_copied, 1)
                mark(dve.tensor_copy(adj_i, adj_n))
                link(dve.tensor_copy(adj_it, ps0))
                for t in range(2):
                    d = slice(t * P, (t + 1) * P)
                    mark(tt(adj_i[:, t, d], adj_i[:, t, d], ident[:, :], ALU.add))
                    mark(tt(adj_it[:, t, d], adj_it[:, t, d], ident[:, :], ALU.add))
                ch.wait()
                for t in range(2):
                    mark(tt(ahatT[:, 0, t * P:(t + 1) * P], adj_i[:, t, t * P:(t + 1) * P], ident[:, :], ALU.mult))
                mark(dve.reduce_sum(deg[:, 0, :], adj_i, axis=AX.X))
                mark(dve.reduce_sum(deg[:, 1, :], adj_it, axis=AX.X))
                ch.wait()
                link(dve.reduce_sum(deg[:, 2, :], ahatT[:, 0, :].rearrange("p (t m) -> p t m", t=2), axis=AX.X))
                link(tt(deg[:, 3, :], deg[:, 0, :], deg[:, 1, :], ALU.add))
                tt(deg[:, 3, :], deg[:, 3, :], deg[:, 2, :], ALU.subtract).then_inc(root_wanted, 1)
                root()
                link(dve.reciprocal(deg[:, 5, :], deg[:, 4, :]))
                mark(ts(adj_i[:, 0, :], adj_i[:, 0, :], deg[:, 5, 0:1], None, ALU.mult))
                ch.wait()
                ts(adj_i[:, 1, :], adj_i[:, 1, :], deg[:, 5, 1:2], None, ALU.mult).then_inc(setup_copied, 1)
                layer_stats(0)
                dve.wait_ge(setup_turned, 2)
                dve.tensor_copy(vec[:, :], ps[:, 1, 0:R_ROWS]).then_inc(setup_copied, 1)
                dve.wait_ge(setup_copied, 3)
                mark(ts(lng_s[:, :], vec[:, R_LNG:R_LNG + E], SC, None, ALU.mult))
                mark(tt(bsum[:, :], vec[:, R_BIH:R_BIH + 16], vec[:, R_BHH:R_BHH + 16], ALU.add))
                dve.wait_ge(setup_turned, 3)
                mark(dve.tensor_copy(w1T, ps[:, 2, 0:GH]))
                dve.tensor_copy(w2T.rearrange("p t d -> p (t d)"), ps[:, 2, GH:2 * GH]).then_inc(setup_copied, 1)
                dve.wait_ge(setup_turned, 4)
                dve.tensor_copy(bmap[:, :], ps[:, 3, 0:T]).then_inc(setup_copied, 1)
                dve.wait_ge(setup_turned, 5)
                ch.wait()
                ts(ahatT[:, 0, :], ps[:, 4, 0:T], deg[:, 5, 0:1], None, ALU.mult)
                ts(ahatT[:, 1, :], ps[:, 4, T:2 * T], deg[:, 5, 1:2], None, ALU.mult).then_inc(setup_copied, 1)

            def normalise_into(dst, j_of, nt):
                for t in range(nt):
                    last = ts(dst(t), j_of(t), stat[:, 0, t:t + 1], stat[:, 5, t:t + 1], ALU.subtract, ALU.mult)
                return last

            def graph0():
                def normalise(c, q):
                    if not (isinstance(c, int) and c < 2):
                        dve.wait_ge(chunk_aggregated, c - 1)
                    for t in range(4):
                        j = c * 4 + t
                        last = ts(xn[q][:, t, :], xt[:, bass.ds(j, 1), :].rearrange("p a d -> p (a d)"),
                                  stat_all[:, 0, bass.ds(j, 1)], stat_all[:, 1, bass.ds(j, 1)],
                                  ALU.subtract, ALU.mult)
                    last.then_inc(chunk_normalised, 1)

                def stats1(c):
                    dve.wait_ge(hidden_copied, 2 * c + 2)
                    for o in range(2):
                        last = dve.bn_stats(bnst[:, o, bass.ds(c, 1), :].rearrange("p a s -> p (a s)"),
                                            hid[:, o, bass.ds(c * 512, 512)])
                    mark(last)

                def pair(j):
                    for q in range(2):
                        normalise(2 * j + q + 2, q)
                        stats1(2 * j + q)
                        low_half(0, j, q, wstage)

                normalise(0, 0)
                normalise(1, 1)
                layer_stats(1)
                pair(0)
                layer_stats(2)
                pair(1)
                layer_stats(3)
                with dve.Fori(2, NCH // 2 - 1) as j:
                    ch.enter(j - 2, 2)
                    pair(j)
                    ch.leave(NCH // 2 - 3)
                stats1(NCH - 2)
                stats1(NCH - 1)
                for k in range(2):
                    low_half(0, E - 1, k, wstage)
                expert_bias()
                ch.wait()
                for o in range(2):
                    mark(dve.bn_aggr(bnag[:, o, :], bnst[:, o, :, :].rearrange("p c s -> p (c s)")))
                ch.wait()
                ts(bnag[:, :, 1], bnag[:, :, 1], EPS, None, ALU.add).then_inc(root_wanted, 1)
                root()
                link(dve.reciprocal(bn1s[:, :], bnag[:, :, 1]))
                link(tt(bn1s[:, :], bn1s[:, :], vec[:, R_G1:R_G1 + 2], ALU.mult))
                link(tt(bn1t[:, :], bnag[:, :, 0], bn1s[:, :], ALU.mult))
                tt(bn1t[:, :], vec[:, R_BE1:R_BE1 + 2], bn1t[:, :], ALU.subtract).then_inc(norm1_ready, 1)
                dve.wait_ge(params_loaded, 16 * PAR_DMAS)
                link(ts(Wrhl[:, :, 0, :], Wr[:, :, :], SC, None, ALU.mult))
                mark(stt(Wrhl[:, :, 1, :], Wr[:, :, :], SC, Wrhl[:, :, 0, :], ALU.mult, ALU.subtract))

                with dve.Fori(0, NCH // 2) as j:
                    ch.enter(j, 2)
                    for q in range(2):
                        c = 2 * j + q
                        dve.wait_ge(output_sums, c + 1)
                        ts(o2T[:, bass.ds(c * 512, 512)], bank(6 + q), vec[:, R_B2:R_B2 + 1], None, ALU.add)\
                            .then_inc(output_copied, 1)
                        dve.wait_ge(output_copied, c + 1)
                        last = dve.bn_stats(bnst[:, 0, bass.ds(c, 1), :].rearrange("p a s -> p (a s)"),
                                            o2T[:, bass.ds(c * 512, 512)])
                        mark(last)
                    ch.leave(NCH // 2)
                ch.wait()
                link(dve.bn_aggr(bnag[:, 0, :], bnst[:, 0, :, :].rearrange("p c s -> p (c s)")))
                ts(bnag[:, 0, 1:2], bnag[:, 0, 1:2], EPS, None, ALU.add).then_inc(root_wanted, 1)
                root()
                link(dve.reciprocal(bn2s[:, :], bnag[:, 0, 1:2]))
                link(tt(bn2s[:, :], bn2s[:, :], vec[:, R_G2:R_G2 + 1], ALU.mult))
                link(tt(bn2t[:, :], bnag[:, 0, 0:1], bn2s[:, :], ALU.mult))
                tt(bn2t[:, :], vec[:, R_BE2:R_BE2 + 1], bn2t[:, :], ALU.subtract).then_inc(norm2_ready, 1)

            def low_half(l, e, k, bufs):
                dve.wait_ge(weights_high, 2 * (E * l + e) + k + 1)
                scale = lng_s[:, bass.ds(e, 1)] if l == 0 and k == 0 else SC
                stt(half_of_weights(e, k, 1), bufs[k].rearrange("p (t c) -> p t c", t=HT), scale,
                    half_of_weights(e, k, 0), ALU.mult, ALU.subtract).then_inc(weights_low, 1)

            def expert_bias():
                dve.wait_ge(bias_folded, E)
                mark(tt(eb1[:, 0, :], ps[:, 6, 0:E * HT], vec[:, R_FB1[0]:R_FB1[0] + E * HT], ALU.add))
                mark(dve.tensor_copy(eb1[:, 1, :], vec[:, R_FB1[1]:R_FB1[1] + E * HT]))

            def bc(ap, n):
                return ap.unsqueeze(2).to_broadcast([ap.shape[0], ap.shape[1], n])

            def mid(ap, m):
                return ap.unsqueeze(1).to_broadcast([ap.shape[0], m, ap.shape[1]])

            def lstm_weights():
                for k in range(NLSTM):
                    dve.wait_ge(lstm_high, k + 1)
                    stt(lstm_half(k, 1), bank(lstm_bank(k)), SC, lstm_half(k, 0), ALU.mult, ALU.subtract)\
                        .then_inc(lstm_low, 1)

            L, ra, rb, oh1, oh2, sm = (route[k][:, :, :] for k in ("L", "a", "b", "oh1", "oh2", "sm"))
            r = lambda k: r16[:, k, :]

            def prep(n, l, g):
                t0 = g * GT
                if l == 0:
                    for c in range(GT // 4):
                        dve.wait_ge(graph_turned, g * (GT // 4) + c + 1)
                        v = xt[:, t0 + 4 * c:t0 + 4 * c + 4, :].rearrange("p t d -> p (t d)")
                        tt(v, v, bank(c % 2), ALU.add).then_inc(graph_added, 1)
                    dve.wait_ge(graph_added, (g + 1) * (GT // 4))
                tile_stats(t0, GT)
                z = lambda k: stat[:, k, :]
                ln_variance(GT)
                ts(z(6), z(3), 1.0 / D, EPS, ALU.mult, ALU.add).then_inc(root_wanted, 1)
                root()
                link(dve.reciprocal(z(5), z(4)))
                stt(z(1), z(0), -1.0, z(5), ALU.mult, ALU.mult).then_inc(deviations_ready, 1)
                if l == 0:
                    link(tt(z(7), z(5), z(5), ALU.mult))
                    link(tt(z(7), z(7), z(3), ALU.mult))
                    ts(z(7), z(7), 1.0 / D, EPS, ALU.mult, ALU.add).then_inc(root_wanted, 1)
                for t in range(GT):
                    if t % 4 < 2:
                        last = ts(lnx[:, t, :], xt[:, t0 + t, :], z(0)[:, t:t + 1], z(5)[:, t:t + 1],
                                  ALU.subtract, ALU.mult)
                    if t % 4 == 1:
                        last.then_inc(tokens_normed_dve, 1)
                if l == 0:
                    root()
                    link(dve.reciprocal(z(7), z(7)))
                    ts(z(7), z(7), SC, None, ALU.mult).then_inc(second_norm_ready, 1)
                    dve.wait_ge(second_norm_ready, g + 1)
                for c in range(GT // 4):
                    dve.wait_ge(router_high, n * (GT // 4) + c + 1)
                    stt(lxT[c % 2][:, 4 * P:8 * P], bank(c), SC, lxT[c % 2][:, 0:4 * P], ALU.mult, ALU.subtract)\
                        .then_inc(router_low, 1)
                    dve.wait_ge(tokens_high, n * (GT // 4) + c + 1)
                    v = lnh[n % 2]
                    if l == 0:
                        for t in range(4 * c, 4 * c + 4):
                            mark(stt(v[:, t, D:2 * D], lnx[:, t, :], z(7)[:, t:t + 1], v[:, t, 0:D],
                                     ALU.mult, ALU.subtract))
                    else:
                        c4 = slice(4 * c, 4 * c + 4)
                        mark(stt(v[:, c4, D:2 * D], lnx[:, c4, :], SC, v[:, c4, 0:D], ALU.mult, ALU.subtract))
                dve.wait_ge(logits_ready, (n + 1) * (GT // 4))
                sums = ps[:, 4, 0:GT * 2 * E].rearrange("p (t k e) -> p t k e", k=2, e=E)
                link(dve.tensor_copy(sm, sums[:, :, 0, :]))
                link(tt(sm, sums[:, :, 1, :], sm, ALU.add))
                link(stt(L, sm, UNSC, mid(brb[:, l, :], GT), ALU.mult, ALU.add))

            def select():
                for k, oh in ((0, oh1), (1, oh2)):
                    link(dve.reduce_max(r(k), L, axis=AX.X))
                    link(tt(ra, L, bc(r(k), E), ALU.is_equal))
                    link(tt(ra, ra, mid(desc[:, :], GT), ALU.mult))
                    link(dve.reduce_max(r(3), ra, axis=AX.X))
                    link(tt(oh, ra, bc(r(3), E), ALU.is_equal))
                    if k == 0:
                        link(stt(L, oh, -3.0e38, L, ALU.mult, ALU.add))
                tt(M16[:, :, :], oh1, oh2, ALU.add).then_inc(mask_ready, 1)
                tt(r(2), r(1), r(0), ALU.subtract).then_inc(differences_ready, 1)

            def take_counts(n):
                dve.wait_ge(counts_ready, n + 1)
                mark(dve.tensor_copy(sm, ps[:, 5, 0:GT * E].rearrange("p (t e) -> p t e", e=E)))
                mark(dve.tensor_copy(ejt[:, :, :], ps[:, 5, 128:128 + GT * E].rearrange("p (t e) -> p e t", e=E)))

            def place_experts(inst):
                ch.wait()
                f = lambda z: z[:, :, :].rearrange("p e t -> p (e t)")
                link(dve.tensor_tensor_scan(f(ejc), ej_mask[:, :], f(ejt), 0.0, ALU.mult, ALU.add))
                mark(tt(ejt[:, :, :], ejc[:, :, :], ejt[:, :, :], ALU.subtract))
                link(tt(gtk[:, :, :], bc(ejc[:, :, GT - 1], KMAX), mid(k_blk[:, :], E), ALU.is_gt))
                link(dve.reduce_sum(r8[:, 0, :], gtk[:, :, :], axis=AX.X))
                link(dve.tensor_tensor_scan(r8[:, 1, :], one8[:, :], r8[:, 0, :], 0.0, ALU.mult, ALU.add))
                link(tt(r8[:, 2, :], r8[:, 1, :], r8[:, 0, :], ALU.subtract))
                mark(ts(r8[:, 2, :], r8[:, 2, :], float(BLK), None, ALU.mult))
                link(tt(geb[:, :, :], bc(iota_b[:, :], E - 1), mid(r8[0:1, 1, 0:E - 1], NBLK), ALU.is_ge))
                with nc.allow_low_precision(reason="counts are small integers"):
                    mark(dve.reduce_sum(ids[0:1, inst, 0:NBLK], geb[:, :, :], axis=AX.X))

            def place_tokens(inst):
                link(tt(sm, sm, ejt[:, :, :].rearrange("p e t -> p t e"), ALU.add))
                link(tt(sm, sm, mid(r8[:, 2, :], GT), ALU.add))
                for k, (oh, b) in enumerate(((oh1, ra), (oh2, rb))):
                    mark(tt(b, oh, sm, ALU.mult))
                ch.wait()
                with nc.allow_low_precision(reason="slots are integers below 2^24"):
                    for k, b in enumerate((ra, rb)):
                        last = dve.reduce_sum(slot[:, inst, k, :], b, axis=AX.X)
                last.then_inc(slots_ready, 1)

            def weights(n, inst):
                dve.wait_ge(exponentials_done, n + 1)
                link(ts(r(4), r(2), 1.0, None, ALU.add))
                link(dve.reciprocal(wts[:, inst, 0, :], r(4)))
                tt(wts[:, inst, 1, :], r(2), wts[:, inst, 0, :], ALU.mult).then_inc(weights_ready, 1)

            def route_group(n, l, g):
                select()
                take_counts(n)
                place_experts(G * l + g)
                place_tokens(G * l + g)
                weights(n, G * l + g)

            assert NBLK - 3 - 4 == GT

            def experts(m, l, g, routed, next_c):
                inst = G * l + g
                lo = m * NBLK
                if routed is not None:
                    n_r, inst_r = prep_order.index(routed), G * routed[0] + routed[1]

                def hidden_high(i, q):
                    dve.wait_ge(gelu_done, 2 * i + (2 * lo + 1))
                    ts(hh[q][:, 0:2, :].rearrange("p t n -> p (t n)"), hf[:, 0:2 * BLK], SC, None, ALU.mult)\
                        .then_inc(hidden_high_done, 1)

                def hidden_low(i, q, hp):
                    if hp == 0:
                        dve.wait_ge(hidden_high_done, i + (lo + 1))
                    else:
                        dve.wait_ge(gelu_done, 2 * i + (2 * lo + 2))
                    f = lambda z: z[q][:, 2 * hp:2 * hp + 2, :].rearrange("p t n -> p (t n)")
                    stt(f(hl), hf[:, hp * 2 * BLK:(hp + 1) * 2 * BLK], SC, f(hh), ALU.mult, ALU.subtract)\
                        .then_inc(hidden_low_done, 1)

                def result(i, q):
                    load_expert_id(dve, regs, q, inst, i)
                    e = expert_id(dve, regs, q)
                    dve.wait_ge(down_done, i + (lo + 1))
                    dve.wait_ge(result_stored[q], by_parity(m, i, q))
                    sums = ps[:, 4 + q, :].rearrange("p (h s d) -> p h s d", h=2, s=2)
                    stt(yb_out[q], sums[:, :, 0, :], UNSC, eb2[l][:, bass.ds(e, 1), :].to_broadcast([P, 2, D]),
                        ALU.mult, ALU.add).then_inc(result_begun, 1)
                    dve.wait_ge(result_begun, i + (lo + 1))
                    stt(yb_out[q], sums[:, :, 1, :], UNSC, yb_out[q], ALU.mult, ALU.add).then_inc(result_ready, 1)

                if routed is not None:
                    select()
                hidden_high(0, 0)
                hidden_low(0, 0, 0)
                hidden_low(0, 0, 1)
                hidden_high(1, 1)
                hidden_low(1, 1, 0)
                if routed is not None:
                    take_counts(n_r)
                hidden_low(1, 1, 1)
                result(0, 0)
                for i in (2, 3):
                    hidden_high(i, i % 2)
                    hidden_low(i, i % 2, 0)
                    hidden_low(i, i % 2, 1)
                    result(i - 1, 1 - i % 2)
                    if routed is not None:
                        place_experts(inst_r) if i == 2 else place_tokens(inst_r)
                if next_c is not None:
                    dve.wait_ge(combined, (GT // 4) * (expert_order.index((0, next_c)) + 1))
                with dve.Fori(4, NBLK - 3, 2) as i:
                    if next_c is not None:
                        for sign, t in ((1, -4), (-1, GT + 3)):
                            dve.bn_stats(st[:, bass.ds(i * sign + t, 1), :].rearrange("p a s -> p (a s)"),
                                         xt[:, bass.ds(i * sign + (next_c * GT + t), 1), :]
                                         .rearrange("p a d -> p (a d)"))
                    for q in range(2):
                        hidden_high(i + q, q)
                        hidden_low(i + q, q, 0)
                        hidden_low(i + q, q, 1)
                        result(i + q - 1, 1 - q)
                for i in range(NBLK - 3, NBLK):
                    hidden_high(i, i % 2)
                    hidden_low(i, i % 2, 0)
                    hidden_low(i, i % 2, 1)
                    result(i - 1, 1 - i % 2)
                if routed is not None:
                    weights(n_r, inst_r)
                result(NBLK - 1, 0)

            def graph1(g):
                n = 2 * g
                NS = len(LSTM_STEPS)
                ln_variance(2 * QT)
                for a in range(2):
                    r = slice(a * QT, (a + 1) * QT)
                    ts(stat[:, 3, r], stat[:, 3, r], 1.0 / D, EPS, ALU.mult, ALU.add).then_inc(c_root_wanted, 1)
                for a in range(2):
                    r = slice(a * QT, (a + 1) * QT)
                    dve.wait_ge(c_root_done, n + a + 1)
                    link(dve.reciprocal(stat[:, 5, r], stat[:, 4, r]))
                    stt(stat[:, 1, r], stat[:, 0, r], -1.0, stat[:, 5, r], ALU.mult, ALU.mult).then_inc(c_deviations, 1)
                    for t in range(0, QT, 2):
                        j = a * QT + t
                        last = ts(xl[a][:, t, :], xt[:, n * QT + j, :], stat[:, 0, j:j + 1], stat[:, 5, j:j + 1],
                                  ALU.subtract, ALU.mult)
                    last.then_inc(c_normed_dve, 1)
                for a in range(2):
                    for h in range(2):
                        dve.wait_ge(c_prod1, 2 * (n + a) + h + 1)
                        tt(h1T[a][:, h * 512:(h + 1) * 512].rearrange("p (b t) -> p b t", b=2),
                           bank(4 * a + 2 + h).rearrange("p (b t) -> p b t", b=2), mid(bmap[:, :], 2), ALU.add)\
                            .then_inc(c_prod1_bias, 1)
                for a in range(2):
                    for h in range(2):
                        dve.wait_ge(c_prod2, 2 * (n + a) + h + 1)
                        tt(u2[a][:, 4 * h:4 * h + 4, :], bank(4 * a + h).rearrange("p (t d) -> p t d", t=4),
                           mid(bg1b[:, :], 4), ALU.add).then_inc(c_prod2_bias, 1)
                for a in range(2):
                    for h in range(2):
                        dve.wait_ge(c_input_high, 2 * (n + a) + h + 1)
                        c = slice(h * 512, (h + 1) * 512)
                        tt(hT[a][:, 1, c], h1T[a][:, c], hT[a][:, 0, c], ALU.subtract).then_inc(c_input_low, 1)
                lo = g * GATES_PER_QUAD
                seen = [0, 0]
                for k, (p, sstep, half) in enumerate(LSTM_STEPS):
                    nw = T // p
                    nb = 2 if p == 1 else 4
                    w = nb * nw

                    def new_cell(a):
                        cv = cell[a][:, 0:w]
                        i, f, c = (gate[a][:, z, 0:w] for z in range(3))
                        dve.wait_ge(gate_done[a], lo + seen[a] + 2)
                        if sstep == 0:
                            tt(cv, i, c, ALU.mult).then_inc(cell_done[a], 1)
                        else:
                            mark(tt(i, i, c, ALU.mult))
                            dve.wait_ge(gate_done[a], lo + seen[a] + 3)
                            link(tt(cv, f, cv, ALU.mult))
                            tt(cv, cv, i, ALU.add).then_inc(cell_done[a], 1)
                        seen[a] += 3 if sstep == 0 else 4

                    def new_hidden(a):
                        hv = hT[a].rearrange("p s (b t) -> p s b t", b=4)
                        dve.wait_ge(cell_tanh[a], g * NS + k + 1)
                        dve.wait_ge(gate_done[a], lo + seen[a])
                        if sstep == p - 1:
                            dst = hv[:, :, nb * half:nb * half + nb, sstep:sstep + (nw - 1) * p + 1:p]
                            v = lambda z: z.rearrange("p (b t) -> p b t", b=nb)
                        else:
                            dst = hcur[a][:, :, 0:w]
                            v = lambda z: z
                        hs = gate[a][:, 3, 0:w]
                        link(tt(hs, hs, gate[a][:, 2, 0:w], ALU.mult))
                        link(ts(dst[:, 0], v(hs), HSC, None, ALU.mult))
                        stt(dst[:, 1], v(hs), HSC, dst[:, 0], ALU.mult, ALU.subtract).then_inc(state_split[a], 1)

                    for a in range(2):
                        new_cell(a)
                        new_hidden(a)
                        if ("C", g) == W_IN and 0 <= k - 2 < E:
                            low_half(1, k - 2, a, wstage1)
                for a in range(2):
                    for h in range(2):
                        dve.wait_ge(c_turned_back, 2 * (n + a) + h + 1)
                        j = n * QT + a * QT + 4 * h
                        v = xt[:, j:j + 4, :].rearrange("p t d -> p (t d)")
                        stt(v, bank(4 * a + h), 1.0 / HSC, v, ALU.mult, ALU.add).then_inc(c_added, 1)
                dve.wait_ge(c_added, 2 * n + 4)

            def combine_last(m, l, g):
                for c in range(GT // 4):
                    dve.wait_ge(gathered[c], 16 * 4 * TOP_K * (m + 1))
                    for k in range(TOP_K):
                        for t in range(4 * c, 4 * c + 4):
                            v = xt[:, g * GT + t, :]
                            last = stt(v, ygat[:, t, k, :], wts[:, G * l + g, k, t:t + 1], v, ALU.mult, ALU.add)
                        if k == 0:
                            link(last)
                    last.then_inc(combined, 1)

            m = 0
            for k, s in enumerate(plan):
                if s[0] == "A":
                    setup()
                    graph0()
                elif s[0] == "W":
                    lstm_weights()
                elif s[0] == "P":
                    n = prep_order.index(s[1:])
                    prep(n, *s[1:])
                    if k + 1 not in routed_with:
                        route_group(n, *s[1:])
                elif s[0] == "X":
                    follows = plan[k + 1] if k + 1 < len(plan) else s
                    experts(m, *s[1:], routed_with.get(k), follows[1] if follows[0] == "C" else None)
                    m += 1
                elif s[0] == "C":
                    graph1(s[1])
            if expert_order:
                combine_last(m - 1, *expert_order[-1])


_INS = ["x", "adj", "L0_gnn_W1", "L0_gnn_b1", "L0_gnn_g1", "L0_gnn_be1", "L0_gnn_W2", "L0_gnn_b2", "L0_gnn_g2",
        "L0_gnn_be2", "L0_ffn_Wr", "L0_ffn_br", "L0_ffn_ln_g", "L0_ffn_ln_b", "L0_ffn_W1", "L0_ffn_b1", "L0_ffn_W2",
        "L0_ffn_b2", "L1_gnn_Wg0", "L1_gnn_bg0", "L1_gnn_Wg1", "L1_gnn_bg1", "L1_gnn_Wih", "L1_gnn_Whh",
        "L1_gnn_bih", "L1_gnn_bhh", "L1_ffn_Wg", "L1_ffn_bg", "L1_ffn_W1", "L1_ffn_b1", "L1_ffn_W2", "L1_ffn_b2"]


def kernel(**inputs):
    import numpy as _np
    import concourse.bacc as _bacc
    from concourse import mybir as _mybir
    from concourse.bass_utils import run_bass_kernel_spmd as _run

    nc = _bacc.Bacc("TRN2", target_bir_lowering=False, num_devices=1)
    arrays, args = {}, []
    for name in _INS:
        a = _np.ascontiguousarray(inputs[name])
        arrays[f"in_{name}"] = a
        args.append(nc.dram_tensor(f"in_{name}", a.shape, _mybir.dt.from_np(a.dtype), kind="ExternalInput").ap())
    args.append(nc.dram_tensor("out_0", (B, T, D), F32, kind="ExternalOutput").ap())
    graph_moe_kernel(nc, *args)
    r = _run(nc, [arrays], core_ids=[0])
    return r.results[0]["out_0"]
```
